# Optimizing a Trainium2 kernel written in Bass

```python
import numpy as np
import jax
import jax.numpy as jnp

def _softmax(x, axis=-1):
    return jax.nn.softmax(x, axis=axis)

def _gelu(x):
    return jax.nn.gelu(x, approximate=True)

def _silu(x):
    return jax.nn.silu(x)

def _sigmoid(x):
    return jax.nn.sigmoid(x)

def _layernorm(x, axis=-1, eps=1e-05):
    m = jnp.mean(x, axis=axis, keepdims=True)
    v = jnp.var(x, axis=axis, keepdims=True)
    return (x - m) / jnp.sqrt(v + eps)

def _scatter_add(tgt, idx, src, axis=0):
    return tgt.at[idx].add(src)

def _segment_sum(src, seg, n):
    return jax.ops.segment_sum(src, seg, n)
kernel_name = 'mk_perceiver_d4_seqx_r8_11f6d2'

def setup_inputs(seed: int=0):
    np.random.seed(seed)
    _w = jnp.asarray

    def _rec_inputs():
        import jax
        import jax.numpy as jnp
        _rk = jax.random.key(seed)
        x = 7.22e-05 + 1 * jax.random.normal(jax.random.fold_in(_rk, 1), (64, 32, 128), jnp.float32)
        _lenS = 32 - jax.random.randint(jax.random.fold_in(_rk, 7), (64,), 0, max(1, 32 // 4) + 1, jnp.int32)
        _lenS2 = 257 - jax.random.randint(jax.random.fold_in(_rk, 8), (64,), 0, max(1, 257 // 4) + 1, jnp.int32)
        _ctx_1024P = jax.random.normal(jax.random.fold_in(_rk, 11), (64, 16, 128), jnp.float32)
        _ctx_1024c = jax.random.dirichlet(jax.random.fold_in(_rk, 511), 0.3 * jnp.ones((16,), jnp.float32), (64, 257))
        _ctx_1024t = jnp.einsum('bsk,bkd->bsd', _ctx_1024c, _ctx_1024P)
        _ctx_1024t = _ctx_1024t * jax.lax.rsqrt(jnp.mean(jnp.square(_ctx_1024t)) + 1e-12) * 0.953939
        ctx_1024 = 4.13588e-05 + 0.999923 * (_ctx_1024t + 0.3 * jax.random.normal(jax.random.fold_in(_rk, 611), (64, 257, 128), jnp.float32))
        _validS = jnp.arange(32)[None, :] < _lenS[:, None]
        _validS2 = jnp.arange(257)[None, :] < _lenS2[:, None]
        _causal = jnp.tril(jnp.ones((32, 32), dtype=bool))
        mask_1xSxS2_ff0 = jnp.where(jnp.ones((1, 32, 257), dtype=bool), 0.0, -1000000000.0).astype(jnp.float32)
        mask_BxS2_ik0 = jnp.where(jnp.broadcast_to(_validS2[:, :], (64, 257)), 0, 1).astype(jnp.int32)
        return (x, ctx_1024, mask_1xSxS2_ff0, mask_BxS2_ik0)
    x, ctx_1024, mask_1xSxS2_ff0, mask_BxS2_ik0 = _rec_inputs()

    def _L0_xattn_setup():
        import jax, jax.numpy as jnp
        import numpy as np
        B, S, D_IN, D_MODEL = (4, 256, 128, 128)
        key = jax.random.key(seed)
        ks = jax.random.split(key, 8)
        glorot = np.sqrt(6.0 / (D_IN + D_MODEL))
        inp = {'q': jax.random.normal(ks[0], (B, S, D_IN), dtype=jnp.float32), 'k': jax.random.normal(ks[1], (B, S, D_IN), dtype=jnp.float32), 'v': jax.random.normal(ks[2], (B, S, D_IN), dtype=jnp.float32), 'mask': jnp.zeros((1, S, S), dtype=jnp.float32), 'kernel_q': jax.random.uniform(ks[3], (1, 1, D_IN, D_MODEL), jnp.float32, -glorot, glorot), 'kernel_k': jax.random.uniform(ks[4], (1, 1, D_IN, D_MODEL), jnp.float32, -glorot, glorot), 'kernel_v': jax.random.uniform(ks[5], (1, 1, D_IN, D_MODEL), jnp.float32, -glorot, glorot), 'bias_q': 0.05 * jax.random.normal(ks[6], (D_MODEL,), dtype=jnp.float32), 'bias_k': 0.05 * jax.random.normal(ks[7], (D_MODEL,), dtype=jnp.float32), 'bias_v': 0.05 * jax.random.normal(jax.random.fold_in(key, 7), (D_MODEL,), dtype=jnp.float32)}
        return inp
    _L0_xattn_all = _L0_xattn_setup()
    _L0_xattn_in = {k: v for k, v in _L0_xattn_all.items() if k in ('kernel_q', 'kernel_k', 'kernel_v', 'bias_q', 'bias_k', 'bias_v')}
    del _L0_xattn_all

    def _L0_attn_setup():
        import jax, jax.numpy as jnp
        import numpy as np
        N_EMBD = 128
        N_HEAD = 16
        HEAD_DIM = N_EMBD // N_HEAD
        ROPE_BASE = 10000.0

        def _apply_rotary(x, cos, sin):
            x1, x2 = (x[..., 0::2], x[..., 1::2])
            return jnp.concatenate([x1 * cos - x2 * sin, x1 * sin + x2 * cos], axis=-1)
        key = jax.random.key(seed)
        k1, k2, k3, k4 = jax.random.split(key, 4)
        B, T, C = (4, 128, N_EMBD)
        x = jax.random.normal(k1, (B, T, C), dtype=jnp.float32)
        Wqkv = jax.random.normal(k2, (C, 3 * C), dtype=jnp.float32) * (1.0 / np.sqrt(C))
        Wproj = jax.random.normal(k3, (C, C), dtype=jnp.float32) * (1.0 / np.sqrt(C))
        cascade_w = jnp.ones((N_HEAD - 1,), dtype=jnp.float32) * 0.1
        return {'x': x, 'Wqkv': Wqkv, 'Wproj': Wproj, 'cascade_w': cascade_w}
    _L0_attn_all = _L0_attn_setup()
    _L0_attn_in = {k: v for k, v in _L0_attn_all.items() if k in ('Wqkv', 'Wproj', 'cascade_w')}
    del _L0_attn_all

    def _L0_ffn_setup():
        import jax, jax.numpy as jnp
        import numpy as np
        E, D, F = (8, 128, 512)
        LN_EPS = 1e-05
        key = jax.random.key(seed)
        k = jax.random.split(key, 8)
        x = jax.random.normal(k[0], (4, 256, D), jnp.float32)
        centroids = jax.random.normal(k[1], (E, D), jnp.float32) * 0.1
        ln_g = jnp.ones((E, D), jnp.float32)
        ln_b = jnp.zeros((E, D), jnp.float32)
        w1 = jax.random.normal(k[2], (E, F, D), jnp.float32) * (1.0 / np.sqrt(D))
        b1 = jnp.zeros((E, F), jnp.float32)
        w2 = jax.random.normal(k[3], (E, D, F), jnp.float32) * (1.0 / np.sqrt(F))
        b2 = jnp.zeros((E, D), jnp.float32)
        return {'input_features': x, 'centroids': centroids, 'ln_g': ln_g, 'ln_b': ln_b, 'w1': w1, 'b1': b1, 'w2': w2, 'b2': b2}
    _L0_ffn_all = _L0_ffn_setup()
    _L0_ffn_in = {k: v for k, v in _L0_ffn_all.items() if k in ('centroids', 'ln_g', 'ln_b', 'w1', 'b1', 'w2', 'b2')}
    del _L0_ffn_all

    def _L1_xattn_setup():
        import jax, jax.numpy as jnp
        import numpy as np
        D_MODEL = 128
        N_HEADS = 16
        HEAD_DIM = 64
        key = jax.random.key(seed)
        ks = jax.random.split(key, 11)
        B, S = (4, 256)
        scale = 1.0 / np.sqrt(D_MODEL)
        return {'query': jax.random.normal(ks[0], (B, S, D_MODEL), jnp.float32), 'key': jax.random.normal(ks[1], (B, S, D_MODEL), jnp.float32), 'value': jax.random.normal(ks[2], (B, S, D_MODEL), jnp.float32), 'Wq': jax.random.normal(ks[3], (D_MODEL, N_HEADS * HEAD_DIM), jnp.float32) * scale, 'bq': jnp.zeros((N_HEADS * HEAD_DIM,), jnp.float32), 'Wk': jax.random.normal(ks[4], (D_MODEL, N_HEADS * HEAD_DIM), jnp.float32) * scale, 'bk': jnp.zeros((N_HEADS * HEAD_DIM,), jnp.float32), 'Wv': jax.random.normal(ks[5], (D_MODEL, N_HEADS * HEAD_DIM), jnp.float32) * scale, 'bv': jnp.zeros((N_HEADS * HEAD_DIM,), jnp.float32), 'Wo': jax.random.normal(ks[6], (N_HEADS * HEAD_DIM, D_MODEL), jnp.float32) * scale, 'bo': jnp.zeros((D_MODEL,), jnp.float32)}
    _L1_xattn_all = _L1_xattn_setup()
    _L1_xattn_in = {k: v for k, v in _L1_xattn_all.items() if k in ('Wq', 'bq', 'Wk', 'bk', 'Wv', 'bv', 'Wo', 'bo')}
    del _L1_xattn_all

    def _L1_attn_setup():
        import jax, jax.numpy as jnp
        import numpy as np
        B, T, DM, H, DH = (4, 256, 128, 16, 64)
        DI = H * DH
        CLIP = 1.0
        LN_EPS = 1e-05
        key = jax.random.key(seed)
        ks = jax.random.split(key, 9)

        def xav(k, shape):
            lim = float(np.sqrt(6.0 / (shape[0] + shape[1])))
            return jax.random.uniform(k, shape, jnp.float32, -lim, lim)

        def kai(k, shape):
            lim = float(1.0 / np.sqrt(shape[1]))
            return jax.random.uniform(k, shape, jnp.float32, -lim, lim)
        return {'x': jax.random.normal(ks[0], (B, T, DM), jnp.float32), 'Wq': xav(ks[1], (DI, DM)), 'Wk': xav(ks[2], (DI, DM)), 'Wv': xav(ks[3], (DI, DM)), 'Wa': kai(ks[4], (DI, DM)), 'ba': jnp.full((DI,), 3.0, jnp.float32), 'Wb': kai(ks[5], (H, DM)), 'bb': jnp.zeros((H,), jnp.float32), 'Wg': kai(ks[6], (H, DM)), 'bg': jnp.zeros((H,), jnp.float32), 'WaR': kai(ks[7], (DI, DM)), 'baR': jnp.full((DI,), 3.0, jnp.float32), 'Wo': xav(ks[8], (DM, DI)), 'ln_w': jnp.ones((DM,), jnp.float32), 'ln_b': jnp.zeros((DM,), jnp.float32)}
    _L1_attn_all = _L1_attn_setup()
    _L1_attn_in = {k: v for k, v in _L1_attn_all.items() if k in ('Wq', 'Wk', 'Wv', 'Wa', 'ba', 'Wb', 'bb', 'Wg', 'bg', 'WaR', 'baR', 'Wo', 'ln_w', 'ln_b')}
    del _L1_attn_all

    def _L1_ffn_setup():
        import jax, jax.numpy as jnp
        import numpy as np
        QMAX = 127.0
        EPS = 1e-08

        def _quantize_per_token(x):
            amax = jnp.clip(jnp.max(jnp.abs(x), axis=-1, keepdims=True), EPS, None)
            scale = amax / QMAX
            x_q = jnp.clip(jnp.round(x / scale), -128, 127)
            return (x_q, scale)

        def _quantize_per_channel(w):
            amax = jnp.clip(jnp.max(jnp.abs(w), axis=-1, keepdims=True), EPS, None)
            scale = amax / QMAX
            w_q = jnp.clip(jnp.round(w / scale), -128, 127)
            return (w_q, scale)
        key = jax.random.key(seed)
        k1, k2, k3 = jax.random.split(key, 3)
        B, S, DIN, DOUT = (8, 512, 128, 128)
        x = jax.random.normal(k1, (B, S, DIN), dtype=jnp.float32)
        weight = jax.random.normal(k2, (DOUT, DIN), dtype=jnp.float32) * 0.02
        bias = jax.random.normal(k3, (DOUT,), dtype=jnp.float32)
        return {'x': x, 'weight': weight, 'bias': bias}
    _L1_ffn_all = _L1_ffn_setup()
    _L1_ffn_in = {k: v for k, v in _L1_ffn_all.items() if k in ('weight', 'bias')}
    del _L1_ffn_all

    def _L2_xattn_setup():
        import jax, jax.numpy as jnp
        import numpy as np
        B, LQ, LK, D = (4, 256, 256, 128)
        H = 16
        HD = D // H

        def _split_heads(x):
            b, l, _ = x.shape
            return x.reshape(b, l, H, HD).transpose(0, 2, 1, 3)
        key = jax.random.key(seed)
        ks = jax.random.split(key, 10)
        s = 0.02
        return {'hidden_states': jax.random.normal(ks[0], (B, LQ, D), jnp.float32), 'context': jax.random.normal(ks[1], (B, LK, D), jnp.float32), 'attention_mask': jax.random.randint(ks[2], (B, LK), 0, 2, jnp.int32), 'q_w': jax.random.normal(ks[3], (D, D), jnp.float32) * s, 'q_b': jnp.zeros((D,), jnp.float32), 'k_w': jax.random.normal(ks[4], (D, D), jnp.float32) * s, 'k_b': jnp.zeros((D,), jnp.float32), 'v_w': jax.random.normal(ks[5], (D, D), jnp.float32) * s, 'v_b': jnp.zeros((D,), jnp.float32)}
    _L2_xattn_all = _L2_xattn_setup()
    _L2_xattn_in = {k: v for k, v in _L2_xattn_all.items() if k in ('q_w', 'q_b', 'k_w', 'k_b', 'v_w', 'v_b')}
    del _L2_xattn_all

    def _L2_attn_setup():
        import jax, jax.numpy as jnp
        import numpy as np
        B, S, D = (4, 512, 128)
        H, HD = (16, 64)
        EPS = 1e-06

        def _feature_map(t):
            return jax.nn.elu(t) + 1.0
        key = jax.random.key(seed)
        ks = jax.random.split(key, 9)
        sd = 1.0 / np.sqrt(D)
        x = jax.random.normal(ks[0], (B, S, D), dtype=jnp.float32)
        wq = jax.random.normal(ks[1], (D, H, HD), dtype=jnp.float32) * sd
        bq = jnp.zeros((H, HD), dtype=jnp.float32)
        wk = jax.random.normal(ks[2], (D, H, HD), dtype=jnp.float32) * sd
        bk = jnp.zeros((H, HD), dtype=jnp.float32)
        wv = jax.random.normal(ks[3], (D, H, HD), dtype=jnp.float32) * sd
        bv = jnp.zeros((H, HD), dtype=jnp.float32)
        wo = jax.random.normal(ks[4], (H, HD, D), dtype=jnp.float32) * (1.0 / np.sqrt(H * HD))
        bo = jnp.zeros((D,), dtype=jnp.float32)
        return {'x': x, 'wq': wq, 'bq': bq, 'wk': wk, 'bk': bk, 'wv': wv, 'bv': bv, 'wo': wo, 'bo': bo}
    _L2_attn_all = _L2_attn_setup()
    _L2_attn_in = {k: v for k, v in _L2_attn_all.items() if k in ('wq', 'bq', 'wk', 'bk', 'wv', 'bv', 'wo', 'bo')}
    del _L2_attn_all

    def _L2_ffn_setup():
        import jax, jax.numpy as jnp
        import numpy as np
        E = 16
        F_C = 2.0
        D = 128
        I = 4 * D
        IS = 2 * D
        B, S = (4, 128)
        key = jax.random.key(seed)
        ks = jax.random.split(key, 8)
        w = 0.02
        return {'hidden_states': jax.random.normal(ks[0], (B, S, D), dtype=jnp.float32), 'gate_w': jax.random.normal(ks[1], (E, D), dtype=jnp.float32) * w, 'Wg': jax.random.normal(ks[2], (E, I, D), dtype=jnp.float32) * w, 'Wu': jax.random.normal(ks[3], (E, I, D), dtype=jnp.float32) * w, 'Wd': jax.random.normal(ks[4], (E, D, I), dtype=jnp.float32) * w, 'Sg': jax.random.normal(ks[5], (IS, D), dtype=jnp.float32) * w, 'Su': jax.random.normal(ks[6], (IS, D), dtype=jnp.float32) * w, 'Sd': jax.random.normal(ks[7], (D, IS), dtype=jnp.float32) * w}
    _L2_ffn_all = _L2_ffn_setup()
    _L2_ffn_in = {k: v for k, v in _L2_ffn_all.items() if k in ('gate_w', 'Wg', 'Wu', 'Wd', 'Sg', 'Su', 'Sd')}
    del _L2_ffn_all

    def _L3_xattn_setup():
        import jax, jax.numpy as jnp
        import numpy as np
        N_EMBD = 128
        N_HEAD = 16
        R = 16
        SCALING = 1.0 / 16.0

        def lora_linear(x, W, b, A, B):
            return x @ W.T + b + x @ A.T @ B.T * SCALING
        key = jax.random.key(seed)
        ks = jax.random.split(key, 16)
        B, T, S, C = (8, 128, 32, N_EMBD)
        std = 0.02
        return {'x': jax.random.normal(ks[0], (B, T, C), jnp.float32), 'feature': jax.random.normal(ks[1], (B, S, C), jnp.float32), 'Wq': jax.random.normal(ks[2], (C, C), jnp.float32) * std, 'bq': jnp.zeros((C,), jnp.float32), 'Aq': jax.random.normal(ks[3], (R, C), jnp.float32) * std, 'Bq': jnp.zeros((C, R), jnp.float32), 'Wf': jax.random.normal(ks[4], (2 * C, C), jnp.float32) * std, 'bf': jnp.zeros((2 * C,), jnp.float32), 'Af': jax.random.normal(ks[5], (R, C), jnp.float32) * std, 'Bf': jnp.zeros((2 * C, R), jnp.float32), 'Wp': jax.random.normal(ks[6], (C, C), jnp.float32) * std, 'bp': jnp.zeros((C,), jnp.float32), 'Ap': jax.random.normal(ks[7], (R, C), jnp.float32) * std, 'Bp': jnp.zeros((C, R), jnp.float32)}
    _L3_xattn_all = _L3_xattn_setup()
    _L3_xattn_in = {k: v for k, v in _L3_xattn_all.items() if k in ('Wq', 'bq', 'Aq', 'Bq', 'Wf', 'bf', 'Af', 'Bf', 'Wp', 'bp', 'Ap', 'Bp')}
    del _L3_xattn_all

    def _L3_attn_setup():
        import jax, jax.numpy as jnp
        import numpy as np
        NUM_HEADS = 16
        EPS = 1e-06

        def _phi(x):
            return jax.nn.elu(x) + 1.0
        key = jax.random.key(seed)
        ks = jax.random.split(key, 5)
        B, L, D = (4, 1024, 128)
        scale = 0.02
        return {'x': jax.random.normal(ks[0], (B, L, D), dtype=jnp.float32), 'Wq': jax.random.normal(ks[1], (D, D), dtype=jnp.float32) * scale, 'Wk': jax.random.normal(ks[2], (D, D), dtype=jnp.float32) * scale, 'Wv': jax.random.normal(ks[3], (D, D), dtype=jnp.float32) * scale, 'Wo': jax.random.normal(ks[4], (D, D), dtype=jnp.float32) * scale}
    _L3_attn_all = _L3_attn_setup()
    _L3_attn_in = {k: v for k, v in _L3_attn_all.items() if k in ('Wq', 'Wk', 'Wv', 'Wo')}
    del _L3_attn_all

    def _L3_ffn_setup():
        import jax, jax.numpy as jnp
        import numpy as np
        B, S, D, E = (2, 512, 128, 8)
        key = jax.random.key(seed)
        ks = jax.random.split(key, 7)
        s = 1.0 / np.sqrt(D)
        return {'x': jax.random.normal(ks[0], (B, S, D), jnp.float32), 'Ws': jax.random.normal(ks[1], (E, D), jnp.float32) * s, 'bs': jax.random.normal(ks[2], (E,), jnp.float32) * s, 'W1': jax.random.normal(ks[3], (E, D, D), jnp.float32) * s, 'b1': jax.random.normal(ks[4], (E, D), jnp.float32) * s, 'W2': jax.random.normal(ks[5], (E, D, D), jnp.float32) * s, 'b2': jax.random.normal(ks[6], (E, D), jnp.float32) * s}
    _L3_ffn_all = _L3_ffn_setup()
    _L3_ffn_in = {k: v for k, v in _L3_ffn_all.items() if k in ('Ws', 'bs', 'W1', 'b1', 'W2', 'b2')}
    del _L3_ffn_all
    return {'x': x, 'ctx_1024': ctx_1024, 'mask_1xSxS2_ff0': mask_1xSxS2_ff0, 'mask_BxS2_ik0': mask_BxS2_ik0, 'L0_xattn_kernel_q': _L0_xattn_in['kernel_q'], 'L0_xattn_kernel_k': _L0_xattn_in['kernel_k'], 'L0_xattn_kernel_v': _L0_xattn_in['kernel_v'], 'L0_xattn_bias_q': _L0_xattn_in['bias_q'], 'L0_xattn_bias_k': _L0_xattn_in['bias_k'], 'L0_xattn_bias_v': _L0_xattn_in['bias_v'], 'L0_attn_Wqkv': _L0_attn_in['Wqkv'], 'L0_attn_Wproj': _L0_attn_in['Wproj'], 'L0_attn_cascade_w': _L0_attn_in['cascade_w'], 'L0_ffn_centroids': _L0_ffn_in['centroids'], 'L0_ffn_ln_g': _L0_ffn_in['ln_g'], 'L0_ffn_ln_b': _L0_ffn_in['ln_b'], 'L0_ffn_w1': _L0_ffn_in['w1'], 'L0_ffn_b1': _L0_ffn_in['b1'], 'L0_ffn_w2': _L0_ffn_in['w2'], 'L0_ffn_b2': _L0_ffn_in['b2'], 'L1_xattn_Wq': _L1_xattn_in['Wq'], 'L1_xattn_bq': _L1_xattn_in['bq'], 'L1_xattn_Wk': _L1_xattn_in['Wk'], 'L1_xattn_bk': _L1_xattn_in['bk'], 'L1_xattn_Wv': _L1_xattn_in['Wv'], 'L1_xattn_bv': _L1_xattn_in['bv'], 'L1_xattn_Wo': _L1_xattn_in['Wo'], 'L1_xattn_bo': _L1_xattn_in['bo'], 'L1_attn_Wq': _L1_attn_in['Wq'], 'L1_attn_Wk': _L1_attn_in['Wk'], 'L1_attn_Wv': _L1_attn_in['Wv'], 'L1_attn_Wa': _L1_attn_in['Wa'], 'L1_attn_ba': _L1_attn_in['ba'], 'L1_attn_Wb': _L1_attn_in['Wb'], 'L1_attn_bb': _L1_attn_in['bb'], 'L1_attn_Wg': _L1_attn_in['Wg'], 'L1_attn_bg': _L1_attn_in['bg'], 'L1_attn_WaR': _L1_attn_in['WaR'], 'L1_attn_baR': _L1_attn_in['baR'], 'L1_attn_Wo': _L1_attn_in['Wo'], 'L1_attn_ln_w': _L1_attn_in['ln_w'], 'L1_attn_ln_b': _L1_attn_in['ln_b'], 'L1_ffn_weight': _L1_ffn_in['weight'], 'L1_ffn_bias': _L1_ffn_in['bias'], 'L2_xattn_q_w': _L2_xattn_in['q_w'], 'L2_xattn_q_b': _L2_xattn_in['q_b'], 'L2_xattn_k_w': _L2_xattn_in['k_w'], 'L2_xattn_k_b': _L2_xattn_in['k_b'], 'L2_xattn_v_w': _L2_xattn_in['v_w'], 'L2_xattn_v_b': _L2_xattn_in['v_b'], 'L2_attn_wq': _L2_attn_in['wq'], 'L2_attn_bq': _L2_attn_in['bq'], 'L2_attn_wk': _L2_attn_in['wk'], 'L2_attn_bk': _L2_attn_in['bk'], 'L2_attn_wv': _L2_attn_in['wv'], 'L2_attn_bv': _L2_attn_in['bv'], 'L2_attn_wo': _L2_attn_in['wo'], 'L2_attn_bo': _L2_attn_in['bo'], 'L2_ffn_gate_w': _L2_ffn_in['gate_w'], 'L2_ffn_Wg': _L2_ffn_in['Wg'], 'L2_ffn_Wu': _L2_ffn_in['Wu'], 'L2_ffn_Wd': _L2_ffn_in['Wd'], 'L2_ffn_Sg': _L2_ffn_in['Sg'], 'L2_ffn_Su': _L2_ffn_in['Su'], 'L2_ffn_Sd': _L2_ffn_in['Sd'], 'L3_xattn_Wq': _L3_xattn_in['Wq'], 'L3_xattn_bq': _L3_xattn_in['bq'], 'L3_xattn_Aq': _L3_xattn_in['Aq'], 'L3_xattn_Bq': _L3_xattn_in['Bq'], 'L3_xattn_Wf': _L3_xattn_in['Wf'], 'L3_xattn_bf': _L3_xattn_in['bf'], 'L3_xattn_Af': _L3_xattn_in['Af'], 'L3_xattn_Bf': _L3_xattn_in['Bf'], 'L3_xattn_Wp': _L3_xattn_in['Wp'], 'L3_xattn_bp': _L3_xattn_in['bp'], 'L3_xattn_Ap': _L3_xattn_in['Ap'], 'L3_xattn_Bp': _L3_xattn_in['Bp'], 'L3_attn_Wq': _L3_attn_in['Wq'], 'L3_attn_Wk': _L3_attn_in['Wk'], 'L3_attn_Wv': _L3_attn_in['Wv'], 'L3_attn_Wo': _L3_attn_in['Wo'], 'L3_ffn_Ws': _L3_ffn_in['Ws'], 'L3_ffn_bs': _L3_ffn_in['bs'], 'L3_ffn_W1': _L3_ffn_in['W1'], 'L3_ffn_b1': _L3_ffn_in['b1'], 'L3_ffn_W2': _L3_ffn_in['W2'], 'L3_ffn_b2': _L3_ffn_in['b2']}

def reference(x, ctx_1024, mask_1xSxS2_ff0, mask_BxS2_ik0, L0_xattn_kernel_q, L0_xattn_kernel_k, L0_xattn_kernel_v, L0_xattn_bias_q, L0_xattn_bias_k, L0_xattn_bias_v, L0_attn_Wqkv, L0_attn_Wproj, L0_attn_cascade_w, L0_ffn_centroids, L0_ffn_ln_g, L0_ffn_ln_b, L0_ffn_w1, L0_ffn_b1, L0_ffn_w2, L0_ffn_b2, L1_xattn_Wq, L1_xattn_bq, L1_xattn_Wk, L1_xattn_bk, L1_xattn_Wv, L1_xattn_bv, L1_xattn_Wo, L1_xattn_bo, L1_attn_Wq, L1_attn_Wk, L1_attn_Wv, L1_attn_Wa, L1_attn_ba, L1_attn_Wb, L1_attn_bb, L1_attn_Wg, L1_attn_bg, L1_attn_WaR, L1_attn_baR, L1_attn_Wo, L1_attn_ln_w, L1_attn_ln_b, L1_ffn_weight, L1_ffn_bias, L2_xattn_q_w, L2_xattn_q_b, L2_xattn_k_w, L2_xattn_k_b, L2_xattn_v_w, L2_xattn_v_b, L2_attn_wq, L2_attn_bq, L2_attn_wk, L2_attn_bk, L2_attn_wv, L2_attn_bv, L2_attn_wo, L2_attn_bo, L2_ffn_gate_w, L2_ffn_Wg, L2_ffn_Wu, L2_ffn_Wd, L2_ffn_Sg, L2_ffn_Su, L2_ffn_Sd, L3_xattn_Wq, L3_xattn_bq, L3_xattn_Aq, L3_xattn_Bq, L3_xattn_Wf, L3_xattn_bf, L3_xattn_Af, L3_xattn_Bf, L3_xattn_Wp, L3_xattn_bp, L3_xattn_Ap, L3_xattn_Bp, L3_attn_Wq, L3_attn_Wk, L3_attn_Wv, L3_attn_Wo, L3_ffn_Ws, L3_ffn_bs, L3_ffn_W1, L3_ffn_b1, L3_ffn_W2, L3_ffn_b2):
    import jax
    import jax.numpy as jnp

    def _L0_xattn_ref(q, k, v, mask, kernel_q, kernel_k, kernel_v, bias_q, bias_k, bias_v):
        import jax, jax.numpy as jnp
        import numpy as np
        B, S, D_IN, D_MODEL = (4, 256, 128, 128)
        Wq, Wk, Wv = (kernel_q[0, 0], kernel_k[0, 0], kernel_v[0, 0])
        qp = jax.nn.relu(jnp.einsum('bsd,de->bse', q, Wq) + bias_q)
        kp = jax.nn.relu(jnp.einsum('bsd,de->bse', k, Wk) + bias_k)
        vp = jax.nn.relu(jnp.einsum('bsd,de->bse', v, Wv) + bias_v)
        scores = jax.nn.relu(jnp.einsum('bqe,bke->bqk', qp, kp))
        dk = jnp.asarray(kp.shape[-1], dtype=scores.dtype)
        logits = scores / jnp.sqrt(dk) + mask
        out = jax.nn.relu(jnp.einsum('bqk,bke->bqe', logits, vp))
        return out

    def _L0_attn_ref(x, Wqkv, Wproj, cascade_w):
        import jax, jax.numpy as jnp
        import numpy as np
        N_EMBD = 128
        N_HEAD = 16
        HEAD_DIM = N_EMBD // N_HEAD
        ROPE_BASE = 10000.0

        def _apply_rotary(x, cos, sin):
            x1, x2 = (x[..., 0::2], x[..., 1::2])
            return jnp.concatenate([x1 * cos - x2 * sin, x1 * sin + x2 * cos], axis=-1)
        B, T, C = x.shape
        H, hd = (N_HEAD, HEAD_DIM)
        qkv = x @ Wqkv
        q, k, v = jnp.split(qkv, 3, axis=-1)
        q = q.reshape(B, T, H, hd).transpose(0, 2, 1, 3)
        k = k.reshape(B, T, H, hd).transpose(0, 2, 1, 3)
        v = v.reshape(B, T, H, hd).transpose(0, 2, 1, 3)
        inv_freq = 1.0 / ROPE_BASE ** (jnp.arange(0, hd, 2, dtype=jnp.float32) / hd)
        t = jnp.arange(T, dtype=jnp.float32)
        causal = jnp.triu(jnp.ones((T, T), dtype=bool), k=1)
        scale = 1.0 / np.sqrt(hd)
        head_outputs = []
        cascade_bias = None
        for i in range(H):
            freq_scale = ROPE_BASE ** (i / H)
            freqs = jnp.outer(t, inv_freq * freq_scale)
            cos, sin = (jnp.cos(freqs), jnp.sin(freqs))
            q_rot = _apply_rotary(q[:, i], cos, sin)
            k_rot = _apply_rotary(k[:, i], cos, sin)
            att = jnp.einsum('btd,bsd->bts', q_rot, k_rot) * scale
            if cascade_bias is not None:
                att = att + cascade_w[i - 1] * cascade_bias
            att = jnp.where(causal, -jnp.inf, att)
            att = jax.nn.softmax(att, axis=-1)
            out_i = jnp.einsum('bts,bsd->btd', att, v[:, i])
            head_outputs.append(out_i)
            cascade_bias = jnp.mean(att, axis=1, keepdims=True)
        out = jnp.concatenate(head_outputs, axis=-1)
        return out @ Wproj

    def _L0_ffn_ref(input_features, centroids, ln_g, ln_b, w1, b1, w2, b2):
        import jax, jax.numpy as jnp
        import numpy as np
        E, D, F = (8, 128, 512)
        LN_EPS = 1e-05
        x = input_features.reshape(-1, D)
        aff = jax.lax.stop_gradient(x) @ centroids.T
        assign = jnp.argmax(aff, axis=1)
        onehot = jax.nn.one_hot(assign, E, dtype=x.dtype)
        mu = jnp.mean(x, axis=-1, keepdims=True)
        var = jnp.mean((x - mu) ** 2, axis=-1, keepdims=True)
        xhat = (x - mu) * jax.lax.rsqrt(var + LN_EPS)
        xn = xhat[None, :, :] * ln_g[:, None, :] + ln_b[:, None, :]
        h = jax.nn.relu(jnp.einsum('etd,efd->etf', xn, w1) + b1[:, None, :])
        y = x[None, :, :] + jnp.einsum('etf,edf->etd', h, w2) + b2[:, None, :]
        alpha = jax.nn.sigmoid(x @ centroids.T)
        a = alpha.T[:, :, None]
        gated = a * y + (1.0 - a) * x[None, :, :]
        out = jnp.einsum('te,etd->td', onehot, gated)
        return out.reshape(input_features.shape)

    def _L1_xattn_ref(query, key, value, Wq, bq, Wk, bk, Wv, bv, Wo, bo):
        import jax, jax.numpy as jnp
        import numpy as np
        D_MODEL = 128
        N_HEADS = 16
        HEAD_DIM = 64
        B, Sq, _ = query.shape
        Sk = key.shape[1]
        q = (query @ Wq + bq).reshape(B, Sq, N_HEADS, HEAD_DIM).transpose(0, 2, 1, 3)
        k = (key @ Wk + bk).reshape(B, Sk, N_HEADS, HEAD_DIM).transpose(0, 2, 1, 3)
        v = (value @ Wv + bv).reshape(B, Sk, N_HEADS, HEAD_DIM).transpose(0, 2, 1, 3)
        scores = jnp.einsum('bhqd,bhkd->bhqk', q, k) / np.sqrt(HEAD_DIM).astype(np.float32)
        probs = jax.nn.softmax(scores, axis=-1)
        z = jnp.einsum('bhqk,bhkd->bhqd', probs, v)
        z = z.transpose(0, 2, 1, 3).reshape(B, Sq, N_HEADS * HEAD_DIM)
        return z @ Wo + bo

    def _L1_attn_ref(x, Wq, Wk, Wv, Wa, ba, Wb, bb, Wg, bg, WaR, baR, Wo, ln_w, ln_b):
        import jax, jax.numpy as jnp
        import numpy as np
        B, T, DM, H, DH = (4, 256, 128, 16, 64)
        DI = H * DH
        CLIP = 1.0
        LN_EPS = 1e-05
        Bs, Ts, _ = x.shape
        residual = x
        mu = jnp.mean(x, -1, keepdims=True)
        var = jnp.mean((x - mu) ** 2, -1, keepdims=True)
        xn = (x - mu) / jnp.sqrt(var + LN_EPS) * ln_w + ln_b
        q = (xn @ Wq.T).reshape(Bs, Ts, H, DH)
        k = (xn @ Wk.T).reshape(Bs, Ts, H, DH)
        v = (xn @ Wv.T).reshape(Bs, Ts, H, DH)
        alpha = jax.nn.sigmoid(xn @ Wa.T + ba).reshape(Bs, Ts, H, DH)
        aR = jax.nn.sigmoid(xn @ WaR.T + baR).reshape(Bs, Ts, H, DH)
        beta = jax.nn.sigmoid(xn @ Wb.T + bb)
        gamma = jax.nn.sigmoid(xn @ Wg.T + bg)
        tm = lambda a: jnp.moveaxis(a, 1, 0)
        xs = (tm(q), tm(k), tm(v), tm(alpha), tm(aR), tm(beta), tm(gamma))
        S0 = jnp.zeros((Bs, H, DH, DH), x.dtype)

        def step(carry, inp):
            S, R = carry
            q_t, k_t, v_t, a_t, aR_t, b_t, g_t = inp
            kn = k_t / jnp.maximum(jnp.linalg.norm(k_t, axis=-1, keepdims=True), 1e-12)
            pred = jnp.einsum('bhji,bhj->bhi', S, kn)
            r = jnp.clip(v_t - pred, -CLIP, CLIP)
            S = a_t[..., None] * S
            kp = jnp.einsum('bhd,bhde->bhe', kn, S)
            S = S + b_t[..., None, None] * kn[..., None] * (v_t - kp)[..., None, :]
            o = jnp.einsum('bhji,bhj->bhi', S, q_t)
            R = aR_t[..., None] * R
            kpR = jnp.einsum('bhd,bhde->bhe', kn, R)
            R = R + g_t[..., None, None] * kn[..., None] * (r - kpR)[..., None, :]
            o = o + jnp.einsum('bhji,bhj->bhi', R, q_t)
            return ((S, R), o)
        _, os = jax.lax.scan(step, (S0, S0), xs)
        out = jnp.moveaxis(os, 0, 1).reshape(Bs, Ts, DI) @ Wo.T
        return out + residual

    def _L1_ffn_ref(x, weight, bias):
        import jax, jax.numpy as jnp
        import numpy as np
        QMAX = 127.0
        EPS = 1e-08

        def _quantize_per_token(x):
            amax = jnp.clip(jnp.max(jnp.abs(x), axis=-1, keepdims=True), EPS, None)
            scale = amax / QMAX
            x_q = jnp.clip(jnp.round(x / scale), -128, 127)
            return (x_q, scale)

        def _quantize_per_channel(w):
            amax = jnp.clip(jnp.max(jnp.abs(w), axis=-1, keepdims=True), EPS, None)
            scale = amax / QMAX
            w_q = jnp.clip(jnp.round(w / scale), -128, 127)
            return (w_q, scale)
        B, S, DIN = x.shape
        w_q, w_scale = _quantize_per_channel(weight.astype(jnp.float32))
        x_flat = x.reshape(-1, DIN).astype(jnp.float32)
        x_q, x_scale = _quantize_per_token(x_flat)
        out = jnp.matmul(x_q, w_q.T) * x_scale * w_scale.T
        out = out.reshape(B, S, -1) + bias
        return out.astype(x.dtype)

    def _L2_xattn_ref(hidden_states, context, attention_mask, q_w, q_b, k_w, k_b, v_w, v_b):
        import jax, jax.numpy as jnp
        import numpy as np
        B, LQ, LK, D = (4, 256, 256, 128)
        H = 16
        HD = D // H

        def _split_heads(x):
            b, l, _ = x.shape
            return x.reshape(b, l, H, HD).transpose(0, 2, 1, 3)
        q = _split_heads(hidden_states @ q_w.T + q_b)
        k = _split_heads(context @ k_w.T + k_b)
        v = _split_heads(context @ v_w.T + v_b)
        scores = jnp.einsum('bhqd,bhkd->bhqk', q, k) / jnp.sqrt(jnp.float32(HD))
        mask = (attention_mask > 0)[:, None, None, :]
        scores = jnp.where(mask, -jnp.inf, scores)
        probs = jax.nn.softmax(scores, axis=-1)
        ctx = jnp.einsum('bhqk,bhkd->bhqd', probs, v)
        ctx = ctx.transpose(0, 2, 1, 3).reshape(ctx.shape[0], ctx.shape[2], H * HD)
        return ctx

    def _L2_attn_ref(x, wq, bq, wk, bk, wv, bv, wo, bo):
        import jax, jax.numpy as jnp
        import numpy as np
        B, S, D = (4, 512, 128)
        H, HD = (16, 64)
        EPS = 1e-06

        def _feature_map(t):
            return jax.nn.elu(t) + 1.0
        q = jnp.einsum('nsf,fhd->nshd', x, wq) + bq
        k = jnp.einsum('nsf,fhd->nshd', x, wk) + bk
        v = jnp.einsum('nsf,fhd->nshd', x, wv) + bv
        qm = _feature_map(q)
        km = _feature_map(k)
        kv = jnp.einsum('nshd,nshm->nhmd', km, v)
        z = 1.0 / (jnp.einsum('nlhd,nhd->nlh', qm, jnp.sum(km, axis=1)) + EPS)
        y = jnp.einsum('nlhd,nhmd,nlh->nlhm', qm, kv, z)
        out = jnp.einsum('nlhm,hmf->nlf', y, wo) + bo
        return out

    def _L2_ffn_ref(hidden_states, gate_w, Wg, Wu, Wd, Sg, Su, Sd):
        import jax, jax.numpy as jnp
        import numpy as np
        E = 16
        F_C = 2.0
        D = 128
        I = 4 * D
        IS = 2 * D
        B, S = (4, 128)
        b, s, d = hidden_states.shape
        T = b * s
        C = int(T * F_C / E)
        flat_x = hidden_states.reshape(T, d)
        logits = flat_x @ gate_w.T
        scores = jax.nn.softmax(logits, axis=-1).T
        topk_weight, topk_idx = jax.lax.top_k(scores, C)
        xg = flat_x[topk_idx]
        g = jnp.einsum('ecd,eid->eci', xg, Wg)
        u = jnp.einsum('ecd,eid->eci', xg, Wu)
        h = jax.nn.gelu(g, approximate=False) * u
        eo = jnp.einsum('eci,edi->ecd', h, Wd)
        eo = eo * topk_weight[..., None]
        flat_out = jnp.zeros_like(flat_x).at[topk_idx.reshape(-1)].add(eo.reshape(-1, d))
        out = flat_out.reshape(b, s, d)
        sg = hidden_states @ Sg.T
        su = hidden_states @ Su.T
        shared = jax.nn.gelu(sg, approximate=False) * su @ Sd.T
        return out + shared

    def _L3_xattn_ref(x, feature, Wq, bq, Aq, Bq, Wf, bf, Af, Bf, Wp, bp, Ap, Bp):
        import jax, jax.numpy as jnp
        import numpy as np
        N_EMBD = 128
        N_HEAD = 16
        R = 16
        SCALING = 1.0 / 16.0

        def lora_linear(x, W, b, A, B):
            return x @ W.T + b + x @ A.T @ B.T * SCALING
        Bsz, T, C = x.shape
        S = feature.shape[1]
        H = N_HEAD
        D = C // H
        q = lora_linear(x, Wq, bq, Aq, Bq).reshape(Bsz, T, H, D).transpose(0, 2, 1, 3)
        kv = lora_linear(feature, Wf, bf, Af, Bf)
        k, v = (kv[..., :C], kv[..., C:])
        k = k.reshape(Bsz, S, H, D).transpose(0, 2, 1, 3)
        v = v.reshape(Bsz, S, H, D).transpose(0, 2, 1, 3)
        att = jnp.einsum('bhtd,bhsd->bhts', q, k) * (1.0 / np.sqrt(D))
        mask = jnp.tril(jnp.ones((T, S), bool))
        att = jnp.where(mask, att, -jnp.inf)
        att = jax.nn.softmax(att, axis=-1)
        y = jnp.einsum('bhts,bhsd->bhtd', att, v)
        y = y.transpose(0, 2, 1, 3).reshape(Bsz, T, C)
        return lora_linear(y, Wp, bp, Ap, Bp)

    def _L3_attn_ref(x, Wq, Wk, Wv, Wo):
        import jax, jax.numpy as jnp
        import numpy as np
        NUM_HEADS = 16
        EPS = 1e-06

        def _phi(x):
            return jax.nn.elu(x) + 1.0
        B, L, D = x.shape
        H = NUM_HEADS
        dh = D // H
        Q = x @ Wq
        K = x @ Wk
        V = x @ Wv
        Qh = Q.reshape(B, L, H, dh).transpose(0, 2, 1, 3)
        Kh = K.reshape(B, L, H, dh).transpose(0, 2, 1, 3)
        Vh = V.reshape(B, L, H, dh).transpose(0, 2, 1, 3)
        Qf = _phi(Qh)
        Kf = _phi(Kh)
        Kv = jnp.einsum('bhlm,bhln->bhmn', Kf, Vh)
        K1 = jnp.sum(Kf, axis=2)
        num = jnp.einsum('bhlm,bhmn->bhln', Qf, Kv)
        den = jnp.einsum('bhlm,bhm->bhl', Qf, K1) + EPS
        out = num / den[..., None]
        out = out.transpose(0, 2, 1, 3).reshape(B, L, D)
        return out @ Wo

    def _L3_ffn_ref(x, Ws, bs, W1, b1, W2, b2):
        import jax, jax.numpy as jnp
        import numpy as np
        B, S, D, E = (2, 512, 128, 8)
        b, s, d = x.shape
        xf = x.reshape(-1, d)
        logits = xf @ Ws.T + bs
        probs = jax.nn.softmax(logits, axis=-1)
        routes = jnp.argmax(probs, axis=-1)
        pmax = jnp.max(probs, axis=-1)
        xf = xf * pmax[:, None]
        perm = jnp.argsort(routes, stable=True)
        xs = xf[perm]
        rs = routes[perm]
        h = jax.nn.relu(jnp.einsum('td,edf->etf', xs, W1) + b1[:, None, :])
        y = jnp.einsum('etf,efd->etd', h, W2) + b2[:, None, :]
        out = y[rs, jnp.arange(rs.shape[0])]
        return out.reshape(b, s, d)
    x = x + _L0_xattn_ref(_layernorm(x, axis=-1), ctx_1024, ctx_1024, mask_1xSxS2_ff0, L0_xattn_kernel_q, L0_xattn_kernel_k, L0_xattn_kernel_v, L0_xattn_bias_q, L0_xattn_bias_k, L0_xattn_bias_v)
    x = x + _L0_attn_ref(_layernorm(x, axis=-1), L0_attn_Wqkv, L0_attn_Wproj, L0_attn_cascade_w)
    x = x + _L0_ffn_ref(_layernorm(x, axis=-1), L0_ffn_centroids, L0_ffn_ln_g, L0_ffn_ln_b, L0_ffn_w1, L0_ffn_b1, L0_ffn_w2, L0_ffn_b2)
    x = x + _L1_xattn_ref(_layernorm(x, axis=-1), ctx_1024, ctx_1024, L1_xattn_Wq, L1_xattn_bq, L1_xattn_Wk, L1_xattn_bk, L1_xattn_Wv, L1_xattn_bv, L1_xattn_Wo, L1_xattn_bo)
    x = x + _L1_attn_ref(_layernorm(x, axis=-1), L1_attn_Wq, L1_attn_Wk, L1_attn_Wv, L1_attn_Wa, L1_attn_ba, L1_attn_Wb, L1_attn_bb, L1_attn_Wg, L1_attn_bg, L1_attn_WaR, L1_attn_baR, L1_attn_Wo, L1_attn_ln_w, L1_attn_ln_b)
    x = x + _L1_ffn_ref(_layernorm(x, axis=-1), L1_ffn_weight, L1_ffn_bias)
    x = x + _L2_xattn_ref(_layernorm(x, axis=-1), ctx_1024, mask_BxS2_ik0, L2_xattn_q_w, L2_xattn_q_b, L2_xattn_k_w, L2_xattn_k_b, L2_xattn_v_w, L2_xattn_v_b)
    x = x + _L2_attn_ref(_layernorm(x, axis=-1), L2_attn_wq, L2_attn_bq, L2_attn_wk, L2_attn_bk, L2_attn_wv, L2_attn_bv, L2_attn_wo, L2_attn_bo)
    x = x + _L2_ffn_ref(_layernorm(x, axis=-1), L2_ffn_gate_w, L2_ffn_Wg, L2_ffn_Wu, L2_ffn_Wd, L2_ffn_Sg, L2_ffn_Su, L2_ffn_Sd)
    x = x + _L3_xattn_ref(_layernorm(x, axis=-1), ctx_1024, L3_xattn_Wq, L3_xattn_bq, L3_xattn_Aq, L3_xattn_Bq, L3_xattn_Wf, L3_xattn_bf, L3_xattn_Af, L3_xattn_Bf, L3_xattn_Wp, L3_xattn_bp, L3_xattn_Ap, L3_xattn_Bp)
    x = x + _L3_attn_ref(_layernorm(x, axis=-1), L3_attn_Wq, L3_attn_Wk, L3_attn_Wv, L3_attn_Wo)
    x = x + _L3_ffn_ref(_layernorm(x, axis=-1), L3_ffn_Ws, L3_ffn_bs, L3_ffn_W1, L3_ffn_b1, L3_ffn_W2, L3_ffn_b2)
    return x

_drawn_inputs = setup_inputs


def setup_inputs(seed=0):
    import zlib

    import numpy as np

    out = dict(_drawn_inputs(seed))
    spreads = {'L0_attn_cascade_w': (0.10000000149011612, 0.6),
     'L0_ffn_ln_g': (1.0, 0.6),
     'L0_ffn_ln_b': (0.0, 0.8),
     'L0_ffn_b1': (0.0, 0.8),
     'L0_ffn_b2': (0.0, 0.8),
     'L1_xattn_bq': (0.0, 0.8),
     'L1_xattn_bk': (0.0, 2.0),
     'L1_xattn_bv': (0.0, 0.8),
     'L1_xattn_bo': (0.0, 0.8),
     'L1_attn_ba': (3.0, 0.6),
     'L1_attn_bb': (0.0, 0.8),
     'L1_attn_bg': (0.0, 0.8),
     'L1_attn_baR': (3.0, 0.6),
     'L1_attn_ln_w': (1.0, 0.6),
     'L1_attn_ln_b': (0.0, 0.8),
     'L2_xattn_q_b': (0.0, 2.0),
     'L2_xattn_k_b': (0.0, 2.0),
     'L2_xattn_v_b': (0.0, 0.8),
     'L2_attn_bq': (0.0, 2.0),
     'L2_attn_bk': (0.0, 2.0),
     'L2_attn_bv': (0.0, 0.8),
     'L2_attn_bo': (0.0, 0.8),
     'L3_xattn_bq': (0.0, 0.8),
     'L3_xattn_Bq': (0.0, 2.0),
     'L3_xattn_bf': (0.0, 0.8),
     'L3_xattn_Bf': (0.0, 0.8),
     'L3_xattn_bp': (0.0, 2.0),
     'L3_xattn_Bp': (0.0, 0.8)}
    factors = {'L0_xattn_bias_q': 6.994,
     'L0_xattn_bias_k': 6.207,
     'L0_attn_Wqkv': 8.0,
     'L0_attn_Wproj': 8.0,
     'L0_ffn_centroids': 8.0,
     'L0_ffn_w1': 8.0,
     'L0_ffn_w2': 8.0,
     'L1_xattn_Wq': 8.0,
     'L1_xattn_Wk': 8.0,
     'L1_xattn_Wv': 8.0,
     'L1_xattn_Wo': 8.0,
     'L1_attn_Wq': 8.0,
     'L1_attn_Wk': 8.0,
     'L1_attn_Wv': 8.0,
     'L1_attn_Wa': 8.0,
     'L1_attn_Wb': 8.0,
     'L1_attn_Wg': 8.0,
     'L1_attn_WaR': 8.0,
     'L1_attn_Wo': 8.0,
     'L1_ffn_weight': 8.0,
     'L1_ffn_bias': 8.0,
     'L2_xattn_q_w': 8.0,
     'L2_xattn_k_w': 8.0,
     'L2_xattn_v_w': 8.0,
     'L2_attn_wq': 8.0,
     'L2_attn_wk': 8.0,
     'L2_attn_wv': 8.0,
     'L2_attn_wo': 8.0,
     'L2_ffn_gate_w': 8.0,
     'L2_ffn_Wg': 8.0,
     'L2_ffn_Wu': 8.0,
     'L2_ffn_Wd': 8.0,
     'L2_ffn_Sg': 8.0,
     'L2_ffn_Su': 8.0,
     'L2_ffn_Sd': 8.0,
     'L3_xattn_Wq': 8.0,
     'L3_xattn_Aq': 37.056,
     'L3_xattn_Wf': 8.0,
     'L3_xattn_Af': 8.0,
     'L3_xattn_Wp': 8.0,
     'L3_xattn_Ap': 23.998,
     'L3_attn_Wq': 64.0,
     'L3_attn_Wk': 37.165,
     'L3_attn_Wv': 8.0,
     'L3_attn_Wo': 8.0,
     'L3_ffn_Ws': 8.0,
     'L3_ffn_bs': 8.0,
     'L3_ffn_W1': 8.0,
     'L3_ffn_b1': 59.226,
     'L3_ffn_W2': 8.0,
     'L3_ffn_b2': 200.0}
    for name, (base, spread) in spreads.items():
        noise = np.random.default_rng([zlib.crc32(name.encode()), seed]).standard_normal(out[name].shape)
        drawn = base * np.exp(spread * noise) if base else spread * noise
        out[name] = jnp.asarray(drawn.astype(out[name].dtype))
    for name, factor in factors.items():
        out[name] = (out[name] * factor).astype(out[name].dtype)
    return out
```

```python
from contextlib import ExitStack

import concourse.bass as bass
import numpy as np
from concourse import mybir

PHASES = (0, 1, 2, 3, 4, 5, 6, 7, 8, 9, 10, 11)

F32 = mybir.dt.float32
BF16 = mybir.dt.bfloat16
I32 = mybir.dt.int32
ALU = mybir.AluOpType
ACT = mybir.ActivationFunctionType
AX = mybir.AxisListType
ds = bass.ds

B, T, D = 64, 32, 128
N = B * T
S2 = 257
KC, NKC = 86, 3
SP2 = KC * NKC
H = 16
CH = 512
NCH = N // CH
TB = 128 // T
NEG = -1.0e30
LN_EPS = 1e-5

CONST = {}
_at = 0
for _name, _w in (("ident", 128), ("mean", 128), ("blk8", 128), ("blk64", 128), ("meanT", 128),
                  ("blk32", 128), ("hmask", H), ("causal", T), ("cos", T), ("sin", T), ("iota", H),
                  ("eps", 1), ("ones", 128), ("bits", 32)):
    CONST[_name] = (_at, _w)
    _at += _w
CW = _at


def constants():
    c = np.zeros((128, CW), np.float32)

    def put(name, a):
        o, w = CONST[name]
        c[:a.shape[0], o:o + w] = a

    p = np.arange(128)
    put("ident", np.eye(128, dtype=np.float32))
    put("mean", np.full((128, 128), 1.0 / D, np.float32))
    put("blk8", (p[:, None] // 8 == p[None] // 8).astype(np.float32))
    put("blk64", (p[:, None] // 64 == p[None] // 64).astype(np.float32))
    put("blk32", (p[:, None] // T == p[None] // T).astype(np.float32))
    put("meanT", (p[:, None] // T == p[None] // T).astype(np.float32) / T)
    put("hmask", (p[:, None] // 8 == np.arange(H)[None]).astype(np.float32))
    put("causal", np.where(np.arange(T)[None] > (p % T)[:, None], NEG, 0.0).astype(np.float32))
    hd = D // H
    inv = (np.float32(1.0) / np.float32(10000.0) ** (np.arange(0, hd, 2, dtype=np.float32) / np.float32(hd)))
    t = np.arange(T, dtype=np.float32)
    cos, sin = np.zeros((128, T), np.float32), np.zeros((128, T), np.float32)
    for h in range(H):
        f = t[:, None] * (inv * np.float32(10000.0 ** (h / H)))[None]
        cos[h * hd:(h + 1) * hd] = np.repeat(np.cos(f).T, 2, 0)
        s = np.repeat(np.sin(f).T, 2, 0)
        s[0::2] *= -1
        sin[h * hd:(h + 1) * hd] = s
    put("cos", cos)
    put("sin", sin)
    put("iota", np.tile(np.arange(H, dtype=np.float32), (128, 1)))
    put("eps", np.full((128, 1), LN_EPS, np.float32))
    put("ones", np.ones((128, 128), np.float32))
    put("bits", np.tile((2.0 ** np.arange(32)).astype(np.float32), (128, 1)))
    return c


class Steps:

    def __init__(self, eng, sem, i=0, per=0, base=0):
        self.eng, self.sem, self.i, self.per, self.base, self.n = eng, sem, i, per, base, 0

    def __call__(self, ins):
        ins.then_inc(self.sem, 1)
        self.n += 1
        self.eng.wait_ge(self.sem, self.i * self.per + self.base + self.n)

    def end(self):
        assert self.per == 0 or self.n == self.per, (self.n, self.per)


class Core:

    def __init__(self, nc, ctx, arr, out):
        self.nc, self.ctx, self.arr, self.out = nc, ctx, arr, out
        self.X = self.sb("X", [128, N])
        self.XN = self.sb("XN", [128, N])
        self.c = self.sb("consts", [128, CW])
        self.ps = [ctx.enter_context(nc.psum_tensor(f"bank{k}", [128, 512], F32)) for k in range(8)]
        self.ln_sems = {n: self.sem("ln_" + n) for n in ("mean", "centred", "square", "var", "std", "steps")}
        self.ln_calls = 0

    def sb(self, name, shape, dt=F32, ctx=None):
        return (ctx or self.ctx).enter_context(self.nc.sbuf_tensor(name, shape, dt))

    def sem(self, name):
        return self.nc.alloc_semaphore(name=name)

    def const(self, name, rows=128):
        o, w = CONST[name]
        return self.c[:rows, o:o + w]


def load_state(k):
    nc = k.nc
    state_in = k.sem("state_in")
    with nc.Block() as block:
        @block.sync
        def _(sp):
            sp.dma_start(k.X[:], k.arr["xT"]).then_inc(state_in, 16)
            sp.dma_start(k.c[:], k.arr["consts"]).then_inc(state_in, 16)
            sp.wait_ge(state_in, 32)


def store_state(k):
    nc = k.nc
    state_out = k.sem("state_out")
    with nc.Block() as block:
        @block.sync
        def _(sp):
            sp.dma_start(k.out, k.X[:]).then_inc(state_out, 16)
            sp.wait_ge(state_out, 16)


def layer_norm(k, src, dst, affine=None):
    nc, ph = k.nc, ExitStack()
    s, b = k.ln_sems, NCH * k.ln_calls
    per = 3 if affine else 2
    steps_base = k.ln_calls * 16
    k.ln_calls += 1
    with ph:
        sq = k.sb(f"ln_sq{b}", [128, CH], ctx=ph)
        std = k.sb(f"ln_std{b}", [128, CH], ctx=ph)
        block = ph.enter_context(nc.Block())
        mean_ps, var_ps = k.ps[0], k.ps[1]

        @block.tensor
        def _(pe):
            with pe.Fori(0, NCH) as c:
                nc.tensor.matmul(mean_ps[:], k.const("mean"), src[:, ds(c * CH, CH)], start=True,
                                 stop=True).then_inc(s["mean"], 1)
                pe.wait_ge(s["square"], c + (b + 1))
                nc.tensor.matmul(var_ps[:], k.const("mean"), sq[:], start=True,
                                 stop=True).then_inc(s["var"], 1)

        @block.scalar
        def _(act):
            with act.Fori(0, NCH) as c:
                act.wait_ge(s["centred"], c + (b + 1))
                nc.scalar.activation(sq[:], dst[:, ds(c * CH, CH)], ACT.Square).then_inc(s["square"], 1)
                act.wait_ge(s["var"], c + (b + 1))
                nc.scalar.activation(std[:], var_ps[:], ACT.Sqrt, bias=k.const("eps")).then_inc(s["std"], 1)

        @block.vector
        def _(dve):
            with dve.Fori(0, NCH) as c:
                step = Steps(dve, s["steps"], c, 4, steps_base)
                d = dst[:, ds(c * CH, CH)]
                dve.wait_ge(s["mean"], c + (b + 1))
                nc.vector.tensor_tensor(d, src[:, ds(c * CH, CH)], mean_ps[:],
                                        ALU.subtract).then_inc(s["centred"], 1)
                dve.wait_ge(s["std"], c + (b + 1))
                step(nc.vector.reciprocal(std[:], std[:]))
                step(nc.vector.tensor_tensor(d, d, std[:], ALU.mult))
                if affine is None:
                    dve.sem_inc(s["steps"], 2)
                    step.n += 2
                else:
                    step(nc.vector.tensor_scalar(d, d, affine[0], affine[1], ALU.mult, ALU.add))
                    dve.sem_inc(s["steps"], 1)
                    step.n += 1
                step.end()


def l0_xattn(k):
    nc, ph = k.nc, ExitStack()
    s = {n: k.sem("l0x_" + n) for n in ("w", "q_mm", "q", "kp_mm", "kp", "v_mm", "v", "sc_mm", "sc0", "sc",
                                        "o_mm", "o")}
    ctx_in = [k.sem(f"l0x_ctx{j}") for j in range(4)]
    with ph:
        wq, wk, wv = (k.sb("l0x_" + n, [128, D], ctx=ph) for n in ("wq", "wk", "wv"))
        bcol = k.sb("l0x_bcol", [128, 2], ctx=ph)
        bvrow = k.sb("l0x_bvrow", [1, D], ctx=ph)
        real = k.sb("l0x_real", [1, NKC, KC], ctx=ph)
        mask = k.sb("l0x_mask", [KC, NKC, T], ctx=ph)
        q = k.sb("l0x_q", [128, N], ctx=ph)
        ctxT = k.sb("l0x_ctxT", [128, 4, SP2], ctx=ph)
        kp = k.sb("l0x_kp", [128, 4, SP2], ctx=ph)
        v = k.sb("l0x_v", [KC, 4, NKC, D], ctx=ph)
        sc = k.sb("l0x_sc", [KC, 4, NKC, T], ctx=ph)
        qb = k.sb("l0x_qb", [128, 4 * T], ctx=ph)
        kp_ps, v_ps, sc_ps, o_ps = k.ps[0:2], k.ps[2:4], k.ps[4:6], k.ps[6:8]
        block = ph.enter_context(nc.Block())

        @block.sync
        def _(sp):
            for dst, name in ((wq[:], "L0_xattn_kernel_q"), (wk[:], "L0_xattn_kernel_k"), (wv[:], "L0_xattn_kernel_v"),
                              (bcol[:], "l0x_bcol"), (bvrow[:], "L0_xattn_bias_v"), (real[:], "real_rows"),
                              (mask[:], "l0x_mask")):
                sp.dma_start(dst, k.arr[name]).then_inc(s["w"], 16)
            for j in range(4):
                sp.dma_start(ctxT[:, j, :], k.arr["ctxT"][:, j * SP2:(j + 1) * SP2]).then_inc(ctx_in[j], 16)
            with sp.Fori(1, B // 4) as i:
                for j in range(4):
                    sp.wait_ge(s["v_mm"], i * 4 + (j - 3))
                    sp.dma_start(ctxT[:, j, :], k.arr["ctxT"][:, ds(i * (4 * SP2) + j * SP2, SP2)]
                                 ).then_inc(ctx_in[j], 16)

        @block.tensor
        def _(pe):
            pe.wait_ge(s["w"], 7 * 16)
            for c in range(NCH):
                if c >= 2:
                    pe.wait_ge(s["q"], c - 1)
                nc.tensor.matmul(kp_ps[c % 2][:], wq[:], k.XN[:, c * CH:(c + 1) * CH], start=True,
                                 stop=True).then_inc(s["q_mm"], 1)
            pe.wait_ge(s["q"], NCH)
            with pe.Fori(0, B // 4) as i:
                for j in range(4):
                    pe.wait_ge(ctx_in[j], i * 16 + 16)
                    pe.wait_ge(s["kp"], i * 4 + (j + 1))
                    nc.tensor.matmul(kp_ps[j % 2][:, :SP2], wk[:], ctxT[:, j, :], start=True,
                                     stop=True).then_inc(s["kp_mm"], 1)
                    pe.wait_ge(s["v"], i * 4 + (j + 1))
                    for c in range(NKC):
                        o = v_ps[j % 2][:KC, c * D:(c + 1) * D]
                        nc.tensor.matmul(o, ctxT[:, j, c * KC:(c + 1) * KC], wv[:], start=True, stop=False)
                        mm = nc.tensor.matmul(o, real[:, c, :], bvrow[:], start=False, stop=True)
                    mm.then_inc(s["v_mm"], 1)
                for j in range(4):
                    pe.wait_ge(s["kp"], i * 4 + (j + 3))
                    if j == 0:
                        pe.wait_ge(s["q"], i + (NCH + 1))
                    pe.wait_ge(s["sc"], i * 4 + (j + 1))
                    for c in range(NKC):
                        mm = nc.tensor.matmul(sc_ps[j % 2][:KC, c * T:(c + 1) * T], kp[:, j, c * KC:(c + 1) * KC],
                                              qb[:, j * T:(j + 1) * T], start=True, stop=True)
                    mm.then_inc(s["sc_mm"], 1)
                for j in range(4):
                    pe.wait_ge(s["v"], i * 4 + (j + 3))
                    pe.wait_ge(s["sc"], i * 4 + (j + 3))
                    if j == 0:
                        pe.wait_ge(s["o"], i + 1)
                    for c in range(NKC):
                        mm = nc.tensor.matmul(o_ps[0][:, j * T:(j + 1) * T], v[:, j, c, :], sc[:, j, c, :],
                                              start=(c == 0), stop=(c == NKC - 1))
                mm.then_inc(s["o_mm"], 1)

        @block.scalar
        def _(act):
            act.wait_ge(s["w"], 7 * 16)
            for c in range(NCH):
                act.wait_ge(s["q_mm"], c + 1)
                nc.scalar.activation(q[:, c * CH:(c + 1) * CH], kp_ps[c % 2][:], ACT.Relu,
                                     bias=bcol[:, 0:1]).then_inc(s["q"], 1)
            act.wait_ge(s["q"], NCH)
            act.sem_inc(s["kp"], 2)
            with act.Fori(0, B // 4) as i:
                act.wait_ge(s["o"], i + 1)
                nc.scalar.copy(qb[:], q[:, ds(i * (4 * T), 4 * T)]).then_inc(s["q"], 1)
                for j in range(4):
                    act.wait_ge(s["kp_mm"], i * 4 + (j + 1))
                    nc.scalar.activation(kp[:, j, :], kp_ps[j % 2][:, :SP2], ACT.Relu,
                                         bias=bcol[:, 1:2]).then_inc(s["kp"], 1)

        @block.vector
        def _(dve):
            dve.wait_ge(s["w"], 7 * 16)
            for n in ("v", "sc"):
                dve.sem_inc(s[n], 2)
            dve.sem_inc(s["o"], 1)
            with dve.Fori(0, B // 4) as i:
                for j in range(4):
                    dve.wait_ge(s["v_mm"], i * 4 + (j + 1))
                    nc.vector.tensor_scalar(v[:, j].rearrange("p c d -> p (c d)"), v_ps[j % 2][:KC, :NKC * D], 0.0, None,
                                            ALU.max).then_inc(s["v"], 1)
                for j in range(4):
                    dve.wait_ge(s["sc_mm"], i * 4 + (j + 1))
                    w = sc[:, j].rearrange("p c d -> p (c d)")
                    nc.vector.tensor_scalar(w, sc_ps[j % 2][:KC, :NKC * T], 0.0, float(1.0 / np.sqrt(np.float32(D))),
                                            ALU.max, ALU.mult).then_inc(s["sc0"], 1)
                    dve.wait_ge(s["sc0"], i * 4 + (j + 1))
                    nc.vector.tensor_tensor(w, w, mask[:].rearrange("p c d -> p (c d)"), ALU.add).then_inc(s["sc"], 1)
                dve.wait_ge(s["o_mm"], i + 1)
                x = k.X[:, ds(i * (4 * T), 4 * T)]
                nc.vector.scalar_tensor_tensor(out=x, in0=o_ps[0][:, :4 * T], scalar=0.0, in1=x, op0=ALU.max,
                                               op1=ALU.add).then_inc(s["o"], 1)


def small_scores(k, nm, w, scores, rotary, keys_from):
    nc, ph = k.nc, ExitStack()
    s = {n: k.sem(nm + n) for n in ("proj_mm", "low_mm", "low", "qk", "spread", "sc_mm", "sc", "kept", "steps")}
    with ph:
        turned = k.sb(nm + "turned", [128, 2, H * T], ctx=ph)
        q, kk = k.sb(nm + "q", [128, CH], ctx=ph), k.sb(nm + "k", [128, CH], ctx=ph)
        tmp = k.sb(nm + "tmp", [128, 2, CH], ctx=ph)
        low = k.sb(nm + "low", [16, 2, CH], ctx=ph)
        spread = k.sb(nm + "spread", [128, 2, TB, H, T], ctx=ph)
        sc_ps = k.ps[4:6]
        block = ph.enter_context(nc.Block())

        @block.tensor
        def _(pe):
            pe.sem_inc(s["sc_mm"], 2)
            with pe.Fori(0, NCH) as c:
                srcs = (k.XN[:, ds(c * CH, CH)], keys_from[:, ds(c * CH, CH)])
                pe.wait_ge(s["qk"], c + 1)
                if rotary:
                    for n, wn in enumerate(("q", "q2", "k", "k2")):
                        mm = nc.tensor.matmul(k.ps[n][:], w[wn], srcs[n // 2], start=True, stop=True)
                    mm.then_inc(s["proj_mm"], 1)
                else:
                    for n, wn in enumerate(("Aq", "Ak")):
                        nc.tensor.matmul(k.ps[2 * n + 1][:16, :], w[wn], srcs[n], start=True,
                                         stop=True).then_inc(s["low_mm"], 1)
                    for n, wn in enumerate(("q", "k")):
                        nc.tensor.matmul(k.ps[2 * n][:], w[wn], srcs[n], start=True, stop=False)
                        pe.wait_ge(s["low"], c * 2 + (n + 1))
                        mm = nc.tensor.matmul(k.ps[2 * n][:], w["B" + wn], low[:, n, :], start=False, stop=True)
                    mm.then_inc(s["proj_mm"], 1)
                pe.wait_ge(s["qk"], c + 2)
                for t in range(4):
                    pe.wait_ge(s["spread"], c * 4 + (t + 1))
                    pe.wait_ge(s["sc"], c * 4 + (t + 1))
                    for b in range(TB):
                        at = (t * TB + b) * T
                        mm = nc.tensor.matmul(sc_ps[t % 2][b * T:(b + 1) * T, :], kk[:, at:at + T],
                                              spread[:, t % 2, b].rearrange("p h q -> p (h q)"), start=True, stop=True)
                    mm.then_inc(s["sc_mm"], 1)

        @block.scalar
        def _(act):
            act.sem_inc(s["kept"], 2)
            with act.Fori(0, NCH) as c:
                if not rotary:
                    for n in range(2):
                        act.wait_ge(s["low_mm"], c * 2 + (n + 1))
                        nc.scalar.mul(low[:, n, :], k.ps[2 * n + 1][:16, :], 1.0 / 16).then_inc(s["low"], 1)
                for t in range(4):
                    act.wait_ge(s["sc"], c * 4 + (t + 3))
                    nc.scalar.copy(scores[:, ds(c * 4 + t, 1)].rearrange("p o h s -> p (o h s)"),
                                   turned[:, t % 2, :]).then_inc(s["kept"], 1)

        @block.gpsimd
        def _(pool):
            with pool.Fori(0, NCH) as c:
                pool.wait_ge(s["qk"], c + 2)
                for t in range(4):
                    pool.wait_ge(s["sc_mm"], c * 4 + (t + 1))
                    for b in range(TB):
                        at = (t * TB + b) * T
                        ins = nc.gpsimd.tensor_tensor(
                            spread[:, t % 2, b], q[:, at:at + T].unsqueeze(1).to_broadcast([128, H, T]),
                            k.const("hmask").unsqueeze(2).to_broadcast([128, H, T]), ALU.mult)
                    ins.then_inc(s["spread"], 1)

        @block.vector
        def _(dve):
            dve.sem_inc(s["qk"], 1)
            dve.sem_inc(s["sc"], 2)
            cos, sin = (k.const(n).unsqueeze(1).to_broadcast([128, CH // T, T]) for n in ("cos", "sin"))
            v3 = lambda a: a.rearrange("p (b t) -> p b t", t=T)
            with dve.Fori(0, NCH) as c:
                step = Steps(dve, s["steps"], c, 5 if rotary else 1)
                dve.wait_ge(s["proj_mm"], c + 1)
                if rotary:
                    for n, dst in enumerate((q, kk)):
                        step(nc.vector.tensor_tensor(v3(dst[:]), v3(k.ps[2 * n][:]), cos, ALU.mult))
                        step(nc.vector.tensor_tensor(v3(tmp[:, n]), v3(k.ps[2 * n + 1][:]), sin, ALU.mult))
                        ins = nc.vector.tensor_tensor(dst[:], dst[:], tmp[:, n], ALU.add)
                        if n == 0:
                            step(ins)
                    ins.then_inc(s["qk"], 1)
                else:
                    step(nc.vector.tensor_scalar(q[:], k.ps[0][:], w["bq"], None, ALU.add))
                    nc.vector.tensor_scalar(kk[:], k.ps[2][:], w["bk"], None, ALU.add).then_inc(s["qk"], 1)
                step.end()
                for t in range(4):
                    dve.wait_ge(s["sc_mm"], c * 4 + (t + 3))
                    dve.wait_ge(s["kept"], c * 4 + (t + 1))
                    nc.vector.transpose(turned[:, t % 2, :], sc_ps[t % 2][:]).then_inc(s["sc"], 1)


def small_values(k, nm, w, attT, values_from, lora):
    nc, ph = k.nc, ExitStack()
    s = {n: k.sem(nm + n) for n in ("stage", "v_mm", "v", "low_mm", "low", "u_mm", "own", "o", "low2_mm", "low2",
                                    "out_mm", "x")}
    with ph:
        src = k.sb(nm + "src", [128, CH], ctx=ph)
        at = k.sb(nm + "at", [128, 4, H * T], ctx=ph)
        v = k.sb(nm + "v", [128, 4, D], ctx=ph)
        own = k.sb(nm + "own", [128, 2, H, T], ctx=ph)
        o = k.sb(nm + "o", [128, CH], ctx=ph)
        low = k.sb(nm + "vlow", [16, 2, CH], ctx=ph)
        v_ps, u_ps, low_ps, out_ps = k.ps[4], k.ps[0:4], k.ps[5], k.ps[6]
        block = ph.enter_context(nc.Block())

        @block.scalar
        def _(act):
            act.sem_inc(s["low2"], 1)
            with act.Fori(0, NCH) as c:
                act.wait_ge(s["x"], c + 1)
                nc.scalar.copy(src[:], values_from[:, ds(c * CH, CH)]).then_inc(s["stage"], 1)
                nc.scalar.copy(at[:].rearrange("p t c -> p (t c)"),
                               attT[:, ds(c * 4, 4)].rearrange("p t h q -> p (t h q)")).then_inc(s["stage"], 1)
                if lora:
                    act.wait_ge(s["low_mm"], c + 1)
                    nc.scalar.mul(low[:, 0, :], low_ps[:16, :], 1.0 / 16).then_inc(s["low"], 1)
                act.wait_ge(s["v_mm"], c + 1)
                nc.scalar.copy(v[:].rearrange("p t d -> p (t d)"), v_ps[:]).then_inc(s["v"], 1)
                if lora:
                    act.wait_ge(s["low2_mm"], c + 1)
                    nc.scalar.mul(low[:, 1, :], low_ps[:16, :], 1.0 / 16).then_inc(s["low2"], 1)

        @block.tensor
        def _(pe):
            with pe.Fori(0, NCH) as c:
                pe.wait_ge(s["stage"], c * 2 + 2)
                if lora:
                    nc.tensor.matmul(low_ps[:16, :], w["Ak"], src[:], start=True, stop=True).then_inc(s["low_mm"], 1)
                    pe.wait_ge(s["low"], c + 1)
                for t in range(4):
                    tile = src[:, t * 128:(t + 1) * 128]
                    o_ap = v_ps[:, t * D:(t + 1) * D]
                    mm = nc.tensor.matmul(o_ap, tile, w["v"], start=True, stop=not lora)
                    if lora:
                        nc.tensor.matmul(o_ap, low[:, 0, t * 128:(t + 1) * 128], w["Bv"], start=False, stop=False)
                        mm = nc.tensor.matmul(o_ap, k.const("ones", 1), w["bv"], start=False, stop=True)
                mm.then_inc(s["v_mm"], 1)
                pe.wait_ge(s["v"], c + 1)
                for n in range(16):
                    t, b = n // TB, n % TB
                    pe.wait_ge(s["own"], c * 16 + (n + 1))
                    nc.tensor.matmul(u_ps[b][:], v[b * T:(b + 1) * T, t, :], at[b * T:(b + 1) * T, t, :],
                                     start=True, stop=True).then_inc(s["u_mm"], 1)
                pe.wait_ge(s["o"], c * 16 + 16)
                if lora:
                    nc.tensor.matmul(low_ps[:16, :], w["Ap"], o[:], start=True, stop=True).then_inc(s["low2_mm"], 1)
                mm = nc.tensor.matmul(out_ps[:], w["p"], o[:], start=True, stop=not lora)
                if lora:
                    pe.wait_ge(s["low2"], c + 2)
                    mm = nc.tensor.matmul(out_ps[:], w["Bp"], low[:, 1, :], start=False, stop=True)
                mm.then_inc(s["out_mm"], 1)

        @block.vector
        def _(dve):
            dve.sem_inc(s["own"], 4)
            dve.sem_inc(s["x"], 1)
            with dve.Fori(0, NCH) as c:
                for n in range(16):
                    dve.wait_ge(s["u_mm"], c * 16 + (n + 1))
                    nc.vector.tensor_tensor(own[:, n % 2], u_ps[n % 4][:].rearrange("p (h q) -> p h q", h=H),
                                            k.const("hmask").unsqueeze(2).to_broadcast([128, H, T]),
                                            ALU.mult).then_inc(s["own"], 1)
                    dve.wait_ge(s["own"], c * 16 + (n + 5))
                    nc.vector.tensor_reduce(o[:, n * T:(n + 1) * T], own[:, n % 2].rearrange("p h q -> p q h"), AX.X,
                                            ALU.add).then_inc(s["o"], 1)
                dve.wait_ge(s["out_mm"], c + 1)
                x = k.X[:, ds(c * CH, CH)]
                if lora:
                    nc.vector.scalar_tensor_tensor(out=x, in0=out_ps[:], scalar=w["bp"], in1=x, op0=ALU.add,
                                                   op1=ALU.add).then_inc(s["x"], 1)
                else:
                    nc.vector.tensor_tensor(x, out_ps[:], x, ALU.add).then_inc(s["x"], 1)


def load(k, nm, pairs):
    sem = k.sem(nm + "w")
    with k.nc.Block() as block:
        @block.sync
        def _(sp):
            for dst, name in pairs:
                sp.dma_start(dst, k.arr[name]).then_inc(sem, 16)
            sp.wait_ge(sem, 16 * len(pairs))


def l0_attn(k):
    nc, ph = k.nc, ExitStack()
    s = {n: k.sem("l0a_" + n) for n in ("bias_mm", "shifted", "exp", "att", "turned", "kept", "steps")}
    with ph:
        wall = k.sb("l0a_w", [128, 5, D], ctx=ph)
        wproj = k.sb("l0a_wp", [128, D], ctx=ph)
        cw = k.sb("l0a_cw", [128, H], ctx=ph)
        scores = k.sb("l0a_scores", [128, N // 128, H, T], ctx=ph)
        attT = k.sb("l0a_attT", [128, N // 128, H, T], ctx=ph)
        load(k, "l0a_", ((wall[:], "l0a_w"), (wproj[:], "L0_attn_Wproj"), (cw[:], "l0a_cw")))
        w = {n: wall[:, j, :] for j, n in enumerate(("q", "q2", "k", "k2", "v"))}
        w["p"] = wproj[:]
        small_scores(k, "l0as_", w, scores, True, k.XN)
        with ExitStack() as st:
            NT = N // 128
            a, att = k.sb("l0a_a", [128, NT, T], ctx=st), k.sb("l0a_att", [128, NT, T], ctx=st)
            turned = k.sb("l0a_turned", [128, NT, T], ctx=st)
            mx, rs = k.sb("l0a_mx", [128, NT], ctx=st), k.sb("l0a_rs", [128, NT], ctx=st)
            bc = lambda m: m[:].unsqueeze(2).to_broadcast([128, NT, T])
            bias_ps = k.ps[0][:].rearrange("p (n s) -> p n s", s=T)
            block = st.enter_context(nc.Block())

            @block.tensor
            def _(pe):
                with pe.Fori(0, H) as h:
                    pe.wait_ge(s["att"], h + 1)
                    nc.tensor.matmul(k.ps[0][:], k.const("meanT"), att[:].rearrange("p n s -> p (n s)"), start=True,
                                     stop=True).then_inc(s["bias_mm"], 1)

            @block.scalar
            def _(act):
                with act.Fori(0, H) as h:
                    act.wait_ge(s["shifted"], h + 1)
                    nc.scalar.activation(a[:], a[:], ACT.Exp).then_inc(s["exp"], 1)

            @block.gpsimd
            def _(pool):
                pool.sem_inc(s["kept"], 1)
                with pool.Fori(0, H) as h:
                    pool.wait_ge(s["turned"], h + 1)
                    nc.gpsimd.tensor_copy(attT[:, :, ds(h, 1), :].rearrange("p n o s -> p n (o s)"),
                                          turned[:]).then_inc(s["kept"], 1)

            @block.vector
            def _(dve):
                nc.vector.memset(att[:], 0.0).then_inc(s["att"], 1)
                with dve.Fori(0, H) as h:
                    step = Steps(dve, s["steps"], h, 5)
                    dve.wait_ge(s["bias_mm"], h + 1)
                    step(nc.vector.scalar_tensor_tensor(
                        out=a[:], in0=bias_ps, scalar=cw[:, ds(h, 1)],
                        in1=k.const("causal").unsqueeze(1).to_broadcast([128, NT, T]), op0=ALU.mult, op1=ALU.add))
                    step(nc.vector.scalar_tensor_tensor(
                        out=a[:], in0=scores[:, :, ds(h, 1), :].rearrange("p n o s -> p n (o s)"),
                        scalar=float((D // H) ** -0.5), in1=a[:], op0=ALU.mult, op1=ALU.add))
                    step(nc.vector.tensor_reduce(mx[:], a[:], AX.X, ALU.max))
                    nc.vector.tensor_tensor(a[:], a[:], bc(mx), ALU.subtract).then_inc(s["shifted"], 1)
                    dve.wait_ge(s["exp"], h + 1)
                    step(nc.vector.tensor_reduce(rs[:], a[:], AX.X, ALU.add))
                    step(nc.vector.reciprocal(rs[:], rs[:]))
                    nc.vector.tensor_tensor(att[:], a[:], bc(rs), ALU.mult).then_inc(s["att"], 1)
                    dve.wait_ge(s["att"], h + 2)
                    dve.wait_ge(s["kept"], h + 1)
                    nc.vector.transpose(turned[:], att[:]).then_inc(s["turned"], 1)
                    step.end()
        small_values(k, "l0av_", w, attT, k.XN, False)


def l3_xattn(k):
    nc, ph = k.nc, ExitStack()
    s = {n: k.sem("l3x_" + n) for n in ("shifted", "exp", "att", "turned", "kept", "steps")}
    with ph:
        wall = k.sb("l3x_w", [128, 4, D], ctx=ph)
        wa = k.sb("l3x_A", [128, 3, 16], ctx=ph)
        wb = k.sb("l3x_B", [16, 4, D], ctx=ph)
        bcol = k.sb("l3x_bcol", [128, 3], ctx=ph)
        bv = k.sb("l3x_bv", [1, D], ctx=ph)
        head = k.sb("l3x_ctx", [128, N], ctx=ph)
        scores = k.sb("l3x_scores", [128, N // 128, H, T], ctx=ph)
        attT = k.sb("l3x_attT", [128, N // 128, H, T], ctx=ph)
        load(k, "l3x_", ((wall[:], "l3x_w"), (wa[:], "l3x_A"), (wb[:], "l3x_B"), (bcol[:], "l3x_bcol"),
                         (bv[:], "l3x_bv"), (head[:], "ctx_head")))
        w = {n: wall[:, j, :] for j, n in enumerate(("q", "k", "v", "p"))}
        w.update({n: wa[:, j, :] for j, n in enumerate(("Aq", "Ak", "Ap"))})
        w.update({n: wb[:, j, :] for j, n in enumerate(("Bq", "Bk", "Bv", "Bp"))})
        w.update(bq=bcol[:, 0:1], bk=bcol[:, 1:2], bp=bcol[:, 2:3], bv=bv[:])
        small_scores(k, "l3xs_", w, scores, False, head)
        with ExitStack() as st:
            a, mx, rs = (k.sb("l3x_" + n, z, ctx=st) for n, z in (("a", [128, 2, H, T]), ("mx", [128, 2, H]),
                                                                  ("rs", [128, 2, H])))
            turned = k.sb("l3x_turned", [128, 2, H * T], ctx=st)
            bc = lambda m: m.unsqueeze(2).to_broadcast([128, H, T])
            block = st.enter_context(nc.Block())

            @block.scalar
            def _(act):
                with act.Fori(0, N // 256) as i:
                    for j in range(2):
                        act.wait_ge(s["shifted"], i * 2 + (j + 1))
                        nc.scalar.activation(a[:, j], a[:, j], ACT.Exp).then_inc(s["exp"], 1)

            @block.gpsimd
            def _(pool):
                pool.sem_inc(s["kept"], 2)
                with pool.Fori(0, N // 256) as i:
                    for j in range(2):
                        pool.wait_ge(s["turned"], i * 2 + (j + 1))
                        nc.gpsimd.tensor_copy(attT[:, ds(i * 2 + j, 1)].rearrange("p o h s -> p (o h s)"),
                                              turned[:, j]).then_inc(s["kept"], 1)

            @block.vector
            def _(dve):
                with dve.Fori(0, N // 256) as i:
                    step = Steps(dve, s["steps"], i, 8)
                    for j in range(2):
                        step(nc.vector.scalar_tensor_tensor(
                            out=a[:, j], in0=scores[:, ds(i * 2 + j, 1)].rearrange("p o h s -> p (o h) s"),
                            scalar=float((D // H) ** -0.5),
                            in1=k.const("causal").unsqueeze(1).to_broadcast([128, H, T]), op0=ALU.mult, op1=ALU.add))
                        step(nc.vector.tensor_reduce(mx[:, j], a[:, j], AX.X, ALU.max))
                        nc.vector.tensor_tensor(a[:, j], a[:, j], bc(mx[:, j]), ALU.subtract).then_inc(s["shifted"], 1)
                    for j in range(2):
                        dve.wait_ge(s["exp"], i * 2 + (j + 1))
                        step(nc.vector.tensor_reduce(rs[:, j], a[:, j], AX.X, ALU.add))
                        step(nc.vector.reciprocal(rs[:, j], rs[:, j]))
                        nc.vector.tensor_tensor(a[:, j], a[:, j], bc(rs[:, j]), ALU.mult).then_inc(s["att"], 1)
                        dve.wait_ge(s["att"], i * 2 + (j + 1))
                        dve.wait_ge(s["kept"], i * 2 + (j + 1))
                        nc.vector.transpose(turned[:, j], a[:, j].rearrange("p h s -> p (h s)")).then_inc(s["turned"], 1)
                    step.end()
        small_values(k, "l3xv_", w, attT, head, True)


NT = N // 128


def gate_logits(k, nm, w, e):
    nc, mm = k.nc, k.sem(nm + "logits")
    with nc.Block() as block:
        @block.tensor
        def _(pe):
            for t in range(NT):
                ins = nc.tensor.matmul(k.ps[0][:, t * e:(t + 1) * e], k.XN[:, t * 128:(t + 1) * 128], w, start=True,
                                       stop=True)
            ins.then_inc(mm, 1)
            pe.wait_ge(mm, 1)
    return k.ps[0][:, :NT * e].rearrange("p (t e) -> p t e", e=e)


def rows_of(k, nm, cols, rows, e):
    nc, mm, done = k.nc, k.sem(nm + "turn_mm"), k.sem(nm + "turn")
    with nc.Block() as block:
        @block.tensor
        def _(pe):
            for t in range(NT):
                ins = nc.tensor.transpose(k.ps[1 + t // 4][:e, (t % 4) * 128:(t % 4 + 1) * 128], cols[:, t, :],
                                          k.const("ident"))
                if t % 4 == 3:
                    ins.then_inc(mm, 1)

        @block.scalar
        def _(act):
            for c in range(NCH):
                act.wait_ge(mm, c + 1)
                nc.scalar.copy(rows[:e, c * CH:(c + 1) * CH], k.ps[1 + c][:e, :]).then_inc(done, 1)
            act.wait_ge(done, NCH)


def first_max(nc, step, vals, mx, hot, tmp, iota, e):
    bc = lambda m: m.unsqueeze(2).to_broadcast([128, NT, e])
    step(nc.vector.tensor_reduce(mx, vals, AX.X, ALU.max))
    step(nc.vector.tensor_tensor(tmp, vals, bc(mx), ALU.is_lt))
    step(nc.vector.scalar_tensor_tensor(out=tmp, in0=tmp, scalar=float(2 * e), in1=iota, op0=ALU.mult, op1=ALU.add))
    step(nc.vector.tensor_reduce(mx, tmp, AX.X, ALU.min))
    step(nc.vector.tensor_tensor(hot, iota, bc(mx), ALU.is_equal))


def experts(k, nm, e_range, f4, gated, coefT, src, wname, gain):
    nc, ph = k.nc, ExitStack()
    e0, ne = e_range
    lanes = min(2, ne)
    nw = 2 if gated else 1
    wc = nw * f4 * 128 + f4 * 128 + (0 if gated else f4 + 1 + 2)
    erows = coefT.shape[0]
    nb = 2 if gated else 4
    s = {n: k.sem(nm + n) for n in ("in", "hid_mm", "g", "h", "y_mm", "cf_mm", "cf", "t", "x")}
    w_in = [k.sem(nm + f"w_in{j}") for j in range(lanes)]
    with ph:
        w = k.sb(nm + "w", [128, lanes, wc], ctx=ph)
        sel = k.sb(nm + "sel", [erows, lanes, 128], ctx=ph)
        xe = k.sb(nm + "xe", [128, 2, CH], ctx=ph) if gain else None
        gl = k.sb(nm + "gl", [128, 2, CH], ctx=ph) if gated else None
        h = k.sb(nm + "h", [128, 2, f4, CH], ctx=ph)
        cf = k.sb(nm + "cf", [128, 2, CH], ctx=ph)
        t_sb = k.sb(nm + "t", [128, 2, CH], ctx=ph)
        block = ph.enter_context(nc.Block())
        y_ps, cf_ps = k.ps[4:6], k.ps[6:8]
        o2 = nw * f4 * 128
        ob = o2 + f4 * 128
        order = [("h", 0), ("h", 1), ("y", 0), ("h", 2), ("y", 1), ("h", 3), ("y", 2), ("y", 3)]

        def item(i, l, c):
            return i * (lanes * NCH) + (l * NCH + c)

        @block.sync
        def _(sp):
            def fetch(l, e):
                sp.dma_start(w[:, l, :], k.arr[wname][ds(e, 1)].rearrange("o p c -> (o p) c")).then_inc(w_in[l], 16)
                sp.dma_start(sel[:, l, :], k.arr["sel"][:erows, ds((e + e0) * 128, 128)]).then_inc(w_in[l], 16)
            for l in range(lanes):
                fetch(l, l)
            if ne > lanes:
                with sp.Fori(1, ne // lanes) as i:
                    for l in range(lanes):
                        sp.wait_ge(s["x"], i * (2 * NCH) + (l - 1) * NCH)
                        fetch(l, i * lanes + l)

        @block.tensor
        def _(pe):
            pe.sem_inc(s["hid_mm"], 2 * f4)
            pe.sem_inc(s["y_mm"], 2)
            with pe.Fori(0, ne // lanes) as i:
                for l in range(lanes):
                    pe.wait_ge(w_in[l], i * 32 + 32)
                    for what, c in order:
                        m = item(i, l, c)
                        if what == "h":
                            if gain:
                                pe.wait_ge(s["in"], m + 1)
                            rhs = xe[:, c % 2, :] if gain else src[:, c * CH:(c + 1) * CH]
                            for f in range(f4):
                                pe.wait_ge(s["h"], m * f4 + (f + 1))
                                for n in range(nw):
                                    bank = k.ps[((c * f4 + f) % nb) * nw + n]
                                    mm = nc.tensor.matmul(bank[:], w[:, l, (n * f4 + f) * 128:(n * f4 + f + 1) * 128],
                                                          rhs, start=True, stop=True)
                                mm.then_inc(s["hid_mm"], 1)
                        else:
                            pe.wait_ge(s["cf"], m + 1)
                            nc.tensor.matmul(cf_ps[c % 2][:], sel[:, l, :], coefT[:, c * CH:(c + 1) * CH], start=True,
                                             stop=True).then_inc(s["cf_mm"], 1)
                            pe.wait_ge(s["h"], m * f4 + (f4 + nb))
                            pe.wait_ge(s["t"], m + 1)
                            for f in range(f4):
                                mm = nc.tensor.matmul(y_ps[c % 2][:], w[:, l, o2 + f * 128:o2 + (f + 1) * 128],
                                                      h[:, c % 2, f, :], start=(f == 0), stop=(f == f4 - 1))
                            mm.then_inc(s["y_mm"], 1)

        @block.scalar
        def _(act):
            act.sem_inc(s["cf"], 2)
            if not gated:
                act.sem_inc(s["h"], nb)
            with act.Fori(0, ne // lanes) as i:
                for l in range(lanes):
                    if not gated:
                        act.wait_ge(w_in[l], i * 32 + 32)
                    for what, c in order:
                        m = item(i, l, c)
                        if what == "h":
                            for f in range(f4):
                                act.wait_ge(s["hid_mm"], m * f4 + (f + 1 + 2 * f4))
                                if gated:
                                    act.wait_ge(s["h"], m * f4 + (f + 1))
                                    nc.scalar.activation(gl[:, (c * f4 + f) % 2, :], k.ps[((c * f4 + f) % nb) * 2][:],
                                                         ACT.Gelu).then_inc(s["g"], 1)
                                else:
                                    if f == 0:
                                        act.wait_ge(s["y_mm"], m + 1)
                                    nc.scalar.activation(h[:, c % 2, f, :], k.ps[(c * f4 + f) % nb][:], ACT.Relu,
                                                         bias=w[:, l, ob + f:ob + f + 1]).then_inc(s["h"], 1)
                        else:
                            act.wait_ge(s["cf_mm"], m + 1)
                            act.wait_ge(s["t"], m + 1)
                            nc.scalar.copy(cf[:, c % 2, :], cf_ps[c % 2][:]).then_inc(s["cf"], 1)

        @block.vector
        def _(dve):
            dve.sem_inc(s["t"], 2)
            if gated:
                dve.sem_inc(s["h"], nb)
            with dve.Fori(0, ne // lanes) as i:
                for l in range(lanes):
                    if not gated:
                        dve.wait_ge(w_in[l], i * 32 + 32)
                    for what, c in order:
                        m = item(i, l, c)
                        if what == "h":
                            if gain:
                                dve.wait_ge(s["hid_mm"], m * f4 + f4)
                                nc.vector.tensor_scalar(xe[:, c % 2, :], src[:, c * CH:(c + 1) * CH],
                                                        w[:, l, ob + f4 + 1:ob + f4 + 2], w[:, l, ob + f4 + 2:ob + f4 + 3],
                                                        ALU.mult, ALU.add).then_inc(s["in"], 1)
                            if gated:
                                dve.wait_ge(s["y_mm"], m + 1)
                                for f in range(f4):
                                    dve.wait_ge(s["g"], m * f4 + (f + 1))
                                    nc.vector.tensor_tensor(h[:, c % 2, f, :], gl[:, (c * f4 + f) % 2, :],
                                                            k.ps[((c * f4 + f) % nb) * 2 + 1][:],
                                                            ALU.mult).then_inc(s["h"], 1)
                        else:
                            dve.wait_ge(s["y_mm"], m + 3)
                            dve.wait_ge(s["cf"], m + 3)
                            if gated:
                                nc.vector.tensor_tensor(t_sb[:, c % 2, :], y_ps[c % 2][:], cf[:, c % 2, :],
                                                        ALU.mult).then_inc(s["t"], 1)
                            else:
                                nc.vector.scalar_tensor_tensor(
                                    out=t_sb[:, c % 2, :], in0=y_ps[c % 2][:], scalar=w[:, l, ob + f4:ob + f4 + 1],
                                    in1=cf[:, c % 2, :], op0=ALU.add, op1=ALU.mult).then_inc(s["t"], 1)
                            dve.wait_ge(s["t"], m + 3)
                            x = k.X[:, c * CH:(c + 1) * CH]
                            nc.vector.tensor_tensor(x, x, t_sb[:, c % 2, :], ALU.add).then_inc(s["x"], 1)


def add_normed(k, nm):
    nc, done = k.nc, k.sem(nm + "residual")
    with nc.Block() as block:
        @block.vector
        def _(dve):
            nc.vector.tensor_tensor(k.X[:], k.X[:], k.XN[:], ALU.add).then_inc(done, 1)
            dve.wait_ge(done, 1)


def l0_ffn(k):
    nc, ph, e = k.nc, ExitStack(), 8
    s = {n: k.sem("l0f_" + n) for n in ("sig", "steps")}
    with ph:
        xn2 = k.sb("l0f_xn2", [128, N], ctx=ph)
        cen = k.sb("l0f_cen", [128, e], ctx=ph)
        coefT = k.sb("l0f_coefT", [e, N], ctx=ph)
        layer_norm(k, k.XN, xn2)
        load(k, "l0f_", ((cen[:], "l0f_cen"),))
        logits = gate_logits(k, "l0f_", cen[:], e)
        with ExitStack() as st:
            sig, hot, tmp, aff = (k.sb("l0f_" + n, [128, NT, e], ctx=st) for n in ("sig", "hot", "tmp", "aff"))
            mx = k.sb("l0f_mx", [128, NT], ctx=st)
            iota = k.const("iota")[:, :e].unsqueeze(1).to_broadcast([128, NT, e])
            with nc.Block() as block:
                @block.scalar
                def _(act):
                    act.wait_ge(s["steps"], 1)
                    nc.scalar.activation(sig[:], aff[:], ACT.Sigmoid).then_inc(s["sig"], 1)

                @block.vector
                def _(dve):
                    step = Steps(dve, s["steps"])
                    step(nc.vector.tensor_copy(aff[:], logits))
                    first_max(nc, step, aff[:], mx[:], hot[:], tmp[:], iota, e)
                    dve.wait_ge(s["sig"], 1)
                    step(nc.vector.tensor_tensor(hot[:], hot[:], sig[:], ALU.mult))
            rows_of(k, "l0f_", hot, coefT, e)
        experts(k, "l0fe_", (0, e), 4, False, coefT, xn2, "l0f_w", True)
        add_normed(k, "l0f_")


def softmax_rows(k, nm, logits, bias, p, mx, e):
    nc = k.nc
    s = {n: k.sem(nm + n) for n in ("sm_in", "sm_exp", "sm_steps")}
    bc = lambda m: m.unsqueeze(2).to_broadcast([128, NT, e])
    with nc.Block() as block:
        @block.vector
        def _(dve):
            step = Steps(dve, s["sm_steps"])
            if bias is None:
                step(nc.vector.tensor_copy(p, logits))
            else:
                step(nc.vector.tensor_tensor(p, logits, bias.unsqueeze(1).to_broadcast([128, NT, e]), ALU.add))
            step(nc.vector.tensor_reduce(mx, p, AX.X, ALU.max))
            nc.vector.tensor_tensor(p, p, bc(mx), ALU.subtract).then_inc(s["sm_in"], 1)
            dve.wait_ge(s["sm_exp"], 1)
            step(nc.vector.tensor_reduce(mx, p, AX.X, ALU.add))
            step(nc.vector.reciprocal(mx, mx))
            step(nc.vector.tensor_tensor(p, p, bc(mx), ALU.mult))

        @block.scalar
        def _(act):
            act.wait_ge(s["sm_in"], 1)
            nc.scalar.activation(p, p, ACT.Exp).then_inc(s["sm_exp"], 1)


def l2_ffn(k):
    nc, ph, e, cap = k.nc, ExitStack(), 16, N * 2 // 16
    s = {n: k.sem("l2f_" + n) for n in ("ones", "loop", "steps")}
    with ph:
        gw = k.sb("l2f_gw", [128, e], ctx=ph)
        coefT = k.sb("l2f_coefT", [e + 1, N], ctx=ph)
        bits = k.sb("l2f_bits", [e, 32], I32, ctx=ph)
        load(k, "l2f_", ((gw[:], "l2f_gw"), (bits[:], "bits_i")))
        logits = gate_logits(k, "l2f_", gw[:], e)
        with ExitStack() as st:
            p, mx = k.sb("l2f_p", [128, NT, e + 1], ctx=st), k.sb("l2f_mx", [128, NT], ctx=st)
            with nc.Block() as block:
                @block.vector
                def _(dve):
                    nc.vector.memset(p[:], 1.0).then_inc(s["ones"], 1)
                    dve.wait_ge(s["ones"], 1)
            softmax_rows(k, "l2f_", logits, None, p[:, :, :e], mx[:], e)
            rows_of(k, "l2f_", p, coefT, e + 1)
        with ExitStack() as st:
            sc = coefT[:e, :]
            junk, eq, cum, ones = (k.sb("l2f_" + n, [e, N], ctx=st) for n in ("junk", "eq", "cum", "ones"))
            thr, cand, bit = (k.sb("l2f_" + n, [e, 1], I32, ctx=st) for n in ("thr", "cand", "bit"))
            cnt, need = (k.sb("l2f_" + n, [e, 1], ctx=st) for n in ("cnt", "need"))
            bitf = k.const("bits", e)
            with nc.Block() as block:
                @block.vector
                def _(dve):
                    step = Steps(dve, s["steps"])
                    step(nc.vector.memset(thr[:], 0))
                    step(nc.vector.memset(ones[:], 1.0))
                    with dve.Fori(0, 31) as r:
                        turn = Steps(dve, s["loop"], r, 4)
                        b = r * -1 + 30
                        turn(nc.vector.tensor_tensor(cand[:], thr[:], bits[:, ds(b, 1)], ALU.bitwise_or))
                        turn(nc.vector.tensor_scalar(junk[:], sc, cand[:].bitcast(F32), 0.0, ALU.is_ge, ALU.add,
                                                     accum_out=cnt[:]))
                        turn(nc.vector.tensor_scalar(bit[:], cnt[:], cap - 0.5, bitf[:, ds(b, 1)], ALU.is_ge, ALU.mult))
                        turn(nc.vector.tensor_tensor(thr[:], thr[:], bit[:], ALU.bitwise_or))
                        turn.end()
                    t = thr[:].bitcast(F32)
                    step(nc.vector.tensor_scalar(junk[:], sc, t, 0.0, ALU.is_gt, ALU.add, accum_out=cnt[:]))
                    step(nc.vector.tensor_scalar(need[:], cnt[:], -1.0, float(cap), ALU.mult, ALU.add))
                    step(nc.vector.tensor_scalar(eq[:], sc, t, None, ALU.is_equal))
                    step(nc.vector.tensor_tensor_scan(cum[:], ones[:], eq[:], 0.0, ALU.mult, ALU.add))
                    step(nc.vector.scalar_tensor_tensor(out=eq[:], in0=cum[:], scalar=need[:], in1=eq[:], op0=ALU.is_le,
                                                        op1=ALU.mult))
                    step(nc.vector.tensor_tensor(junk[:], junk[:], eq[:], ALU.add))
                    step(nc.vector.tensor_tensor(sc, sc, junk[:], ALU.mult))
        experts(k, "l2fe_", (0, e), 4, True, coefT, k.XN, "l2f_w", False)
        experts(k, "l2fs_", (e, 1), 2, True, coefT, k.XN, "l2f_s", False)


def sorted_by_expert(k, coefT, top, e, xs):
    nc, ph = k.nc, ExitStack()
    s = {n: k.sem("l3s_" + n) for n in ("bc_mm", "bc", "steps", "start_mm", "rank", "pos_mm", "tok_mm", "tok", "hot",
                                        "sum_mm", "sum", "end")}
    with ph:
        cum, ones, after = (k.sb("l3s_" + n, [e, N], ctx=ph) for n in ("cum", "ones", "after"))
        start, pos = k.sb("l3s_start", [e, 2], ctx=ph), k.sb("l3s_pos", [128, NT], ctx=ph)
        place = k.sb("l3s_place", [128, N], ctx=ph)
        tri = k.sb("l3s_tri", [e, e], ctx=ph)
        tok = k.sb("l3s_tok", [128, NT, D], ctx=ph)
        hot = k.sb("l3s_hot", [128, 2, N], ctx=ph)
        load(k, "l3s_", ((place[:], "places"), (tri[:], "l3f_tri")))
        with nc.Block() as block:
            @block.tensor
            def _(pe):
                for c in range(NCH):
                    nc.tensor.matmul(k.ps[c][:], top[:], coefT[:, c * CH:(c + 1) * CH], start=True,
                                     stop=True).then_inc(s["bc_mm"], 1)
                for t in range(NT):
                    if t % 4 == 0:
                        pe.wait_ge(s["bc"], t // 4 + 1)
                    ins = nc.tensor.transpose(k.ps[t // 4][:, (t % 4) * 128:(t % 4 + 1) * 128],
                                              xs[:, t * 128:(t + 1) * 128], k.const("ident"))
                    if t % 4 == 3:
                        ins.then_inc(s["tok_mm"], 1)
                pe.wait_ge(s["rank"], 1)
                nc.tensor.matmul(k.ps[4][:e, 0:1], tri[:], cum[:, N - 1:N], start=True,
                                 stop=True).then_inc(s["start_mm"], 1)
                pe.wait_ge(s["rank"], 2)
                for t in range(NT):
                    ins = nc.tensor.matmul(k.ps[5][:, t:t + 1], cum[:, t * 128:(t + 1) * 128], k.const("ones", e)[:, 0:1],
                                           start=True, stop=True)
                ins.then_inc(s["pos_mm"], 1)
                pe.wait_ge(s["tok"], NCH)
                for t in range(NT):
                    pe.wait_ge(s["hot"], t + 1)
                    for c in range(NCH):
                        ins = nc.tensor.matmul(k.ps[c][:], tok[:, t, :], hot[:, t % 2, c * CH:(c + 1) * CH],
                                               start=(t == 0), stop=(t == NT - 1))
                    ins.then_inc(s["sum_mm"], 1)

            @block.scalar
            def _(act):
                for c in range(NCH):
                    act.wait_ge(s["tok_mm"], c + 1)
                    nc.scalar.copy(tok[:, c * 4:(c + 1) * 4, :].rearrange("p t d -> p (t d)"),
                                   k.ps[c][:]).then_inc(s["tok"], 1)
                act.wait_ge(s["sum_mm"], NT)
                for c in range(NCH):
                    nc.scalar.copy(xs[:, c * CH:(c + 1) * CH], k.ps[c][:]).then_inc(s["sum"], 1)
                act.wait_ge(s["sum"], NCH)

            @block.vector
            def _(dve):
                step = Steps(dve, s["steps"])
                for c in range(NCH):
                    dve.wait_ge(s["bc_mm"], c + 1)
                    nc.vector.tensor_tensor(xs[:, c * CH:(c + 1) * CH], k.XN[:, c * CH:(c + 1) * CH], k.ps[c][:],
                                            ALU.mult).then_inc(s["bc"], 1)
                route = coefT[:e, :]
                step(nc.vector.memset(ones[:], 1.0))
                nc.vector.tensor_tensor_scan(cum[:], ones[:], route, 0.0, ALU.mult, ALU.add).then_inc(s["rank"], 1)
                dve.wait_ge(s["start_mm"], 1)
                dve.wait_ge(s["rank"], 1)
                step(nc.vector.tensor_copy(start[:, 0:1], k.ps[4][:e, 0:1]))
                step(nc.vector.tensor_tensor(start[:, 1:2], start[:, 0:1], cum[:, N - 1:N], ALU.add))
                step(nc.vector.tensor_scalar(cum[:], cum[:], start[:, 0:1], -1.0, ALU.add, ALU.add))
                nc.vector.tensor_tensor(cum[:], cum[:], route, ALU.mult).then_inc(s["rank"], 1)
                dve.wait_ge(s["rank"], 2)
                step(nc.vector.tensor_scalar(after[:], place[:e, :], start[:, 0:1], None, ALU.is_ge))
                step(nc.vector.scalar_tensor_tensor(out=route, in0=place[:e, :], scalar=start[:, 1:2], in1=after[:],
                                                    op0=ALU.is_lt, op1=ALU.mult))
                dve.wait_ge(s["pos_mm"], 1)
                step(nc.vector.tensor_copy(pos[:], k.ps[5][:, :NT]))
                for t in range(NT):
                    if t >= 2:
                        dve.wait_ge(s["sum_mm"], t - 1)
                    nc.vector.tensor_scalar(hot[:, t % 2, :], place[:], pos[:, t:t + 1], None,
                                            ALU.is_equal).then_inc(s["hot"], 1)


def l3_ffn(k):
    nc, ph, e = k.nc, ExitStack(), 8
    s = {n: k.sem("l3f_" + n) for n in ("steps",)}
    with ph:
        gw = k.sb("l3f_gw", [128, e], ctx=ph)
        bs = k.sb("l3f_bs", [128, e], ctx=ph)
        coefT = k.sb("l3f_coefT", [e + 1, N], ctx=ph)
        top = k.sb("l3f_top", [e + 1, 128], ctx=ph)
        xs = k.sb("l3f_xs", [128, N], ctx=ph)
        load(k, "l3f_", ((gw[:], "l3f_gw"), (bs[:], "l3f_bs"), (top[:], "l3f_top")))
        logits = gate_logits(k, "l3f_", gw[:], e)
        with ExitStack() as st:
            p, tmp = (k.sb("l3f_" + n, [128, NT, e], ctx=st) for n in ("p", "tmp"))
            mx = k.sb("l3f_mx", [128, NT], ctx=st)
            hot = k.sb("l3f_hot", [128, NT, e + 1], ctx=st)
            iota = k.const("iota")[:, :e].unsqueeze(1).to_broadcast([128, NT, e])
            softmax_rows(k, "l3f_", logits, bs[:], p[:], mx[:], e)
            with nc.Block() as block:
                @block.vector
                def _(dve):
                    step = Steps(dve, s["steps"])
                    step(nc.vector.tensor_reduce(hot[:, :, e:e + 1].rearrange("p t o -> p (t o)"), p[:], AX.X, ALU.max))
                    first_max(nc, step, p[:], mx[:], hot[:, :, :e], tmp[:], iota, e)
            rows_of(k, "l3f_", hot, coefT, e + 1)
        sorted_by_expert(k, coefT, top, e, xs)
        experts(k, "l3fe_", (0, e), 1, False, coefT, xs, "l3f_w", False)


def l1_ffn(k):
    nc, ph = k.nc, ExitStack()
    magic = 1.5 * 2.0 ** 23
    s = {n: k.sem("l1f_" + n) for n in ("wq", "w_mm", "wT", "src", "tok_mm", "steps", "xq", "xqT_mm", "xqT", "out_mm",
                                        "out", "turn_mm", "x")}
    with ph:
        wt = k.sb("l1f_wt", [128, D], ctx=ph)
        bias = k.sb("l1f_bias", [128, 1], ctx=ph)
        wsc, am = k.sb("l1f_wsc", [128, 2], ctx=ph), k.sb("l1f_am", [128, 2, 4], ctx=ph)
        wtmp = k.sb("l1f_wtmp", [128, D], ctx=ph)
        wqb, wqT, identb = (k.sb("l1f_" + n, [128, D], BF16, ctx=ph) for n in ("wqb", "wqT", "identb"))
        src, tmp, y = (k.sb("l1f_" + n, [128, CH], ctx=ph) for n in ("src", "tmp", "y"))
        xq, xqT = (k.sb("l1f_" + n, [128, CH], BF16, ctx=ph) for n in ("xq", "xqT"))
        load(k, "l1f_", ((wt[:], "L1_ffn_weight"), (bias[:], "l1f_bias")))
        t3 = lambda a: a.rearrange("p (t d) -> p t d", d=128)
        bc = lambda m: m.unsqueeze(2).to_broadcast([128, 4, 128])
        xqT_ps = k.ps[1][:].bitcast(BF16)
        block = ph.enter_context(nc.Block())

        def rounded(step, out, v):
            step(nc.vector.tensor_scalar(v, v, magic, None, ALU.add))
            step(nc.vector.tensor_scalar(v, v, magic, None, ALU.subtract))
            return nc.vector.tensor_scalar(out, v, 127.0, -128.0, ALU.min, ALU.max)

        @block.vector
        def _(dve):
            step = Steps(dve, s["wq"])
            step(nc.vector.tensor_copy(identb[:], k.const("ident")))
            step(nc.vector.tensor_reduce(wsc[:, 0:1], wt[:], AX.X, ALU.max, apply_absolute_value=True))
            step(nc.vector.tensor_scalar(wsc[:, 0:1], wsc[:, 0:1], 1e-8, 1.0 / 127.0, ALU.max, ALU.mult))
            step(nc.vector.reciprocal(wsc[:, 1:2], wsc[:, 0:1]))
            step(nc.vector.tensor_scalar(wtmp[:], wt[:], wsc[:, 1:2], None, ALU.mult))
            step(rounded(step, wqb[:], wtmp[:]))
            with dve.Fori(0, NCH) as c:
                step = Steps(dve, s["steps"], c, 7)
                dve.wait_ge(s["tok_mm"], c + 1)
                step(nc.vector.tensor_reduce(am[:, 0, :], t3(k.ps[0][:]), AX.X, ALU.max, apply_absolute_value=True))
                step(nc.vector.tensor_scalar(am[:, 0, :], am[:, 0, :], 1e-8, 1.0 / 127.0, ALU.max, ALU.mult))
                step(nc.vector.reciprocal(am[:, 1, :], am[:, 0, :]))
                step(nc.vector.tensor_tensor(t3(tmp[:]), t3(k.ps[0][:]), bc(am[:, 1, :]), ALU.mult))
                rounded(step, xq[:], tmp[:]).then_inc(s["xq"], 1)
                dve.wait_ge(s["out_mm"], c + 1)
                nc.vector.tensor_tensor(t3(y[:]), t3(k.ps[2][:]), bc(am[:, 0, :]), ALU.mult).then_inc(s["out"], 1)
                dve.wait_ge(s["turn_mm"], c + 1)
                step(nc.vector.tensor_scalar(tmp[:], k.ps[3][:], wsc[:, 0:1], bias[:], ALU.mult, ALU.add))
                x = k.X[:, ds(c * CH, CH)]
                nc.vector.tensor_tensor(x, x, tmp[:], ALU.add).then_inc(s["x"], 1)
                step.end()

        @block.tensor
        def _(pe):
            pe.wait_ge(s["wq"], 8)
            nc.tensor.transpose(xqT_ps[:, :D], wqb[:], identb[:]).then_inc(s["w_mm"], 1)
            with pe.Fori(0, NCH) as c:
                pe.wait_ge(s["src"], c + 1)
                for t in range(4):
                    ins = nc.tensor.transpose(k.ps[0][:, t * 128:(t + 1) * 128], src[:, t * 128:(t + 1) * 128],
                                              k.const("ident"))
                ins.then_inc(s["tok_mm"], 1)
                pe.wait_ge(s["xq"], c + 1)
                pe.wait_ge(s["wT"], 1)
                for t in range(4):
                    ins = nc.tensor.transpose(xqT_ps[:, t * 128:(t + 1) * 128], xq[:, t * 128:(t + 1) * 128], identb[:])
                ins.then_inc(s["xqT_mm"], 1)
                pe.wait_ge(s["xqT"], c + 1)
                for t in range(4):
                    ins = nc.tensor.matmul(k.ps[2][:, t * 128:(t + 1) * 128], xqT[:, t * 128:(t + 1) * 128], wqT[:],
                                           start=True, stop=True)
                ins.then_inc(s["out_mm"], 1)
                pe.wait_ge(s["out"], c + 1)
                for t in range(4):
                    ins = nc.tensor.transpose(k.ps[3][:, t * 128:(t + 1) * 128], y[:, t * 128:(t + 1) * 128],
                                              k.const("ident"))
                ins.then_inc(s["turn_mm"], 1)

        @block.scalar
        def _(act):
            act.wait_ge(s["w_mm"], 1)
            nc.scalar.copy(wqT[:], xqT_ps[:, :D]).then_inc(s["wT"], 1)
            act.sem_inc(s["x"], 1)
            with act.Fori(0, NCH) as c:
                act.wait_ge(s["x"], c + 1)
                nc.scalar.copy(src[:], k.XN[:, ds(c * CH, CH)]).then_inc(s["src"], 1)
                act.wait_ge(s["xqT_mm"], c + 1)
                nc.scalar.copy(xqT[:], xqT_ps[:, :CH]).then_inc(s["xqT"], 1)


def l2_attn(k):
    nc, ph, hp, w2 = k.nc, ExitStack(), H // 2, 1024
    s = {n: k.sem("l2a_" + n) for n in ("src", "v_mm", "v", "p_mm", "neg", "exp", "relu", "phi", "a_mm", "a", "y_mm", "rec",
                                        "y", "o_mm", "x", "steps")}
    with ph:
        wq, wk, wv = (k.sb("l2a_" + n, [128, w2], ctx=ph) for n in ("wq", "wk", "wv"))
        wo = k.sb("l2a_wo", [128, hp, D], ctx=ph)
        bq, bk = k.sb("l2a_bq", [128, hp], ctx=ph), k.sb("l2a_bk", [128, hp], ctx=ph)
        bv, bo = k.sb("l2a_bv", [128, w2], ctx=ph), k.sb("l2a_bo", [128, 1], ctx=ph)
        src = k.sb("l2a_src", [128, CH], ctx=ph)
        v = k.sb("l2a_v", [128, 4, w2], ctx=ph)
        neg, ex, pos, phi = (k.sb("l2a_" + n, [128, 2, 2, CH], ctx=ph) for n in ("neg", "ex", "pos", "phi"))
        a = k.sb("l2a_a", [128, 2, 2, CH], ctx=ph)
        rec, y = k.sb("l2a_rec", [128, CH], ctx=ph), k.sb("l2a_y", [128, 2, CH], ctx=ph)
        load(k, "l2a_", ((wq[:], "l2a_wq"), (wk[:], "l2a_wk"), (wv[:], "l2a_wv"), (wo[:], "l2a_wo"), (bq[:], "l2a_bq"),
                         (bk[:], "l2a_bk"), (bv[:], "l2a_bv"), (bo[:], "l2a_bo")))
        p_ps, a_ps, num_ps, den_ps, o_ps, v_ps = k.ps[0:2], k.ps[2:4], k.ps[4], k.ps[5], k.ps[6], k.ps[7]
        block = ph.enter_context(nc.Block())

        @block.tensor
        def _(pe):
            with pe.Fori(0, NCH) as c:
                pe.wait_ge(s["src"], c + 1)
                for t in range(4):
                    for n in range(2):
                        pe.wait_ge(s["v"], c * 8 + (t * 2 + n + 1))
                        nc.tensor.matmul(v_ps[:], src[:, t * 128:(t + 1) * 128], wv[:, n * 512:(n + 1) * 512], start=True,
                                         stop=True).then_inc(s["v_mm"], 1)
                for n in range(hp + 3):
                    if n < hp:
                        pe.wait_ge(s["relu"], c * 16 + (n * 2 + 2))
                        pe.wait_ge(s["neg"], c * 16 + (n * 2 + 2))
                        nc.tensor.matmul(p_ps[0][:], wq[:, n * 128:(n + 1) * 128], src[:], start=True,
                                         stop=True).then_inc(s["p_mm"], 1)
                        nc.tensor.matmul(p_ps[1][:], wk[:, n * 128:(n + 1) * 128], src[:], start=True,
                                         stop=True).then_inc(s["p_mm"], 1)
                    m = n - 1
                    if 0 <= m < hp:
                        pe.wait_ge(s["phi"], c * 16 + (m * 2 + 2))
                        pe.wait_ge(s["a"], c * 16 + (m * 2 + 2))
                        for h in range(2):
                            r = slice(h * 64, h * 64 + 64)
                            for t in range(4):
                                cols = slice(t * 128, t * 128 + 128)
                                mm = nc.tensor.matmul(a_ps[h][:, cols], phi[r, m % 2, 1, cols], phi[r, m % 2, 0, cols],
                                                      start=True, stop=True)
                        mm.then_inc(s["a_mm"], 1)
                    m = n - 2
                    if 0 <= m < hp:
                        pe.wait_ge(s["a"], c * 16 + (m * 2 + 4))
                        if m == 0:
                            pe.wait_ge(s["v"], c * 8 + 9)
                        pe.wait_ge(s["y"], c * 8 + (m + 1))
                        for h in range(2):
                            r = slice(h * 64, h * 64 + 64)
                            for t in range(4):
                                cols = slice(t * 128, t * 128 + 128)
                                nc.tensor.matmul(num_ps[r, cols], v[:, t, (2 * m + h) * 64:(2 * m + h + 1) * 64],
                                                 a[:, m % 2, h, cols], start=True, stop=True)
                            mm = nc.tensor.matmul(den_ps[r, :], k.const("ones")[:, :64], a[:, m % 2, h, :], start=True,
                                                  stop=True)
                        mm.then_inc(s["y_mm"], 1)
                    m = n - 3
                    if 0 <= m < hp:
                        pe.wait_ge(s["y"], c * 8 + (m + 2))
                        if m == 0:
                            pe.wait_ge(s["x"], c + 1)
                        mm = nc.tensor.matmul(o_ps[:], wo[:, m, :], y[:, m % 2, :], start=(m == 0), stop=(m == hp - 1))
                mm.then_inc(s["o_mm"], 1)

        @block.scalar
        def _(act):
            act.sem_inc(s["relu"], 2)
            with act.Fori(0, NCH) as c:
                act.wait_ge(s["x"], c + 1)
                nc.scalar.copy(src[:], k.XN[:, ds(c * CH, CH)]).then_inc(s["src"], 1)
                for n in range(hp):
                    for j in range(2):
                        m = c * 16 + (n * 2 + j)
                        act.wait_ge(s["neg"], m + 3)
                        act.wait_ge(s["a_mm"], c * 8 + (n + 1))
                        nc.scalar.activation(pos[:, n % 2, j, :], p_ps[j][:], ACT.Relu,
                                             bias=(bq, bk)[j][:, n:n + 1]).then_inc(s["relu"], 1)
                        nc.scalar.activation(ex[:, n % 2, j, :], neg[:, n % 2, j, :], ACT.Exp).then_inc(s["exp"], 1)

        @block.gpsimd
        def _(pool):
            with pool.Fori(0, NCH) as c:
                for n in range(hp):
                    for j in range(2):
                        m = c * 16 + (n * 2 + j)
                        pool.wait_ge(s["exp"], m + 1)
                        pool.wait_ge(s["relu"], m + 3)
                        pool.wait_ge(s["a_mm"], c * 8 + (n + 1))
                        nc.gpsimd.tensor_tensor(phi[:, n % 2, j, :], pos[:, n % 2, j, :], ex[:, n % 2, j, :],
                                                ALU.add).then_inc(s["phi"], 1)

        @block.vector
        def _(dve):
            for n, z in (("v", 1), ("neg", 2), ("a", 2), ("y", 1), ("x", 1), ("a_mm", 2)):
                dve.sem_inc(s[n], z)
            blk = k.const("blk32").unsqueeze(1).to_broadcast([128, 4, 128])
            with dve.Fori(0, NCH) as c:
                step = Steps(dve, s["steps"], c, hp + 1)
                for t in range(4):
                    for n in range(2):
                        dve.wait_ge(s["v_mm"], c * 8 + (t * 2 + n + 1))
                        nc.vector.tensor_tensor(v[:, t, n * 512:(n + 1) * 512], v_ps[:], bv[:, n * 512:(n + 1) * 512],
                                                ALU.add).then_inc(s["v"], 1)
                for n in range(hp + 2):
                    if n < hp:
                        for j in range(2):
                            dve.wait_ge(s["p_mm"], c * 16 + (n * 2 + j + 1))
                            if n >= 2:
                                dve.wait_ge(s["exp"], c * 16 + ((n - 2) * 2 + j + 1))
                            nc.vector.tensor_scalar(neg[:, n % 2, j, :], p_ps[j][:], (bq, bk)[j][:, n:n + 1], 0.0, ALU.add,
                                                    ALU.min).then_inc(s["neg"], 1)
                    m = n - 1
                    if 0 <= m < hp:
                        dve.wait_ge(s["a_mm"], c * 8 + (m + 3))
                        for h in range(2):
                            nc.vector.tensor_tensor(a[:, m % 2, h, :].rearrange("p (t l) -> p t l", t=4),
                                                    a_ps[h][:].rearrange("p (t l) -> p t l", t=4), blk,
                                                    ALU.mult).then_inc(s["a"], 1)
                    m = n - 2
                    if 0 <= m < hp:
                        dve.wait_ge(s["y_mm"], c * 8 + (m + 1))
                        step(nc.vector.tensor_scalar(rec[:], den_ps[:], 1e-6, None, ALU.add))
                        nc.vector.reciprocal(rec[:], rec[:]).then_inc(s["rec"], 1)
                        dve.wait_ge(s["rec"], c * 8 + (m + 1))
                        nc.vector.tensor_tensor(y[:, m % 2, :], num_ps[:], rec[:], ALU.mult).then_inc(s["y"], 1)
                dve.wait_ge(s["o_mm"], c + 1)
                step(nc.vector.tensor_scalar(rec[:], o_ps[:], bo[:], None, ALU.add))
                x = k.X[:, ds(c * CH, CH)]
                nc.vector.tensor_tensor(x, x, rec[:], ALU.add).then_inc(s["x"], 1)
                step.end()


def l3_attn(k):
    nc, ph = k.nc, ExitStack()
    s = {n: k.sem("l3a_" + n) for n in ("src", "p_mm", "neg", "exp", "relu", "phi", "v", "kv_mm", "kv", "y_mm", "rec", "y",
                                        "o_mm", "x", "steps")}
    with ph:
        w = k.sb("l3a_w", [128, 4, D], ctx=ph)
        src = k.sb("l3a_src", [128, CH], ctx=ph)
        neg, pos, phi = (k.sb("l3a_" + n, [128, 2, CH], ctx=ph) for n in ("neg", "pos", "phi"))
        v = k.sb("l3a_v", [128, 4, 2 * D], ctx=ph)
        kv = k.sb("l3a_kv", [128, 4, 2 * D], ctx=ph)
        rec, y = k.sb("l3a_rec", [128, CH], ctx=ph), k.sb("l3a_y", [128, CH], ctx=ph)
        load(k, "l3a_", ((w[:], "l3a_w"),))
        q_ps, k_ps, v_ps, kv_ps, num_ps, den_ps = k.ps[0], k.ps[1], k.ps[2], k.ps[2:6], k.ps[6], k.ps[7]
        o_ps = k.ps[0]
        block = ph.enter_context(nc.Block())

        @block.tensor
        def _(pe):
            with pe.Fori(0, NCH) as c:
                pe.wait_ge(s["src"], c + 1)
                nc.tensor.matmul(q_ps[:], w[:, 0, :], src[:], start=True, stop=True).then_inc(s["p_mm"], 1)
                for n, bank in ((1, k_ps), (2, v_ps)):
                    for t in range(4):
                        mm = nc.tensor.matmul(bank[:, t * D:(t + 1) * D], src[:, t * 128:(t + 1) * 128], w[:, n, :],
                                              start=True, stop=True)
                    mm.then_inc(s["p_mm"], 1)
                pe.wait_ge(s["phi"], c * 2 + 2)
                pe.wait_ge(s["v"], c + 2)

                def out(n):
                    pe.wait_ge(s["kv"], c * 16 + (n + 5))
                    for j, bank in enumerate((num_ps, den_ps)):
                        ins = nc.tensor.matmul(bank[:, n * T:(n + 1) * T], kv[:, n % 4, j * D:(j + 1) * D],
                                               phi[:, 0, n * T:(n + 1) * T], start=True, stop=True)
                    ins.then_inc(s["y_mm"], 1)

                for n in range(16):
                    r = slice((n % 4) * T, (n % 4 + 1) * T)
                    pe.wait_ge(s["kv"], c * 16 + (n + 1))
                    nc.tensor.matmul(kv_ps[n % 4][:, :2 * D], phi[r, 1, (n // 4) * D:(n // 4 + 1) * D], v[r, n // 4, :],
                                     start=True, stop=True).then_inc(s["kv_mm"], 1)
                    if n >= 2:
                        out(n - 2)
                out(14)
                out(15)
                pe.wait_ge(s["y"], c + 1)
                nc.tensor.matmul(o_ps[:], w[:, 3, :], y[:], start=True, stop=True).then_inc(s["o_mm"], 1)

        @block.scalar
        def _(act):
            with act.Fori(0, NCH) as c:
                act.wait_ge(s["x"], c + 1)
                nc.scalar.copy(src[:], k.XN[:, ds(c * CH, CH)]).then_inc(s["src"], 1)
                for j, bank in enumerate((q_ps, k_ps)):
                    act.wait_ge(s["neg"], c * 2 + (j + 1))
                    nc.scalar.activation(pos[:, j, :], bank[:], ACT.Relu).then_inc(s["relu"], 1)
                    nc.scalar.activation(neg[:, j, :], neg[:, j, :], ACT.Exp).then_inc(s["exp"], 1)

        @block.gpsimd
        def _(pool):
            with pool.Fori(0, NCH) as c:
                for j in range(2):
                    pool.wait_ge(s["exp"], c * 2 + (j + 1))
                    pool.wait_ge(s["relu"], c * 2 + (j + 1))
                    nc.gpsimd.tensor_tensor(phi[:, j, :], pos[:, j, :], neg[:, j, :], ALU.add).then_inc(s["phi"], 1)

        @block.vector
        def _(dve):
            dve.sem_inc(s["x"], 1)
            dve.sem_inc(s["kv"], 4)
            nc.vector.memset(v[:], 1.0).then_inc(s["v"], 1)
            dve.wait_ge(s["v"], 1)
            blk = k.const("blk8").unsqueeze(1).to_broadcast([128, 2, D])
            with dve.Fori(0, NCH) as c:
                step = Steps(dve, s["steps"], c, 1)
                for j, bank in enumerate((q_ps, k_ps)):
                    dve.wait_ge(s["p_mm"], c * 3 + (j + 1))
                    nc.vector.tensor_scalar(neg[:, j, :], bank[:], 0.0, None, ALU.min).then_inc(s["neg"], 1)
                dve.wait_ge(s["p_mm"], c * 3 + 3)
                nc.vector.tensor_copy(v[:, :, :D], v_ps[:].rearrange("p (t d) -> p t d", d=D)).then_inc(s["v"], 1)
                for n in range(16):
                    dve.wait_ge(s["kv_mm"], c * 16 + (n + 1))
                    if n >= 4:
                        dve.wait_ge(s["y_mm"], c * 16 + (n - 3))
                    nc.vector.tensor_tensor(kv[:, n % 4, :].rearrange("p (j d) -> p j d", j=2),
                                            kv_ps[n % 4][:, :2 * D].rearrange("p (j d) -> p j d", j=2), blk,
                                            ALU.mult).then_inc(s["kv"], 1)
                dve.wait_ge(s["y_mm"], c * 16 + 16)
                step(nc.vector.tensor_scalar(rec[:], den_ps[:], 1e-6, None, ALU.add))
                nc.vector.reciprocal(rec[:], rec[:]).then_inc(s["rec"], 1)
                dve.wait_ge(s["rec"], c + 1)
                nc.vector.tensor_tensor(y[:], num_ps[:], rec[:], ALU.mult).then_inc(s["y"], 1)
                dve.wait_ge(s["o_mm"], c + 1)
                x = k.X[:, ds(c * CH, CH)]
                nc.vector.tensor_tensor(x, x, o_ps[:], ALU.add).then_inc(s["x"], 1)
                step.end()


def context_attention(k, nm, queries, u_out, project=None):
    nc, ph = k.nc, ExitStack()
    s = {n: k.sem(nm + n) for n in ("qx", "s_mm", "mx", "exp", "rec", "p", "t_mm", "pt", "u_mm", "u", "own", "o", "kv_mm",
                                    "kv", "mask", "pad")}
    ctx_in = [k.sem(nm + f"ctx_in{j}") for j in range(2)]
    mask_in = k.sem(nm + "mask_in")
    val_in = [k.sem(nm + f"val_in{j}") for j in range(2)]
    turns = B // 2
    with ph:
        ctxT = k.sb(nm + "ctxT", [128, 2, SP2], ctx=ph)
        vals = k.sb(nm + "vals", [KC, 2, NKC, D], ctx=ph)
        qx = k.sb(nm + "qx", [128, 2, H, T], ctx=ph)
        p = k.sb(nm + "p", [128, 2, SP2], ctx=ph)
        pt = k.sb(nm + "pt", [KC, 2, NKC, H * T], ctx=ph)
        col = k.sb(nm + "col", [128, 3, 4], ctx=ph)
        if project:
            keys = k.sb(nm + "keys", [128, 2, SP2], ctx=ph)
            mask_i = k.sb(nm + "mask_i", [1, B * SP2], I32, ctx=ph)
            mask = k.sb(nm + "mask", [1, 2, SP2], BF16, ctx=ph)
            one = k.sb(nm + "one", [1, 128], BF16, ctx=ph)
            own = k.sb(nm + "own", [128, 2, H, T], ctx=ph)
            o = k.sb(nm + "o", [128, 2, T], ctx=ph)
        else:
            keys = ctxT
        s_ps, t_ps, u_ps, k_ps, v_ps = k.ps[0:2], k.ps[2:4], k.ps[4:6], k.ps[6], k.ps[7]
        block = ph.enter_context(nc.Block())

        def turns_of(eng, first, body):
            first()
            with eng.Fori(0, turns - 1) as i:
                for j in range(8):
                    body(i, j, lambda jj: True)
            for j in range(8):
                body(turns - 1, j, lambda jj: jj < 8)

        @block.sync
        def _(sp):
            def fetch(l, g):
                sp.dma_start(ctxT[:, l, :], k.arr["ctxT"][:, ds(g * SP2, SP2)]).then_inc(ctx_in[l], 16)

            def fetch_rows(l, g):
                sp.dma_start(vals[:, l], k.arr["ctx_rows"][ds(g, 1)].rearrange("o p c d -> (o p) c d")
                             ).then_inc(val_in[l], 16)

            if project:
                sp.dma_start(mask_i[:], k.arr["ctx_mask"]).then_inc(mask_in, 16)
            for l in range(2):
                fetch(l, l)
                if not project:
                    fetch_rows(l, l)
            with sp.Fori(1, turns) as i:
                for l in range(2):
                    if project:
                        sp.wait_ge(s["kv_mm"], i * 4 + 2 * l)
                    else:
                        sp.wait_ge(s["s_mm"], i * 8 + (l * 4 + 4))
                    fetch(l, i * 2 + l)
                    if not project:
                        sp.wait_ge(s["u_mm"], i * 2 + (l + 1))
                        fetch_rows(l, i * 2 + l)

        @block.gpsimd
        def _(pool):
            with pool.Fori(0, turns) as i:
                for l in range(2):
                    pool.wait_ge(s["s_mm"], i * 8 + (l * 4 + 4))
                    queries(i * 2 + l, qx[:, l]).then_inc(s["qx"], 1)

        @block.tensor
        def _(pe):
            pe.sem_inc(s["s_mm"], 8)
            pe.sem_inc(s["t_mm"], 2)
            pe.sem_inc(s["u_mm"], 2)
            if project:
                pe.sem_inc(s["kv_mm"], 2)

            def make_kv(i, l):
                g = i * 2 + l
                sl = l % 2
                pe.wait_ge(ctx_in[sl], (i + l // 2) * 16 + 16)
                pe.wait_ge(s["kv"], g * 2 + 1)
                nc.tensor.matmul(k_ps[:, :SP2], project["k"], ctxT[:, sl, :], start=True, stop=True
                                 ).then_inc(s["kv_mm"], 1)
                pe.wait_ge(s["kv"], g * 2 + 2)
                for c in range(NKC):
                    mm = nc.tensor.matmul(v_ps[:KC, c * D:(c + 1) * D], ctxT[:, sl, c * KC:(c + 1) * KC], project["v"],
                                          start=True, stop=True)
                mm.then_inc(s["kv_mm"], 1)

            def score(i, j):
                n, l, sl = i * 8 + j, j // 4, (j // 4) % 2
                if j % 4 == 0:
                    pe.wait_ge(s["qx"], i * 2 + (l + 1))
                    if project:
                        pe.wait_ge(s["kv"], (i * 2 + l) * 2 + 3)
                        pe.wait_ge(s["mask"], i * 2 + (l + 2))
                    else:
                        pe.wait_ge(ctx_in[sl], (i + l // 2) * 16 + 16)
                pe.wait_ge(s["exp"], n + 1)
                q = qx[:, sl].rearrange("p h q -> p (h q)")[:, (j % 4) * 128:(j % 4 + 1) * 128]
                mm = nc.tensor.matmul(s_ps[j % 2][:, :S2], q, keys[:, sl, :S2], start=True, stop=not project)
                if project:
                    mm = nc.tensor.matmul(s_ps[j % 2][:, :S2], one[:], mask[:, sl, :S2], start=False, stop=True)
                mm.then_inc(s["s_mm"], 1)
                if project and j % 4 == 2:
                    return l + 1
                return None

            def turn(i, j):
                n = i * 8 + j
                pe.wait_ge(s["p"], n + 1)
                pe.wait_ge(s["pt"], n + 1)
                for c in range(NKC):
                    mm = nc.tensor.transpose(t_ps[j % 2][:KC, c * 128:(c + 1) * 128], p[:, j % 2, c * KC:(c + 1) * KC],
                                             k.const("ident"))
                mm.then_inc(s["t_mm"], 1)

            def first():
                if project:
                    make_kv(0, 0)
                score(0, 0)
                score(0, 1)
                turn(0, 0)
                nxt = score(0, 2)
                if nxt is not None:
                    make_kv(0, nxt)

            def body(i, j, there):
                if there(j + 1):
                    turn(i, j + 1)
                if there(j + 3):
                    nxt = score(i, j + 3)
                    if nxt is not None and there(nxt * 4):
                        make_kv(i, nxt)
                if j % 4 == 3:
                    l = j // 4
                    g = i * 2 + l
                    pe.wait_ge(s["pt"], i * 8 + (j + 3))
                    pe.wait_ge(s["u"], g + 1)
                    if project:
                        pe.wait_ge(s["kv"], g * 2 + 4)
                    else:
                        pe.wait_ge(val_in[l], i * 16 + 16)
                    for c in range(NKC):
                        mm = nc.tensor.matmul(u_ps[l][:], vals[:, l, c, :], pt[:, l, c, :], start=(c == 0),
                                              stop=(c == NKC - 1))
                    mm.then_inc(s["u_mm"], 1)

            turns_of(pe, first, body)

        def take_turned(eng, copy, i, j):
            l = j // 4
            eng.wait_ge(s["t_mm"], i * 8 + (j + 3))
            if j % 4 == 0:
                eng.wait_ge(s["u_mm"], i * 2 + (l + 1))
            copy(pt[:, l, :, (j % 4) * 128:(j % 4 + 1) * 128],
                 t_ps[j % 2][:KC, :NKC * 128].rearrange("p (c r) -> p c r", c=NKC)).then_inc(s["pt"], 1)

        @block.scalar
        def _(act):
            act.sem_inc(s["exp"], 2)
            if project:
                act.sem_inc(s["kv"], 2)
                act.sem_inc(s["pt"], 2)
            else:
                act.sem_inc(s["u"], 2)

            def take_keys(i, l):
                g = i * 2 + l
                act.wait_ge(s["kv_mm"], g * 2 + 3)
                act.wait_ge(s["s_mm"], g * 4 + 4)
                nc.scalar.activation(keys[:, l % 2, :], k_ps[:, :SP2], ACT.Identity, bias=project["kb"]
                                     ).then_inc(s["kv"], 1)

            def take_values(i, l):
                g = i * 2 + l
                act.wait_ge(s["kv_mm"], g * 2 + 4)
                act.wait_ge(s["u_mm"], g + 1)
                nc.scalar.copy(vals[:, l % 2].rearrange("p c d -> p (c d)"), v_ps[:KC, :NKC * D]).then_inc(s["kv"], 1)

            def exp(i, j):
                n = i * 8 + j
                act.wait_ge(s["mx"], n + 1)
                act.wait_ge(s["t_mm"], n + 1)
                nc.scalar.activation(p[:, j % 2, :S2], s_ps[j % 2][:, :S2], ACT.Exp, bias=col[:, 0, j % 4:j % 4 + 1],
                                     accum_out=col[:, 1, j % 4:j % 4 + 1]).then_inc(s["exp"], 1)
                if project and j % 4 == 1:
                    return j // 4 + 1
                return None

            def first():
                act.wait_ge(s["pad"], 1)
                if project:
                    take_keys(0, 0)
                    take_values(0, 0)
                for j in range(2):
                    nxt = exp(0, j)
                if nxt is not None:
                    take_keys(0, nxt)

            def body(i, j, there):
                if there(j + 2):
                    nxt = exp(i, j + 2)
                    if nxt is not None and there(nxt * 4):
                        take_keys(i, nxt)
                if project and j % 4 == 0 and there(j + 4):
                    take_values(i, j // 4 + 1)
                if project:
                    take_turned(act, nc.scalar.copy, i, j)
                elif j % 4 == 3:
                    l = j // 4
                    act.wait_ge(s["u_mm"], i * 2 + (l + 3))
                    u_out(nc.scalar, u_ps[l], i * 2 + l).then_inc(s["u"], 1)

            turns_of(act, first, body)

        @block.vector
        def _(dve):
            if project:
                dve.sem_inc(s["u"], 2)
                nc.vector.memset(one[:], 1.0).then_inc(s["mask"], 1)
                dve.wait_ge(mask_in, 16)
            else:
                dve.sem_inc(s["pt"], 2)
            nc.vector.memset(p[:, :, S2:], 0.0).then_inc(s["pad"], 1)

            def make_mask(i, l):
                sl = l % 2
                dve.wait_ge(s["s_mm"], (i * 2 + l) * 4 + 4)
                nc.vector.tensor_scalar(mask[:, sl, :], mask_i[:, ds((i * 2 + l) * SP2, SP2)], 0.0, NEG, ALU.is_gt, ALU.mult
                                        ).then_inc(s["mask"], 1)

            def maximum(i, j):
                dve.wait_ge(s["s_mm"], i * 8 + (j + 9))
                nc.vector.tensor_reduce(col[:, 0, j % 4:j % 4 + 1], s_ps[j % 2][:, :S2], AX.X, ALU.max, negate=True
                                        ).then_inc(s["mx"], 1)
                if project and j % 4 == 0:
                    return j // 4 + 1
                return None

            def normalize(i, j):
                n = i * 8 + j
                dve.wait_ge(s["exp"], n + 3)
                r = col[:, 2, j % 4:j % 4 + 1]
                nc.vector.reciprocal(r, col[:, 1, j % 4:j % 4 + 1]).then_inc(s["rec"], 1)
                dve.wait_ge(s["rec"], n + 1)
                nc.vector.tensor_scalar(p[:, j % 2, :], p[:, j % 2, :], r, None, ALU.mult).then_inc(s["p"], 1)

            def gather(i, l):
                g = i * 2 + l
                dve.wait_ge(s["u_mm"], g + 3)
                nc.vector.tensor_tensor(own[:, l], u_ps[l][:].rearrange("p (h q) -> p h q", h=H),
                                        k.const("hmask").unsqueeze(2).to_broadcast([128, H, T]), ALU.mult
                                        ).then_inc(s["u"], 1)
                dve.wait_ge(s["u"], g + 3)
                nc.vector.tensor_reduce(o[:, l, :], own[:, l].rearrange("p h q -> p q h"), AX.X, ALU.add
                                        ).then_inc(s["own"], 1)
                dve.wait_ge(s["own"], g + 1)
                x = k.X[:, ds(g * T, T)]
                nc.vector.scalar_tensor_tensor(out=x, in0=o[:, l, :], scalar=project["vb"], in1=x, op0=ALU.add, op1=ALU.add
                                               ).then_inc(s["o"], 1)

            def first():
                if project:
                    make_mask(0, 0)
                for j in range(2):
                    nxt = maximum(0, j)
                    if nxt is not None:
                        make_mask(0, nxt)
                normalize(0, 0)

            def body(i, j, there):
                if there(j + 2):
                    nxt = maximum(i, j + 2)
                    if nxt is not None and there(nxt * 4):
                        make_mask(i, nxt)
                if there(j + 1):
                    normalize(i, j + 1)
                if not project:
                    take_turned(dve, nc.vector.tensor_copy, i, j)
                elif j == 4:
                    gather(i, 0)
                elif j == 7:
                    gather(i, 1)

            turns_of(dve, first, body)


def l1_xattn(k):
    nc, ph, hp = k.nc, ExitStack(), H // 2
    s = {n: k.sem("l1x_" + n) for n in ("w_mm", "w", "b_mm", "b", "q_mm", "q", "o_mm", "x")}
    with ph:
        wqk, wvo = (k.sb("l1x_" + n, [128, H, D], ctx=ph) for n in ("wqk", "wvo"))
        bqk, bo = k.sb("l1x_bqk", [128, H], ctx=ph), k.sb("l1x_bo", [128, 2], ctx=ph)
        qt = k.sb("l1x_qt", [128, H, N], ctx=ph)
        with ExitStack() as st:
            wq, wk, wv, wo = (k.sb("l1x_" + n, [128, hp, D], ctx=st) for n in ("wq", "wk", "wv", "wo"))
            bq, bv = (k.sb("l1x_" + n, [128, hp], ctx=st) for n in ("bq", "bv"))
            load(k, "l1xw_", ((wq[:], "l1x_wq"), (wk[:], "l1x_wk"), (wv[:], "l1x_wv"), (wo[:], "l1x_wo"),
                             (bq[:], "l1x_bq"), (bv[:], "l1x_bv"), (bo[:, 0:1], "l1x_bo")))
            with nc.Block() as block:
                @block.tensor
                def _(pe):
                    for h in range(H):
                        r = slice(64 * (h % 2), 64 * (h % 2) + 64)
                        for j, (a, b) in enumerate(((wq, wk), (wv, wo))):
                            m = 2 * h + j
                            if m >= 4:
                                pe.wait_ge(s["w"], m - 3)
                            nc.tensor.matmul(k.ps[m % 4][:, :D], a[r, h // 2, :], b[r, h // 2, :], start=True, stop=True
                                             ).then_inc(s["w_mm"], 1)
                        ins = nc.tensor.matmul(k.ps[4 + h % 2][:, h:h + 1], wk[r, h // 2, :], bq[r, h // 2:h // 2 + 1],
                                               start=True, stop=True)
                    for j in range(hp):
                        ins = nc.tensor.matmul(k.ps[6][:, 0:1], wo[:, j, :], bv[:, j:j + 1], start=(j == 0),
                                               stop=(j == hp - 1))
                    ins.then_inc(s["b_mm"], 1)

                @block.scalar
                def _(act):
                    for m in range(2 * H):
                        act.wait_ge(s["w_mm"], m + 1)
                        nc.scalar.copy((wqk, wvo)[m % 2][:, m // 2, :], k.ps[m % 4][:, :D]).then_inc(s["w"], 1)

                @block.vector
                def _(dve):
                    dve.wait_ge(s["b_mm"], 1)
                    for j in range(2):
                        nc.vector.tensor_copy(bqk[:].rearrange("p (h j) -> p j h", j=2)[:, j, :],
                                              k.ps[4 + j][:, :H].rearrange("p (h j) -> p j h", j=2)[:, j, :]
                                              ).then_inc(s["b"], 1)
                    nc.vector.tensor_tensor(bo[:, 1:2], bo[:, 0:1], k.ps[6][:, 0:1], ALU.add).then_inc(s["b"], 1)
        with nc.Block() as block:
            @block.tensor
            def _(pe):
                with pe.Fori(0, NCH) as c:
                    for h in range(H):
                        pe.wait_ge(s["q"], c * H + (h + 1))
                        nc.tensor.matmul(k.ps[h % 8][:], wqk[:, h, :], k.XN[:, ds(c * CH, CH)], start=True, stop=True
                                         ).then_inc(s["q_mm"], 1)

            @block.vector
            def _(dve):
                dve.sem_inc(s["q"], 8)
                with dve.Fori(0, NCH) as c:
                    for h in range(H):
                        dve.wait_ge(s["q_mm"], c * H + (h + 1))
                        nc.vector.tensor_scalar(qt[:, h, ds(c * CH, CH)], k.ps[h % 8][:], bqk[:, h:h + 1], 0.125, ALU.add,
                                                ALU.mult).then_inc(s["q"], 1)

        def queries(g, dst):
            return nc.gpsimd.tensor_copy(dst, qt[:, :, ds(g * T, T)])

        def u_out(act, bank, g):
            return act.copy(qt[:, :, ds(g * T, T)], bank[:].rearrange("p (h q) -> p h q", h=H))

        context_attention(k, "l1xc_", queries, u_out)
        with nc.Block() as block:
            @block.tensor
            def _(pe):
                with pe.Fori(0, NCH) as c:
                    pe.wait_ge(s["x"], c + 1)
                    for h in range(H):
                        mm = nc.tensor.matmul(k.ps[0][:], wvo[:, h, :], qt[:, h, ds(c * CH, CH)], start=(h == 0),
                                              stop=(h == H - 1))
                    mm.then_inc(s["o_mm"], 1)

            @block.vector
            def _(dve):
                dve.sem_inc(s["x"], 1)
                with dve.Fori(0, NCH) as c:
                    dve.wait_ge(s["o_mm"], c + 1)
                    x = k.X[:, ds(c * CH, CH)]
                    nc.vector.scalar_tensor_tensor(out=x, in0=k.ps[0][:], scalar=bo[:, 1:2], in1=x, op0=ALU.add,
                                                   op1=ALU.add).then_inc(s["x"], 1)


def l2_xattn(k):
    nc, ph = k.nc, ExitStack()
    s = {n: k.sem("l2x_" + n) for n in ("q_mm", "q")}
    with ph:
        w = k.sb("l2x_w", [128, 3, D], ctx=ph)
        b = k.sb("l2x_b", [128, 3], ctx=ph)
        q = k.sb("l2x_q", [128, N], ctx=ph)
        load(k, "l2x_", ((w[:], "l2x_w"), (b[:], "l2x_b")))
        with nc.Block() as block:
            @block.tensor
            def _(pe):
                for c in range(NCH):
                    nc.tensor.matmul(k.ps[c][:], w[:, 0, :], k.XN[:, c * CH:(c + 1) * CH], start=True, stop=True
                                     ).then_inc(s["q_mm"], 1)

            @block.vector
            def _(dve):
                for c in range(NCH):
                    dve.wait_ge(s["q_mm"], c + 1)
                    nc.vector.tensor_scalar(q[:, c * CH:(c + 1) * CH], k.ps[c][:], b[:, 0:1],
                                            float(1.0 / np.sqrt(np.float32(D // H))), ALU.add, ALU.mult
                                            ).then_inc(s["q"], 1)

        def queries(g, dst):
            return nc.gpsimd.tensor_tensor(dst, q[:, ds(g * T, T)].unsqueeze(1).to_broadcast([128, H, T]),
                                           k.const("hmask").unsqueeze(2).to_broadcast([128, H, T]), ALU.mult)

        context_attention(k, "l2xc_", queries, None,
                          {"k": w[:, 1, :], "v": w[:, 2, :], "kb": b[:, 1:2], "vb": b[:, 2:3]})


def delta_slots():
    s = {h: 4 * (h // 4) + 2 * (h % 2) + (h % 4) // 2 for h in range(H)}
    r = {h: 8 * (h // 8) + 4 * (h % 2) + (h % 8) // 2 for h in range(H)}
    return s, r


LEVELS = 5
DELTA_STEPS_DVE = 97
DELTA_STEPS_POOL = 18


def l1_attn(k):
    nc, ph, hp = k.nc, ExitStack(), H // 2
    slot_s, slot_r = delta_slots()
    names = ("src", "pj_mm", "q", "k", "ksq", "apre", "gate", "nb_mm", "nrm", "bg", "small", "bc_mm", "kn", "v_mm", "v",
             "rowS", "rowR", "mS_mm", "mS", "mR_mm", "mR", "turned", "back", "wide", "u_mm", "u", "pr_mm", "r", "w_mm", "wout",
             "o_mm", "o", "out_mm", "x", "dve", "pool", "zero", "p0", "seen")
    s = {n: k.sem("l1d_" + n) for n in names}
    with ph:
        sb = lambda n, shape, dt=F32: k.sb("l1d_" + n, shape, dt, ctx=ph)
        xn2, lncol = sb("xn2", [128, N]), sb("lncol", [128, 2])
        wp = sb("wp", [128, 4, 1024])
        wv, wo, wbg = sb("wv", [128, 1024]), sb("wo", [128, hp, D]), sb("wbg", [128, 2, H])
        abias, bgcol = sb("abias", [128, 2, hp]), sb("bgcol", [H, 2])
        hsum, hsel = sb("hsum", [128, hp, H]), sb("hsel", [H, hp, 128])
        lmask, imask = sb("lmask", [128, LEVELS, 64], I32), sb("imask", [128, 128], I32)
        src = sb("src", [128, 128])
        q, kk, ksq, a, ar = (sb(n, [128, hp, 128]) for n in ("q", "k", "ksq", "a", "ar"))
        small, nrm = sb("small", [H, 3, 128]), sb("nrm", [H, 128])
        kn3 = sb("kn3", [128, 3, hp, 128])
        sx, px, sxr = (sb(n, [128, hp, 128]) for n in ("sx", "px", "sxr"))
        rows_sr = sb("rows_sr", [128, 5 * 1024])
        row_s = rows_sr[:, :3072].rearrange("p (l h f t) -> p l h f t", l=2, h=hp, f=3)
        row_r = rows_sr[:, 3072:].rearrange("p (l h f t) -> p l h f t", l=2, h=hp, f=2)
        col_s, col_r = sb("col_s", [128, 2, hp, 128]), sb("col_r", [128, 2, hp, 128])
        ms, mr = sb("ms", [128, H, 3, 128]), sb("mr", [128, H, 2, 128])
        xi, wmat = sb("xi", [128, T, T]), sb("wmat", [128, 16, 16])
        wide = sb("wide", [128, 2 * H, 128])
        tmp = rows_sr
        flat3 = lambda t: t[:].rearrange("p h t -> p (h t)")
        v, u, r, w, ot = flat3(ksq), flat3(sx), flat3(px), flat3(sxr), kk
        kc, lt = (flat3(t).rearrange("p (t c) -> p t c", t=T) for t in (a, ar))
        load(k, "l1d_", ((lncol[:], "l1d_ln"), (wp[:], "l1d_wp"), (wv[:], "l1d_wv"), (wo[:], "l1d_wo"), (wbg[:], "l1d_wbg"),
                         (abias[:], "l1d_ab"), (bgcol[:], "l1d_bg"), (hsum[:], "l1d_hsum"), (hsel[:], "l1d_hsel"),
                         (lmask[:], "l1d_lmask"), (imask[:], "l1d_imask")))
        layer_norm(k, k.XN, xn2, (lncol[:, 0:1], lncol[:, 1:2]))
        ones = k.const("ones")[:, 0:1]
        kn, kb, kg = kn3[:, 0], kn3[:, 1], kn3[:, 2]

        def half(ap, m, up):
            x = ap.rearrange("p h (n two m) -> p h n two m", two=2, m=m)
            return x[:, :, :, up, :]

        def packed(ap, m):
            return ap.rearrange("p h (n m) -> p h n m", m=m)

        def last(ap, m):
            return ap[:, :, :, m - 1:m].to_broadcast([128, hp, 64 // m, m])

        block = ph.enter_context(nc.Block())

        @block.scalar
        def _(act):
            act.sem_inc(s["x"], 1)
            with act.Fori(0, NT) as i:
                act.wait_ge(s["x"], i + 1)
                nc.scalar.copy(src[:], xn2[:, ds(i * 128, 128)]).then_inc(s["src"], 1)
                flat = lambda t, j: t[:, 4 * j:4 * j + 4, :].rearrange("p h t -> p (h t)")
                for j in range(2):
                    act.wait_ge(s["pj_mm"], i * 8 + (j + 1))
                    nc.scalar.copy(flat(q, j), k.ps[j][:]).then_inc(s["q"], 1)
                for j in range(2):
                    act.wait_ge(s["pj_mm"], i * 8 + (j + 3))
                    nc.scalar.copy(flat(kk, j), k.ps[2 + j][:]).then_inc(s["k"], 1)
                    nc.scalar.activation(flat(ksq, j), k.ps[2 + j][:], ACT.Square).then_inc(s["ksq"], 1)
                for j, t in enumerate((a, ar)):
                    act.wait_ge(s["apre"], i * 4 + (2 * j + 2))
                    nc.scalar.activation(t[:], t[:], ACT.Sigmoid).then_inc(s["gate"], 1)
                act.wait_ge(s["nb_mm"], i + 1)
                for j in range(2):
                    nc.scalar.activation(small[:, 1 + j, :], k.ps[1][:H, j * 128:(j + 1) * 128], ACT.Sigmoid,
                                         bias=bgcol[:, j:j + 1]).then_inc(s["bg"], 1)
                nc.scalar.activation(nrm[:], k.ps[0][:H, :128], ACT.Sqrt).then_inc(s["nrm"], 1)
                for j in range(2):
                    act.wait_ge(s["v_mm"], i * 2 + (j + 1))
                    nc.scalar.copy(v[:, j * 512:(j + 1) * 512], k.ps[6 + j][:]).then_inc(s["v"], 1)
                act.wait_ge(s["zero"], 3)
                act.wait_ge(s["back"], i + 1)
                for b in range(TB):
                    rows = slice(b * T, b * T + T)
                    nc.scalar.copy(wide[rows, :, b * T:b * T + T], kc[rows].rearrange("p t c -> p c t")
                                   ).then_inc(s["wide"], 1)
                for nm, mm, dst, b0 in (("u", "u_mm", u, 0), ("wout", "w_mm", w, 4)):
                    for j in range(2):
                        act.wait_ge(s[mm], i * 2 + (j + 1))
                        nc.scalar.copy(dst[:, j * 512:(j + 1) * 512], k.ps[b0 + j][:]).then_inc(s[nm], 1)
                for j in range(2):
                    act.wait_ge(s["o_mm"], i * 2 + (j + 1))
                    nc.scalar.copy(flat(ot, j), k.ps[6 + j][:]).then_inc(s["o"], 1)

        @block.tensor
        def _(pe):
            with pe.Fori(0, NT) as i:
                pe.wait_ge(s["src"], i + 1)
                for n in range(4):
                    for j in range(2):
                        for e in range(4):
                            c = (4 * j + e) * 128
                            mm = nc.tensor.matmul(k.ps[2 * n + j][:, e * 128:(e + 1) * 128], wp[:, n, c:c + 128], src[:],
                                                  start=True, stop=True)
                        mm.then_inc(s["pj_mm"], 1)
                pe.wait_ge(s["q"], i * 2 + 2)
                pe.wait_ge(s["ksq"], i * 2 + 2)
                for j in range(2):
                    nc.tensor.matmul(k.ps[1][:H, j * 128:(j + 1) * 128], wbg[:, j, :], src[:], start=True, stop=True)
                for p in range(hp):
                    mm = nc.tensor.matmul(k.ps[0][:H, :128], hsum[:, p, :], ksq[:, p, :], start=(p == 0),
                                          stop=(p == hp - 1))
                mm.then_inc(s["nb_mm"], 1)
                pe.wait_ge(s["apre"], i * 4 + 4)
                for j in range(2):
                    nc.tensor.matmul(k.ps[6 + j][:], src[:], wv[:, j * 512:(j + 1) * 512], start=True, stop=True
                                     ).then_inc(s["v_mm"], 1)
                pe.wait_ge(s["small"], i + 1)
                for p in range(hp):
                    if p >= 4:
                        pe.wait_ge(s["kn"], i * 8 + (p - 3))
                    nc.tensor.matmul(k.ps[2 + p % 4][:, :384], hsel[:, p, :], small[:].rearrange("p n t -> p (n t)"),
                                     start=True, stop=True).then_inc(s["bc_mm"], 1)
                pe.wait_ge(s["kn"], i * 8 + 8)
                pe.wait_ge(s["v"], i * 2 + 2)
                ns, nr = 4 + 8 * LEVELS, 4 + 4 * LEVELS

                def fill(which, at, heads, cols, lhs, rhs):
                    sem, done, per = ("mS_mm", "mS", ns) if which == "S" else ("mR_mm", "mR", nr)
                    bank = k.ps[(0 if which == "S" else 4) + at % 4]
                    if at >= 4:
                        pe.wait_ge(s[done], i * per + (at - 3))
                    for e, h in enumerate(heads):
                        rr = slice(64 * (h % 2), 64 * (h % 2) + 64)
                        mm = nc.tensor.matmul(bank[:, e * cols:(e + 1) * cols], lhs[rr, h // 2, :], rhs(rr, h // 2),
                                              start=True, stop=True)
                    mm.then_inc(s[sem], 1)

                for which, key in (("S", kb), ("R", kg)):
                    for at in range(4):
                        fill(which, at, [8 * (at // 2) + 2 * e + at % 2 for e in range(4)], 128, key,
                             lambda rr, p: q[rr, p, :])
                for lv in range(LEVELS):
                    pe.wait_ge(s["rowS"], i * LEVELS + (lv + 1))
                    for g in range(8):
                        fill("S", 4 + lv * 8 + g, [4 * (g // 2) + g % 2 + 2 * e for e in range(2)], 192,
                             kb if lv == 0 else col_s[:, lv % 2],
                             lambda rr, p: row_s[rr, lv % 2, p].rearrange("p f t -> p (f t)"))
                    pe.wait_ge(s["rowR"], i * LEVELS + (lv + 1))
                    for g in range(4):
                        fill("R", 4 + lv * 4 + g, [8 * (g // 2) + g % 2 + 2 * e for e in range(4)], 128,
                             kg if lv == 0 else col_r[:, lv % 2],
                             lambda rr, p: row_r[rr, lv % 2, p].rearrange("p f t -> p (f t)"))

                def apply(bank0, sem, lhs, rhs):
                    for h in range(H):
                        mm = nc.tensor.matmul(k.ps[bank0 + h // 8][:, (h % 8) * 64:(h % 8 + 1) * 64], lhs(h),
                                              rhs[:, h * 64:(h + 1) * 64], start=True, stop=True)
                        if h % 8 == 7:
                            mm.then_inc(s[sem], 1)

                pe.wait_ge(s["wide"], i * 4 + 4)
                apply(0, "u_mm", lambda h: wide[:, slot_s[h], :], v)
                pe.wait_ge(s["u"], i * 2 + 2)
                apply(2, "pr_mm", lambda h: ms[:, slot_s[h], 1, :], u)
                pe.wait_ge(s["r"], i + 1)
                apply(4, "w_mm", lambda h: wide[:, H + slot_r[h], :], r)
                pe.wait_ge(s["wout"], i * 2 + 2)
                for h in range(H):
                    out = k.ps[6 + h // 8][64 * (h % 2):64 * (h % 2) + 64, (h // 2 % 4) * 128:(h // 2 % 4 + 1) * 128]
                    nc.tensor.matmul(out, u[:, h * 64:(h + 1) * 64], ms[:, slot_s[h], 2, :], start=True, stop=False)
                    mm = nc.tensor.matmul(out, w[:, h * 64:(h + 1) * 64], mr[:, slot_r[h], 1, :], start=False, stop=True)
                    if h % 8 == 7:
                        mm.then_inc(s["o_mm"], 1)
                pe.wait_ge(s["o"], i * 2 + 2)
                for p in range(hp):
                    mm = nc.tensor.matmul(k.ps[0][:, :128], wo[:, p, :], ot[:, p, :], start=(p == 0), stop=(p == hp - 1))
                mm.then_inc(s["out_mm"], 1)

        @block.gpsimd
        def _(pool):
            tt = nc.gpsimd.tensor_tensor
            one = lambda m: ones.unsqueeze(2).unsqueeze(3).to_broadcast([128, hp, 64 // m, m])
            with pool.Fori(0, NT) as i:
                step = Steps(pool, s["pool"], i, DELTA_STEPS_POOL)
                pool.wait_ge(s["gate"], i * 2 + 2)
                pool.wait_ge(s["kn"], i * 8 + 8)
                for lv in range(LEVELS):
                    m = 1 << lv
                    lo, up = (lambda t: half(t, m, 0)), (lambda t: half(t[:], m, 1))
                    if lv >= 2:
                        pool.wait_ge(s["mR_mm"], i * (4 + 4 * LEVELS) + (4 + 4 * (lv - 1)))
                    if lv >= 1:
                        step(tt(half(col_r[:, lv % 2], m, 0), half(kg, m, 0), half(sxr[:], m, 0), ALU.mult))
                    step(tt(packed(row_r[:, lv % 2, :, 0, :], m), half(kn, m, 1), up(ar), ALU.mult))
                    tt(packed(row_r[:, lv % 2, :, 1, :], m), up(q), up(ar), ALU.mult).then_inc(s["rowR"], 1)
                    pool.wait_ge(s["rowR"], i * LEVELS + (lv + 1))
                    if lv == LEVELS - 1:
                        break
                    if lv == 0:
                        step(tt(half(sxr[:], m, 0), half(ar[:], m, 1), one(m), ALU.mult))
                        step(tt(half(sxr[:], m, 1), one(m), one(m), ALU.mult))
                    else:
                        step(tt(half(sxr[:], m, 0), half(sxr[:], m, 0), last(up(ar), m), ALU.mult))
                    step(tt(up(ar), up(ar), last(half(ar[:], m, 0), m), ALU.mult))
                step.end()

        @block.vector
        def _(dve):
            tt, vc = nc.vector.tensor_tensor, nc.vector
            vc.memset(wide[:], 0.0).then_inc(s["zero"], 1)
            vc.memset(ms[:], 0.0).then_inc(s["zero"], 1)
            vc.memset(mr[:], 0.0).then_inc(s["zero"], 1)
            vc.memset(col_s[:], 0.0).then_inc(s["p0"], 1)
            vc.memset(col_r[:], 0.0).then_inc(s["p0"], 1)
            dve.wait_ge(s["zero"], 3)
            dve.wait_ge(s["p0"], 2)
            ns, nr = 4 + 8 * LEVELS, 4 + 4 * LEVELS
            with dve.Fori(0, NT) as i:
                step = Steps(dve, s["dve"], i, DELTA_STEPS_DVE)
                for n, t in enumerate((a, ar)):
                    for j in range(2):
                        dve.wait_ge(s["pj_mm"], i * 8 + (5 + 2 * n + j))
                        tt(t[:, 4 * j:4 * j + 4, :], k.ps[4 + 2 * n + j][:].rearrange("p (h t) -> p h t", t=128),
                           abias[:, n, 4 * j:4 * j + 4].unsqueeze(2).to_broadcast([128, 4, 128]), ALU.add
                           ).then_inc(s["apre"], 1)
                dve.wait_ge(s["nrm"], i + 1)
                dve.wait_ge(s["bg"], i * 2 + 2)
                step(vc.tensor_scalar(nrm[:], nrm[:], 1e-12, None, ALU.max))
                step(vc.reciprocal(small[:, 0, :], nrm[:]))
                tt(small[:, 1:3, :], small[:, 1:3, :], small[:, 0:1, :].to_broadcast([H, 2, 128]), ALU.mult
                   ).then_inc(s["small"], 1)
                dve.wait_ge(s["k"], i * 2 + 2)
                for p in range(hp):
                    dve.wait_ge(s["bc_mm"], i * 8 + (p + 1))
                    tt(kn3[:, :, p, :], k.ps[2 + p % 4][:, :384].rearrange("p (n t) -> p n t", n=3),
                       kk[:, p:p + 1, :].to_broadcast([128, 3, 128]), ALU.mult).then_inc(s["kn"], 1)
                dve.wait_ge(s["kn"], i * 8 + 8)
                dve.wait_ge(s["gate"], i * 2 + 1)

                def rows(lv):
                    m = 1 << lv
                    up, lo = (lambda t: half(t[:], m, 1)), (lambda t: half(t[:], m, 0))
                    if lv >= 2:
                        dve.wait_ge(s["mS_mm"], i * ns + (4 + 8 * (lv - 1)))
                    if lv >= 1:
                        step(tt(half(col_s[:, lv % 2], m, 0), half(kb, m, 0), lo(sx), ALU.mult))
                    step(tt(packed(row_s[:, lv % 2, :, 0, :], m), half(kn, m, 1), up(a), ALU.mult))
                    if lv == 0:
                        step(vc.tensor_copy(packed(row_s[:, lv % 2, :, 1, :], m), half(kn, m, 1)))
                    else:
                        step(tt(packed(row_s[:, lv % 2, :, 1, :], m), half(kn, m, 1), up(px), ALU.mult))
                    tt(packed(row_s[:, lv % 2, :, 2, :], m), up(q), up(a), ALU.mult).then_inc(s["rowS"], 1)
                    dve.wait_ge(s["rowS"], i * LEVELS + (lv + 1))
                    if lv == LEVELS - 1:
                        return
                    if lv == 0:
                        step(vc.memset(sx[:], 1.0))
                        step(vc.memset(px[:], 1.0))
                        step(vc.tensor_copy(lo(sx), up(a)))
                        step(vc.tensor_copy(up(px), lo(a)))
                    else:
                        step(tt(lo(sx), lo(sx), last(up(a), m), ALU.mult))
                        step(tt(up(px), up(px), last(lo(a), m), ALU.mult))
                    step(tt(up(a), up(a), last(lo(a), m), ALU.mult))

                def keep(lv):
                    m = 1 << lv
                    n = 64 // m
                    msk = lmask[:, lv].rearrange("p (n m) -> p n m", m=m).unsqueeze(1)
                    cut = lambda x, f: x.rearrange("p s f (n two m) -> p (s f) n two m", two=2, m=m)[:, :, :, 1, :]
                    for g in range(8):
                        at = 4 + lv * 8 + g
                        dve.wait_ge(s["mS_mm"], i * ns + (at + 1))
                        dve.sem_inc(s["seen"], 1)
                        vc.copy_predicated(cut(ms[:, 2 * g:2 * g + 2], 3), msk.to_broadcast([128, 6, n, m]),
                                           k.ps[at % 4][:, :384].rearrange("p (f n m) -> p f n m", n=n, m=m)
                                           ).then_inc(s["mS"], 1)
                    for g in range(4):
                        at = 4 + lv * 4 + g
                        dve.wait_ge(s["mR_mm"], i * nr + (at + 1))
                        dve.sem_inc(s["seen"], 1)
                        vc.copy_predicated(cut(mr[:, 4 * g:4 * g + 4], 2), msk.to_broadcast([128, 8, n, m]),
                                           k.ps[4 + at % 4][:].rearrange("p (f n m) -> p f n m", n=n, m=m)
                                           ).then_inc(s["mR"], 1)

                rows(0)
                im = imask[:].unsqueeze(1)
                for at in range(4):
                    dve.wait_ge(s["mS_mm"], i * ns + (at + 1))
                    dve.sem_inc(s["seen"], 1)
                    pr, g8 = at % 2, at // 2
                    for e in range(2):
                        o = 8 * g8 + 4 * e + 2 * pr
                        ins = vc.copy_predicated(ms[:, o:o + 2, 2, :], im.to_broadcast([128, 2, 128]),
                                                 k.ps[at][:, e * 256:(e + 1) * 256].rearrange("p (s t) -> p s t", s=2))
                    ins.then_inc(s["mS"], 1)
                for at in range(4):
                    dve.wait_ge(s["mR_mm"], i * nr + (at + 1))
                    dve.sem_inc(s["seen"], 1)
                    vc.copy_predicated(mr[:, 4 * at:4 * at + 4, 1, :], im.to_broadcast([128, 4, 128]),
                                       k.ps[4 + at][:].rearrange("p (s t) -> p s t", s=4)).then_inc(s["mR"], 1)
                for lv in range(LEVELS):
                    if lv + 1 < LEVELS:
                        rows(lv + 1)
                    keep(lv)
                dve.wait_ge(s["mS"], i * ns + ns)
                dve.wait_ge(s["mR"], i * nr + nr)
                by_t = lambda x: x.rearrange("p s (b t) -> p s t b", b=TB)
                step(vc.tensor_reduce(kc[:, :, :H].rearrange("p t c -> p c t"), by_t(ms[:, :, 0, :]), AX.X, ALU.add))
                step(vc.tensor_reduce(kc[:, :, H:].rearrange("p t c -> p c t"), by_t(mr[:, :, 0, :]), AX.X, ALU.add))
                step(vc.transpose(lt.rearrange("p t c -> p (t c)"), kc.rearrange("p t c -> p (t c)")))
                step(vc.tensor_scalar(xi[:], lt, -1.0, None, ALU.mult))
                step(vc.memset(xi[:].rearrange("p t c -> p (t c)")[:, 0:T * T:T + 1], 1.0))
                for lv in range(1, LEVELS):
                    m = 1 << lv
                    t4 = tmp[:, :m * m * m].rearrange("p (r c k) -> p r c k", r=m, c=m)
                    for b in range(T // (2 * m)):
                        lo, hi = slice(2 * m * b, 2 * m * b + m), slice(2 * m * b + m, 2 * m * b + 2 * m)
                        rk = lambda x: x.unsqueeze(2).to_broadcast([128, m, m, m])
                        kc_ = lambda x: x.rearrange("p k c -> p c k").unsqueeze(1).to_broadcast([128, m, m, m])
                        step(tt(t4, rk(lt[:, hi, lo]), kc_(xi[:, lo, lo]), ALU.mult))
                        step(vc.tensor_reduce(wmat[:, :m, :m], t4, AX.X, ALU.add))
                        step(tt(t4, rk(xi[:, hi, hi]), kc_(wmat[:, :m, :m]), ALU.mult))
                        step(vc.tensor_reduce(xi[:, hi, lo], t4, AX.X, ALU.add, negate=True))
                vc.transpose(kc.rearrange("p t c -> p (t c)"), xi[:].rearrange("p t c -> p (t c)")
                             ).then_inc(s["back"], 1)
                for j in range(2):
                    dve.wait_ge(s["pr_mm"], i * 2 + (j + 1))
                    c = slice(j * 512, j * 512 + 512)
                    step(tt(r[:, c], v[:, c], k.ps[2 + j][:], ALU.subtract))
                vc.tensor_scalar(r, r, 1.0, -1.0, ALU.min, ALU.max).then_inc(s["r"], 1)
                dve.wait_ge(s["out_mm"], i + 1)
                x = k.X[:, ds(i * 128, 128)]
                tt(x, x, k.ps[0][:, :128], ALU.add).then_inc(s["x"], 1)
                step.end()
        ph.pop_all().close()
        add_normed(k, "l1d_")


SUBLAYERS = {4: l1_attn, 3: l1_xattn, 6: l2_xattn, 0: l0_xattn, 1: l0_attn, 2: l0_ffn, 5: l1_ffn, 7: l2_attn, 10: l3_attn, 8: l2_ffn, 9: l3_xattn, 11: l3_ffn}


def program(nc, arr, out):
    ctx = ExitStack()
    with ctx:
        k = Core(nc, ctx, arr, out)
        load_state(k)
        for p in PHASES:
            before = nc.snapshot_sems()
            layer_norm(k, k.X, k.XN)
            SUBLAYERS[p](k)
            nc.clear_and_free_semaphores(nc.allocated_since(before))
            nc.all_engine_barrier()
        store_state(k)


def laid_out(a):
    f = lambda v: np.ascontiguousarray(v)
    ctx = a["ctx_1024"]
    pad = np.concatenate([ctx, np.zeros((B, SP2 - S2, D), ctx.dtype)], 1)
    m = a["mask_1xSxS2_ff0"][0]
    mpad = np.concatenate([m, np.zeros((T, SP2 - S2), m.dtype)], 1)
    real = np.ones((1, SP2), np.float32)
    real[:, S2:] = 0
    r = {
        "xT": f(a["x"].reshape(N, D).T),
        "consts": constants(),
        "ctxT": f(pad.transpose(2, 0, 1).reshape(D, B * SP2)),
        "real_rows": real.reshape(1, NKC, KC),
        "l0x_mask": f(mpad.T.reshape(NKC, KC, T).transpose(1, 0, 2)),
        "l0x_bcol": f(np.stack([a["L0_xattn_bias_q"], a["L0_xattn_bias_k"]], 1)),
        "L0_xattn_bias_v": f(a["L0_xattn_bias_v"].reshape(1, D)),
    }
    wq, wk, wv = np.split(a["L0_attn_Wqkv"], 3, 1)
    swap = np.arange(D) ^ 1
    r["l0a_w"] = f(np.stack([wq, wq[:, swap], wk, wk[:, swap], wv], 1))
    r["L0_attn_Wproj"] = f(a["L0_attn_Wproj"])
    r["l0a_cw"] = f(np.tile(np.concatenate([np.zeros(1, np.float32), a["L0_attn_cascade_w"]]), (128, 1)))
    r["ctx_head"] = f(ctx[:, :T].reshape(N, D).T)
    L = lambda n: a["L3_xattn_" + n]
    r["l3x_w"] = f(np.stack([L("Wq").T, L("Wf")[:D].T, L("Wf")[D:].T, L("Wp").T], 1))
    r["l3x_A"] = f(np.stack([L("Aq").T, L("Af").T, L("Ap").T], 1))
    r["l3x_B"] = f(np.stack([L("Bq").T, L("Bf")[:D].T, L("Bf")[D:].T, L("Bp").T], 1))
    r["l3x_bcol"] = f(np.stack([L("bq"), L("bf")[:D], L("bp")], 1))
    r["l3x_bv"] = f(L("bf")[D:].reshape(1, D))
    def expert_pack(up, down, cols):
        e, d, ff = down.shape
        return f(np.concatenate([u.transpose(0, 2, 1) for u in up]
                                + [down.transpose(0, 2, 1).reshape(e, ff // 128, 128, d).transpose(0, 2, 1, 3)
                                   .reshape(e, 128, ff)] + cols, 2))

    G = lambda n: a["L0_ffn_" + n]
    r["l0f_cen"] = f(G("centroids").T)
    r["l0f_w"] = expert_pack([G("w1")], G("w2"), [G("b1").reshape(8, 4, 128).transpose(0, 2, 1)]
                             + [G(n)[:, :, None] for n in ("b2", "ln_g", "ln_b")])
    r["sel"] = np.repeat(np.eye(17, dtype=np.float32), 128, 1)
    r["bits_i"] = np.tile((np.int64(1) << np.arange(32)).astype(np.uint32).view(np.int32), (16, 1))
    G2 = lambda n: a["L2_ffn_" + n]
    r["l2f_gw"] = f(G2("gate_w").T)
    r["l2f_w"] = expert_pack([G2("Wg"), G2("Wu")], G2("Wd"), [])
    r["l2f_s"] = expert_pack([G2("Sg")[None], G2("Su")[None]], G2("Sd")[None], [])
    G3 = lambda n: a["L3_ffn_" + n]
    r["places"] = np.tile(np.arange(N, dtype=np.float32), (128, 1))
    r["l3f_tri"] = np.triu(np.ones((8, 8), np.float32), 1)
    r["l3f_gw"] = f(G3("Ws").T)
    r["l3f_bs"] = f(np.tile(G3("bs")[None], (128, 1)))
    r["l3f_top"] = f(np.repeat(np.eye(9, dtype=np.float32)[:, 8:], 128, 1))
    r["l3f_w"] = f(np.concatenate([G3("W1"), G3("W2"), G3("b1")[:, :, None], G3("b2")[:, :, None],
                                   np.zeros((8, D, 2), np.float32)], 2))
    r["L1_ffn_weight"], r["l1f_bias"] = f(a["L1_ffn_weight"]), f(a["L1_ffn_bias"][:, None])
    A = lambda n: a["L2_attn_" + n]
    for n in ("q", "k", "v"):
        r["l2a_w" + n] = f(A("w" + n).reshape(D, 1024))
    r["l2a_wo"] = f(A("wo").reshape(8, 128, D).transpose(1, 0, 2))
    r["l2a_bq"], r["l2a_bk"] = f(A("bq").reshape(8, 128).T), f(A("bk").reshape(8, 128).T)
    r["l2a_bv"], r["l2a_bo"] = f(np.tile(A("bv").reshape(1, 1024), (128, 1))), f(A("bo")[:, None])
    r["l3a_w"] = f(np.stack([a["L3_attn_W" + n] for n in "qkvo"], 1))
    r["ctx_rows"] = f(pad.reshape(B, NKC, KC, D).transpose(0, 2, 1, 3))
    M = a["mask_BxS2_ik0"]
    r["ctx_mask"] = f(np.concatenate([M, np.zeros((B, SP2 - S2), M.dtype)], 1).reshape(1, B * SP2))
    Q = lambda n: a["L1_xattn_" + n]
    for n in ("q", "k", "v"):
        r["l1x_w" + n] = f(Q("W" + n).T.reshape(8, 128, D).transpose(1, 0, 2))
    r["l1x_wo"] = f(Q("Wo").reshape(8, 128, D).transpose(1, 0, 2))
    r["l1x_bq"], r["l1x_bv"], r["l1x_bo"] = f(Q("bq").reshape(8, 128).T), f(Q("bv").reshape(8, 128).T), f(Q("bo")[:, None])
    V = lambda n: a["L2_xattn_" + n]
    r["l2x_w"] = f(np.stack([V(n + "_w").T for n in "qkv"], 1))
    r["l2x_b"] = f(np.stack([V(n + "_b") for n in "qkv"], 1))
    E = lambda n: a["L1_attn_" + n]
    r["l1d_ln"] = f(np.stack([E("ln_w"), E("ln_b")], 1))
    r["l1d_wp"] = f(np.stack([E(n).T for n in ("Wq", "Wk", "Wa", "WaR")], 1))
    r["l1d_wv"] = f(E("Wv").T)
    r["l1d_wo"] = f(E("Wo").T.reshape(8, 128, D).transpose(1, 0, 2))
    r["l1d_wbg"] = f(np.stack([E("Wb").T, E("Wg").T], 1))
    r["l1d_ab"] = f(np.stack([E("ba").reshape(8, 128).T, E("baR").reshape(8, 128).T], 1))
    r["l1d_bg"] = f(np.stack([E("bb"), E("bg")], 1))
    p128 = np.arange(128)
    head_of = 2 * np.arange(8)[None] + p128[:, None] // 64
    hot = (head_of[:, :, None] == np.arange(H)).astype(np.float32)
    r["l1d_hsum"] = f(hot)
    r["l1d_hsel"] = f(hot.transpose(2, 1, 0))
    lm = np.zeros((128, LEVELS, 64), np.int32)
    for lv in range(LEVELS):
        m = 1 << lv
        up = p128.reshape(-1, 2, m)[:, 1].reshape(-1)
        lm[:, lv] = (p128[:, None] // (2 * m) == up[None] // (2 * m)) & ((p128[:, None] // m) % 2 == 0)
    r["l1d_lmask"] = lm
    r["l1d_imask"] = np.eye(128, dtype=np.int32)
    for n in ("q", "k", "v"):
        r["L0_xattn_kernel_" + n] = f(a["L0_xattn_kernel_" + n].reshape(D, D))
    return r


def kernel(**inputs):
    import concourse.bacc as bacc
    from concourse.bass_utils import run_bass_kernel_spmd

    nc = bacc.Bacc("TRN2", target_bir_lowering=False, num_devices=1)
    arrays = laid_out({n: np.asarray(v) for n, v in inputs.items()})
    arr = {n: nc.dram_tensor("in_" + n, v.shape, mybir.dt.from_np(v.dtype), kind="ExternalInput").ap()
           for n, v in arrays.items()}
    out = nc.dram_tensor("out_xT", (D, N), F32, kind="ExternalOutput").ap()
    program(nc, arr, out)
    r = run_bass_kernel_spmd(nc, [{"in_" + n: v for n, v in arrays.items()}], core_ids=[0])
    return np.ascontiguousarray(r.results[0]["out_xT"].T).reshape(B, T, D)
```

```python
from contextlib import ExitStack

import concourse.bass as bass
import numpy as np
from concourse import mybir

PHASES = (0, 1, 2, 3, 4, 5, 6, 7, 8, 9, 10, 11)

F32 = mybir.dt.float32
BF16 = mybir.dt.bfloat16
I32 = mybir.dt.int32
ALU = mybir.AluOpType
ACT = mybir.ActivationFunctionType
AX = mybir.AxisListType
ds = bass.ds

B, T, D = 64, 32, 128
N = B * T
S2 = 257
KC, NKC = 86, 3
SP2 = KC * NKC
H = 16
CH = 512
NCH = N // CH
TB = 128 // T
NEG = -1.0e30
LN_EPS = 1e-5

CONST = {}
_at = 0
for _name, _w in (("ident", 128), ("mean", 128), ("blk8", 128), ("blk64", 128), ("meanT", 128),
                  ("blk32", 128), ("hmask", H), ("hmask4", 4), ("causal", T), ("cos", T), ("sin", T), ("iota", H),
                  ("eps", 1), ("ones", 128), ("bits", 32)):
    CONST[_name] = (_at, _w)
    _at += _w
CW = _at


def constants():
    c = np.zeros((128, CW), np.float32)

    def put(name, a):
        o, w = CONST[name]
        c[:a.shape[0], o:o + w] = a

    p = np.arange(128)
    put("ident", np.eye(128, dtype=np.float32))
    put("mean", np.full((128, 128), 1.0 / D, np.float32))
    put("blk8", (p[:, None] // 8 == p[None] // 8).astype(np.float32))
    put("blk64", (p[:, None] // 64 == p[None] // 64).astype(np.float32))
    put("blk32", (p[:, None] // T == p[None] // T).astype(np.float32))
    put("meanT", (p[:, None] // T == p[None] // T).astype(np.float32) / T)
    put("hmask", (p[:, None] // 8 == np.arange(H)[None]).astype(np.float32))
    put("hmask4", (p[:, None] % 32 // 8 == np.arange(4)[None]).astype(np.float32))
    put("causal", np.where(np.arange(T)[None] > (p % T)[:, None], NEG, 0.0).astype(np.float32))
    hd = D // H
    inv = (np.float32(1.0) / np.float32(10000.0) ** (np.arange(0, hd, 2, dtype=np.float32) / np.float32(hd)))
    t = np.arange(T, dtype=np.float32)
    cos, sin = np.zeros((128, T), np.float32), np.zeros((128, T), np.float32)
    for h in range(H):
        f = t[:, None] * (inv * np.float32(10000.0 ** (h / H)))[None]
        cos[h * hd:(h + 1) * hd] = np.repeat(np.cos(f).T, 2, 0)
        s = np.repeat(np.sin(f).T, 2, 0)
        s[0::2] *= -1
        sin[h * hd:(h + 1) * hd] = s
    put("cos", cos)
    put("sin", sin)
    put("iota", np.tile(np.arange(H, dtype=np.float32), (128, 1)))
    put("eps", np.full((128, 1), LN_EPS, np.float32))
    put("ones", np.ones((128, 128), np.float32))
    put("bits", np.tile((2.0 ** np.arange(32)).astype(np.float32), (128, 1)))
    return c


class Steps:

    def __init__(self, eng, sem, i=0, per=0, base=0):
        self.eng, self.sem, self.i, self.per, self.base, self.n = eng, sem, i, per, base, 0

    def __call__(self, ins):
        ins.then_inc(self.sem, 1)
        self.n += 1
        self.eng.wait_ge(self.sem, self.i * self.per + self.base + self.n)

    def end(self):
        assert self.per == 0 or self.n == self.per, (self.n, self.per)


class Core:

    def __init__(self, nc, ctx, arr, out):
        self.nc, self.ctx, self.arr, self.out = nc, ctx, arr, out
        self.X = self.sb("X", [128, N])
        self.XN = self.sb("XN", [128, N])
        self.c = self.sb("consts", [128, CW])
        self.ps = [ctx.enter_context(nc.psum_tensor(f"bank{k}", [128, 512], F32)) for k in range(8)]
        self.ln_calls = 0

    def sb(self, name, shape, dt=F32, ctx=None):
        return (ctx or self.ctx).enter_context(self.nc.sbuf_tensor(name, shape, dt))

    def sem(self, name):
        return self.nc.alloc_semaphore(name=name)

    def const(self, name, rows=128):
        o, w = CONST[name]
        return self.c[:rows, o:o + w]


def load_state(k):
    nc = k.nc
    state_in = k.sem("state_in")
    with nc.Block() as block:
        @block.sync
        def _(sp):
            sp.dma_start(k.X[:], k.arr["xT"]).then_inc(state_in, 16)
            sp.dma_start(k.c[:], k.arr["consts"]).then_inc(state_in, 16)
            sp.wait_ge(state_in, 32)


def store_state(k):
    nc = k.nc
    state_out = k.sem("state_out")
    with nc.Block() as block:
        @block.sync
        def _(sp):
            sp.dma_start(k.out, k.X[:]).then_inc(state_out, 16)
            sp.wait_ge(state_out, 16)


def layer_norm(k, src, dst, affine=None):
    nc, ph = k.nc, ExitStack()
    call, k.ln_calls = k.ln_calls, k.ln_calls + 1
    s = {n: k.sem(f"ln{call}_{n}") for n in ("mean", "centred", "square", "var", "std", "rstd", "diag", "spread", "done")}
    per = CH // 128
    with ph:
        sq = k.sb(f"ln_sq{call}", [128, 2, CH], ctx=ph)
        rstd = k.sb(f"ln_rstd{call}", [128, NCH * per], ctx=ph)
        block = ph.enter_context(nc.Block())
        var_ps = k.ps[NCH]

        @block.tensor
        def _(pe):
            for c in range(NCH):
                nc.tensor.matmul(k.ps[c][:], k.const("mean"), src[:, c * CH:(c + 1) * CH], start=True,
                                 stop=True).then_inc(s["mean"], 1)
            for c in range(NCH):
                pe.wait_ge(s["square"], c + 1)
                for j in range(per):
                    t = c * per + j
                    mm = nc.tensor.matmul(var_ps[:, t:t + 1], sq[:, c % 2, j * 128:(j + 1) * 128],
                                          k.const("mean")[:, :1], start=True, stop=True)
                mm.then_inc(s["var"], 1)
            for c in range(NCH):
                pe.wait_ge(s["diag"], c + 1)
                nc.tensor.matmul(k.ps[c][:], k.const("ones"), sq[:, c % 2, :], start=True,
                                 stop=True).then_inc(s["spread"], 1)

        @block.scalar
        def _(act):
            for c in range(NCH):
                if c >= 2:
                    act.wait_ge(s["var"], c - 1)
                act.wait_ge(s["centred"], c + 1)
                nc.scalar.activation(sq[:, c % 2, :], dst[:, c * CH:(c + 1) * CH], ACT.Square).then_inc(s["square"], 1)
            act.wait_ge(s["var"], NCH)
            nc.scalar.activation(rstd[:], var_ps[:, :NCH * per], ACT.Sqrt, bias=k.const("eps")).then_inc(s["std"], 1)

        @block.vector
        def _(dve):
            for c in range(NCH):
                dve.wait_ge(s["mean"], c + 1)
                nc.vector.tensor_tensor(dst[:, c * CH:(c + 1) * CH], src[:, c * CH:(c + 1) * CH], k.ps[c][:],
                                        ALU.subtract).then_inc(s["centred"], 1)
            dve.wait_ge(s["std"], 1)
            nc.vector.reciprocal(rstd[:], rstd[:]).then_inc(s["rstd"], 1)
            dve.wait_ge(s["rstd"], 1)

            def diagonals(c):
                if c >= 2:
                    dve.wait_ge(s["spread"], c - 1)
                nc.vector.tensor_tensor(sq[:, c % 2, :].rearrange("p (j t) -> p j t", j=per),
                                        k.const("ident").unsqueeze(1).to_broadcast([128, per, 128]),
                                        rstd[:, c * per:(c + 1) * per].unsqueeze(2).to_broadcast([128, per, 128]),
                                        ALU.mult).then_inc(s["diag"], 1)

            diagonals(0)
            diagonals(1)
            for c in range(NCH):
                d = dst[:, c * CH:(c + 1) * CH]
                dve.wait_ge(s["spread"], c + 1)
                nc.vector.tensor_tensor(d, d, k.ps[c][:], ALU.mult).then_inc(s["done"], 1)
                if c + 2 < NCH:
                    diagonals(c + 2)
                if affine is not None:
                    dve.wait_ge(s["done"], c + 1)
                    nc.vector.tensor_scalar(d, d, affine[0], affine[1], ALU.mult, ALU.add)


def l0_xattn(k):
    nc, ph = k.nc, ExitStack()
    s = {n: k.sem("l0x_" + n) for n in ("w", "q_mm", "q", "kp_mm", "kp", "v_mm", "v0", "v", "sc_mm", "sc",
                                        "o_mm", "o")}
    ctx_in = [k.sem(f"l0x_ctx{j}") for j in range(4)]
    with ph:
        wq, wk, wv = (k.sb("l0x_" + n, [128, D], ctx=ph) for n in ("wq", "wk", "wv"))
        bcol = k.sb("l0x_bcol", [128, 2], ctx=ph)
        bv = k.sb("l0x_bv", [KC, NKC, D], ctx=ph)
        mask = k.sb("l0x_mask", [KC, NKC, T], ctx=ph)
        q = k.sb("l0x_q", [128, N], ctx=ph)
        ctxT = k.sb("l0x_ctxT", [128, 4, SP2], ctx=ph)
        kp = k.sb("l0x_kp", [128, 4, SP2], ctx=ph)
        v = k.sb("l0x_v", [KC, 4, NKC, D], ctx=ph)
        sc = k.sb("l0x_sc", [KC, 4, NKC, T], ctx=ph)
        qb = k.sb("l0x_qb", [128, 4 * T], ctx=ph)
        kp_ps, v_ps, sc_ps, o_ps = k.ps[0:2], k.ps[2:4], k.ps[4:6], k.ps[6:8]
        block = ph.enter_context(nc.Block())

        @block.sync
        def _(sp):
            for dst, name in ((wq[:], "L0_xattn_kernel_q"), (wk[:], "L0_xattn_kernel_k"), (wv[:], "L0_xattn_kernel_v"),
                              (bcol[:], "l0x_bcol"), (bv[:], "l0x_bv"),
                              (mask[:], "l0x_mask")):
                sp.dma_start(dst, k.arr[name]).then_inc(s["w"], 16)
            for j in range(4):
                sp.dma_start(ctxT[:, j, :], k.arr["ctxT"][:, j * SP2:(j + 1) * SP2]).then_inc(ctx_in[j], 16)
            with sp.Fori(1, B // 4) as i:
                for j in range(4):
                    sp.wait_ge(s["v_mm"], i * 4 + (j - 3))
                    sp.dma_start(ctxT[:, j, :], k.arr["ctxT"][:, ds(i * (4 * SP2) + j * SP2, SP2)]
                                 ).then_inc(ctx_in[j], 16)

        @block.tensor
        def _(pe):
            pe.wait_ge(s["w"], 6 * 16)
            for c in range(NCH):
                if c >= 2:
                    pe.wait_ge(s["q"], c - 1)
                nc.tensor.matmul(kp_ps[c % 2][:], wq[:], k.XN[:, c * CH:(c + 1) * CH], start=True,
                                 stop=True).then_inc(s["q_mm"], 1)
            pe.wait_ge(s["q"], NCH)
            with pe.Fori(0, B // 4) as i:
                for j in range(4):
                    pe.wait_ge(ctx_in[j], i * 16 + 16)
                    pe.wait_ge(s["kp"], i * 4 + (j + 1))
                    nc.tensor.matmul(kp_ps[j % 2][:, :SP2], wk[:], ctxT[:, j, :], start=True,
                                     stop=True).then_inc(s["kp_mm"], 1)
                    pe.wait_ge(s["v"], i * 4 + (j + 1))
                    for c in range(NKC):
                        o = v_ps[j % 2][:KC, c * D:(c + 1) * D]
                        mm = nc.tensor.matmul(o, ctxT[:, j, c * KC:(c + 1) * KC], wv[:], start=True, stop=True)
                    mm.then_inc(s["v_mm"], 1)
                for j in range(4):
                    pe.wait_ge(s["kp"], i * 4 + (j + 3))
                    if j == 0:
                        pe.wait_ge(s["q"], i + (NCH + 1))
                    pe.wait_ge(s["sc"], i * 4 + (j + 1))
                    for c in range(NKC):
                        mm = nc.tensor.matmul(sc_ps[j % 2][:KC, c * T:(c + 1) * T], kp[:, j, c * KC:(c + 1) * KC],
                                              qb[:, j * T:(j + 1) * T], start=True, stop=True)
                    mm.then_inc(s["sc_mm"], 1)
                for j in range(4):
                    pe.wait_ge(s["v"], i * 4 + (j + 3))
                    pe.wait_ge(s["sc"], i * 4 + (j + 3))
                    if j == 0:
                        pe.wait_ge(s["o"], i + 1)
                    for c in range(NKC):
                        n = min(KC, S2 - c * KC)
                        mm = nc.tensor.matmul(o_ps[0][:, j * T:(j + 1) * T], v[:n, j, c, :], sc[:n, j, c, :],
                                              start=(c == 0), stop=(c == NKC - 1))
                mm.then_inc(s["o_mm"], 1)

        @block.scalar
        def _(act):
            act.wait_ge(s["w"], 6 * 16)
            for c in range(NCH):
                act.wait_ge(s["q_mm"], c + 1)
                nc.scalar.activation(q[:, c * CH:(c + 1) * CH], kp_ps[c % 2][:], ACT.Relu,
                                     bias=bcol[:, 0:1]).then_inc(s["q"], 1)
            act.wait_ge(s["q"], NCH)
            act.sem_inc(s["kp"], 2)
            with act.Fori(0, B // 4) as i:
                act.wait_ge(s["o"], i + 1)
                nc.scalar.mul(qb[:], q[:, ds(i * (4 * T), 4 * T)], float(1.0 / np.sqrt(np.float32(D)))
                              ).then_inc(s["q"], 1)
                for j in range(4):
                    act.wait_ge(s["kp_mm"], i * 4 + (j + 1))
                    nc.scalar.activation(kp[:, j, :], kp_ps[j % 2][:, :SP2], ACT.Relu,
                                         bias=bcol[:, 1:2]).then_inc(s["kp"], 1)

        @block.vector
        def _(dve):
            dve.wait_ge(s["w"], 6 * 16)
            for n in ("v", "sc"):
                dve.sem_inc(s[n], 2)
            dve.sem_inc(s["o"], 1)
            with dve.Fori(0, B // 4) as i:
                for j in range(4):
                    dve.wait_ge(s["v_mm"], i * 4 + (j + 1))
                    vj = v[:, j].rearrange("p c d -> p (c d)")
                    nc.vector.tensor_tensor(vj, v_ps[j % 2][:KC, :NKC * D], bv[:].rearrange("p c d -> p (c d)"),
                                            ALU.add).then_inc(s["v0"], 1)
                    dve.wait_ge(s["v0"], i * 4 + (j + 1))
                    nc.vector.tensor_scalar(vj, vj, 0.0, None, ALU.max).then_inc(s["v"], 1)
                for j in range(4):
                    dve.wait_ge(s["sc_mm"], i * 4 + (j + 1))
                    w = sc[:, j].rearrange("p c d -> p (c d)")
                    nc.vector.scalar_tensor_tensor(out=w, in0=sc_ps[j % 2][:KC, :NKC * T], scalar=0.0,
                                                   in1=mask[:].rearrange("p c d -> p (c d)"), op0=ALU.max, op1=ALU.add
                                                   ).then_inc(s["sc"], 1)
                dve.wait_ge(s["o_mm"], i + 1)
                x = k.X[:, ds(i * (4 * T), 4 * T)]
                nc.vector.scalar_tensor_tensor(out=x, in0=o_ps[0][:, :4 * T], scalar=0.0, in1=x, op0=ALU.max,
                                               op1=ALU.add).then_inc(s["o"], 1)


def small_scores(k, nm, w, scores, rotary, keys_from):
    nc, ph = k.nc, ExitStack()
    s = {n: k.sem(nm + n) for n in ("proj_mm", "low_mm", "low", "qk", "spread", "spread2", "sc_mm", "sc", "kept", "steps")}
    with ph:
        turned = k.sb(nm + "turned", [128, 2, H * T], ctx=ph)
        q, kk = k.sb(nm + "q", [128, CH], ctx=ph), k.sb(nm + "k", [128, CH], ctx=ph)
        tmp = k.sb(nm + "tmp", [128, 2, CH], ctx=ph)
        low = k.sb(nm + "low", [16, 2, CH], ctx=ph)
        spread = k.sb(nm + "spread", [128, 2, TB, H, T], ctx=ph)
        sc_ps = k.ps[4:6]

        def spread_batch(eng, t, b):
            at = (t * TB + b) * T
            return eng.tensor_tensor(spread[:, t % 2, b], q[:, at:at + T].unsqueeze(1).to_broadcast([128, H, T]),
                                     k.const("hmask").unsqueeze(2).to_broadcast([128, H, T]), ALU.mult)

        block = ph.enter_context(nc.Block())

        @block.tensor
        def _(pe):
            pe.sem_inc(s["sc_mm"], 2)
            with pe.Fori(0, NCH) as c:
                srcs = (k.XN[:, ds(c * CH, CH)], keys_from[:, ds(c * CH, CH)])
                pe.wait_ge(s["qk"], c + 1)
                if rotary:
                    for n, wn in enumerate(("q", "q2", "k", "k2")):
                        mm = nc.tensor.matmul(k.ps[n][:], w[wn], srcs[n // 2], start=True, stop=True)
                    mm.then_inc(s["proj_mm"], 1)
                else:
                    for n, wn in enumerate(("Aq", "Ak")):
                        nc.tensor.matmul(k.ps[2 * n + 1][:16, :], w[wn], srcs[n], start=True,
                                         stop=True).then_inc(s["low_mm"], 1)
                    for n, wn in enumerate(("q", "k")):
                        nc.tensor.matmul(k.ps[2 * n][:], w[wn], srcs[n], start=True, stop=False)
                        pe.wait_ge(s["low"], c * 2 + (n + 1))
                        mm = nc.tensor.matmul(k.ps[2 * n][:], w["B" + wn], low[:, n, :], start=False, stop=True)
                    mm.then_inc(s["proj_mm"], 1)
                pe.wait_ge(s["qk"], c + 2)
                for t in range(4):
                    pe.wait_ge(s["spread"], c * 4 + (t + 1))
                    pe.wait_ge(s["spread2"], c * 4 + (t + 1))
                    pe.wait_ge(s["sc"], c * 4 + (t + 1))
                    for b in range(TB):
                        at = (t * TB + b) * T
                        mm = nc.tensor.matmul(sc_ps[t % 2][b * T:(b + 1) * T, :], kk[:, at:at + T],
                                              spread[:, t % 2, b].rearrange("p h q -> p (h q)"), start=True, stop=True)
                    mm.then_inc(s["sc_mm"], 1)

        @block.scalar
        def _(act):
            act.sem_inc(s["kept"], 2)
            with act.Fori(0, NCH) as c:
                if not rotary:
                    for n in range(2):
                        act.wait_ge(s["low_mm"], c * 2 + (n + 1))
                        nc.scalar.mul(low[:, n, :], k.ps[2 * n + 1][:16, :], 1.0 / 16).then_inc(s["low"], 1)
                for t in range(4):
                    act.wait_ge(s["sc"], c * 4 + (t + 3))
                    nc.scalar.copy(scores[:, ds(c * 4 + t, 1)].rearrange("p o h s -> p (o h s)"),
                                   turned[:, t % 2, :]).then_inc(s["kept"], 1)

        @block.gpsimd
        def _(pool):
            with pool.Fori(0, NCH) as c:
                pool.wait_ge(s["qk"], c + 2)
                for t in range(4):
                    pool.wait_ge(s["sc_mm"], c * 4 + (t + 1))
                    for b in range(2):
                        ins = spread_batch(nc.gpsimd, t, b)
                    ins.then_inc(s["spread"], 1)

        @block.vector
        def _(dve):
            dve.sem_inc(s["qk"], 1)
            dve.sem_inc(s["sc"], 2)
            cos, sin = (k.const(n).unsqueeze(1).to_broadcast([128, CH // T, T]) for n in ("cos", "sin"))
            v3 = lambda a: a.rearrange("p (b t) -> p b t", t=T)
            with dve.Fori(0, NCH) as c:
                step = Steps(dve, s["steps"], c, 5 if rotary else 1)
                dve.wait_ge(s["proj_mm"], c + 1)
                if rotary:
                    for n, dst in enumerate((q, kk)):
                        step(nc.vector.tensor_tensor(v3(dst[:]), v3(k.ps[2 * n][:]), cos, ALU.mult))
                        step(nc.vector.tensor_tensor(v3(tmp[:, n]), v3(k.ps[2 * n + 1][:]), sin, ALU.mult))
                        ins = nc.vector.tensor_tensor(dst[:], dst[:], tmp[:, n], ALU.add)
                        if n == 0:
                            step(ins)
                    ins.then_inc(s["qk"], 1)
                else:
                    step(nc.vector.tensor_scalar(q[:], k.ps[0][:], w["bq"], None, ALU.add))
                    nc.vector.tensor_scalar(kk[:], k.ps[2][:], w["bk"], None, ALU.add).then_inc(s["qk"], 1)
                step.end()
                dve.wait_ge(s["qk"], c + 2)

                def spread_tile(t):
                    dve.wait_ge(s["sc_mm"], c * 4 + (t + 1))
                    for b in range(2, TB):
                        ins = spread_batch(nc.vector, t, b)
                    ins.then_inc(s["spread2"], 1)

                spread_tile(0)
                spread_tile(1)
                for t in range(4):
                    if t >= 1 and t + 1 < 4:
                        spread_tile(t + 1)
                    dve.wait_ge(s["sc_mm"], c * 4 + (t + 3))
                    dve.wait_ge(s["kept"], c * 4 + (t + 1))
                    nc.vector.transpose(turned[:, t % 2, :], sc_ps[t % 2][:]).then_inc(s["sc"], 1)


def small_values(k, nm, w, attT, values_from, lora):
    nc, ph = k.nc, ExitStack()
    s = {n: k.sem(nm + n) for n in ("stage", "v_mm", "v", "low_mm", "low", "tile", "u_mm", "own", "o", "low2_mm", "low2",
                                    "out_mm", "x")}
    with ph:
        src = k.sb(nm + "src", [128, CH], ctx=ph)
        at = k.sb(nm + "at", [128, 4, H * T], ctx=ph)
        v = k.sb(nm + "v", [128, 4, D], ctx=ph)
        own = k.sb(nm + "own", [128, 2, TB, 4, T], ctx=ph)
        o = k.sb(nm + "o", [128, CH], ctx=ph)
        low = k.sb(nm + "vlow", [16, 2, CH], ctx=ph)
        v_ps, u_ps, low_ps, out_ps = k.ps[4], k.ps[0:4], k.ps[5], k.ps[6]
        block = ph.enter_context(nc.Block())

        @block.scalar
        def _(act):
            act.sem_inc(s["low2"], 1)
            with act.Fori(0, NCH) as c:
                act.wait_ge(s["x"], c + 1)
                nc.scalar.copy(src[:], values_from[:, ds(c * CH, CH)]).then_inc(s["stage"], 1)
                nc.scalar.copy(at[:].rearrange("p t c -> p (t c)"),
                               attT[:, ds(c * 4, 4)].rearrange("p t h q -> p (t h q)")).then_inc(s["stage"], 1)
                if lora:
                    act.wait_ge(s["low_mm"], c + 1)
                    nc.scalar.mul(low[:, 0, :], low_ps[:16, :], 1.0 / 16).then_inc(s["low"], 1)
                act.wait_ge(s["v_mm"], c + 1)
                nc.scalar.copy(v[:].rearrange("p t d -> p (t d)"), v_ps[:]).then_inc(s["v"], 1)
                if lora:
                    act.wait_ge(s["low2_mm"], c + 1)
                    nc.scalar.mul(low[:, 1, :], low_ps[:16, :], 1.0 / 16).then_inc(s["low2"], 1)

        @block.tensor
        def _(pe):
            with pe.Fori(0, NCH) as c:
                pe.wait_ge(s["stage"], c * 2 + 2)
                if lora:
                    nc.tensor.matmul(low_ps[:16, :], w["Ak"], src[:], start=True, stop=True).then_inc(s["low_mm"], 1)
                    pe.wait_ge(s["low"], c + 1)
                for t in range(4):
                    tile = src[:, t * 128:(t + 1) * 128]
                    o_ap = v_ps[:, t * D:(t + 1) * D]
                    mm = nc.tensor.matmul(o_ap, tile, w["v"], start=True, stop=not lora)
                    if lora:
                        nc.tensor.matmul(o_ap, low[:, 0, t * 128:(t + 1) * 128], w["Bv"], start=False, stop=False)
                        mm = nc.tensor.matmul(o_ap, k.const("ones", 1), w["bv"], start=False, stop=True)
                mm.then_inc(s["v_mm"], 1)
                pe.wait_ge(s["v"], c + 1)
                for t in range(4):
                    pe.wait_ge(s["own"], c * 16 + (t * TB + TB))
                    pe.sem_inc(s["tile"], 1)
                    for g in range(4):
                        for b in range(TB):
                            mm = nc.tensor.matmul(u_ps[b][32 * g:32 * g + 32, :128],
                                                  v[b * T:(b + 1) * T, t, 32 * g:32 * g + 32],
                                                  at[b * T:(b + 1) * T, t, 128 * g:128 * g + 128], start=True, stop=True)
                    mm.then_inc(s["u_mm"], 1)
                pe.wait_ge(s["o"], c * 4 + 4)
                if lora:
                    nc.tensor.matmul(low_ps[:16, :], w["Ap"], o[:], start=True, stop=True).then_inc(s["low2_mm"], 1)
                mm = nc.tensor.matmul(out_ps[:], w["p"], o[:], start=True, stop=not lora)
                if lora:
                    pe.wait_ge(s["low2"], c + 2)
                    mm = nc.tensor.matmul(out_ps[:], w["Bp"], low[:, 1, :], start=False, stop=True)
                mm.then_inc(s["out_mm"], 1)

        @block.vector
        def _(dve):
            dve.sem_inc(s["own"], 4)
            dve.sem_inc(s["x"], 1)
            with dve.Fori(0, NCH) as c:
                for t in range(4):
                    dve.wait_ge(s["u_mm"], c * 4 + (t + 1))
                    for b in range(TB):
                        nc.vector.tensor_tensor(own[:, t % 2, b], u_ps[b][:, :128].rearrange("p (h q) -> p h q", h=4),
                                                k.const("hmask4").unsqueeze(2).to_broadcast([128, 4, T]),
                                                ALU.mult).then_inc(s["own"], 1)
                    dve.wait_ge(s["own"], c * 16 + (t * TB + 2 * TB))
                    nc.vector.tensor_reduce(o[:, t * 128:(t + 1) * 128].rearrange("p (b q) -> p b q", b=TB),
                                            own[:, t % 2].rearrange("p b h q -> p b q h"), AX.X, ALU.add
                                            ).then_inc(s["o"], 1)
                dve.wait_ge(s["out_mm"], c + 1)
                x = k.X[:, ds(c * CH, CH)]
                if lora:
                    nc.vector.scalar_tensor_tensor(out=x, in0=out_ps[:], scalar=w["bp"], in1=x, op0=ALU.add,
                                                   op1=ALU.add).then_inc(s["x"], 1)
                else:
                    nc.vector.tensor_tensor(x, out_ps[:], x, ALU.add).then_inc(s["x"], 1)


def load(k, nm, pairs):
    sem = k.sem(nm + "w")
    with k.nc.Block() as block:
        @block.sync
        def _(sp):
            for dst, name in pairs:
                sp.dma_start(dst, k.arr[name]).then_inc(sem, 16)
            sp.wait_ge(sem, 16 * len(pairs))


def l0_attn(k):
    nc, ph = k.nc, ExitStack()
    s = {n: k.sem("l0a_" + n) for n in ("bias_mm", "shifted", "exp", "att", "turned", "kept", "steps")}
    with ph:
        wall = k.sb("l0a_w", [128, 5, D], ctx=ph)
        wproj = k.sb("l0a_wp", [128, D], ctx=ph)
        cw = k.sb("l0a_cw", [128, H], ctx=ph)
        scores = k.sb("l0a_scores", [128, N // 128, H, T], ctx=ph)
        attT = k.sb("l0a_attT", [128, N // 128, H, T], ctx=ph)
        load(k, "l0a_", ((wall[:], "l0a_w"), (wproj[:], "L0_attn_Wproj"), (cw[:], "l0a_cw")))
        w = {n: wall[:, j, :] for j, n in enumerate(("q", "q2", "k", "k2", "v"))}
        w["p"] = wproj[:]
        small_scores(k, "l0as_", w, scores, True, k.XN)
        with ExitStack() as st:
            NT = N // 128
            a, att = k.sb("l0a_a", [128, NT, T], ctx=st), k.sb("l0a_att", [128, NT, T], ctx=st)
            turned = k.sb("l0a_turned", [128, NT, T], ctx=st)
            mx, rs = k.sb("l0a_mx", [128, NT], ctx=st), k.sb("l0a_rs", [128, NT], ctx=st)
            bc = lambda m: m[:].unsqueeze(2).to_broadcast([128, NT, T])
            bias_ps = k.ps[0][:].rearrange("p (n s) -> p n s", s=T)
            block = st.enter_context(nc.Block())

            @block.tensor
            def _(pe):
                with pe.Fori(0, H) as h:
                    pe.wait_ge(s["att"], h + 1)
                    nc.tensor.matmul(k.ps[0][:], k.const("meanT"), att[:].rearrange("p n s -> p (n s)"), start=True,
                                     stop=True).then_inc(s["bias_mm"], 1)

            @block.scalar
            def _(act):
                with act.Fori(0, H) as h:
                    act.wait_ge(s["shifted"], h + 1)
                    nc.scalar.activation(a[:], a[:], ACT.Exp).then_inc(s["exp"], 1)

            @block.gpsimd
            def _(pool):
                pool.sem_inc(s["kept"], 1)
                with pool.Fori(0, H) as h:
                    pool.wait_ge(s["turned"], h + 1)
                    nc.gpsimd.tensor_copy(attT[:, :, ds(h, 1), :].rearrange("p n o s -> p n (o s)"),
                                          turned[:]).then_inc(s["kept"], 1)

            @block.vector
            def _(dve):
                nc.vector.memset(att[:], 0.0).then_inc(s["att"], 1)
                with dve.Fori(0, H) as h:
                    step = Steps(dve, s["steps"], h, 5)
                    dve.wait_ge(s["bias_mm"], h + 1)
                    step(nc.vector.scalar_tensor_tensor(
                        out=a[:], in0=bias_ps, scalar=cw[:, ds(h, 1)],
                        in1=k.const("causal").unsqueeze(1).to_broadcast([128, NT, T]), op0=ALU.mult, op1=ALU.add))
                    step(nc.vector.scalar_tensor_tensor(
                        out=a[:], in0=scores[:, :, ds(h, 1), :].rearrange("p n o s -> p n (o s)"),
                        scalar=float((D // H) ** -0.5), in1=a[:], op0=ALU.mult, op1=ALU.add))
                    step(nc.vector.tensor_reduce(mx[:], a[:], AX.X, ALU.max))
                    nc.vector.tensor_tensor(a[:], a[:], bc(mx), ALU.subtract).then_inc(s["shifted"], 1)
                    dve.wait_ge(s["exp"], h + 1)
                    step(nc.vector.tensor_reduce(rs[:], a[:], AX.X, ALU.add))
                    step(nc.vector.reciprocal(rs[:], rs[:]))
                    nc.vector.tensor_tensor(att[:], a[:], bc(rs), ALU.mult).then_inc(s["att"], 1)
                    dve.wait_ge(s["att"], h + 2)
                    dve.wait_ge(s["kept"], h + 1)
                    nc.vector.transpose(turned[:], att[:]).then_inc(s["turned"], 1)
                    step.end()
        small_values(k, "l0av_", w, attT, k.XN, False)


def l3_xattn(k):
    nc, ph = k.nc, ExitStack()
    s = {n: k.sem("l3x_" + n) for n in ("shifted", "exp", "att", "turned", "kept", "steps")}
    with ph:
        wall = k.sb("l3x_w", [128, 4, D], ctx=ph)
        wa = k.sb("l3x_A", [128, 3, 16], ctx=ph)
        wb = k.sb("l3x_B", [16, 4, D], ctx=ph)
        bcol = k.sb("l3x_bcol", [128, 3], ctx=ph)
        bv = k.sb("l3x_bv", [1, D], ctx=ph)
        head = k.sb("l3x_ctx", [128, N], ctx=ph)
        scores = k.sb("l3x_scores", [128, N // 128, H, T], ctx=ph)
        attT = k.sb("l3x_attT", [128, N // 128, H, T], ctx=ph)
        load(k, "l3x_", ((wall[:], "l3x_w"), (wa[:], "l3x_A"), (wb[:], "l3x_B"), (bcol[:], "l3x_bcol"),
                         (bv[:], "l3x_bv"), (head[:], "ctx_head")))
        w = {n: wall[:, j, :] for j, n in enumerate(("q", "k", "v", "p"))}
        w.update({n: wa[:, j, :] for j, n in enumerate(("Aq", "Ak", "Ap"))})
        w.update({n: wb[:, j, :] for j, n in enumerate(("Bq", "Bk", "Bv", "Bp"))})
        w.update(bq=bcol[:, 0:1], bk=bcol[:, 1:2], bp=bcol[:, 2:3], bv=bv[:])
        small_scores(k, "l3xs_", w, scores, False, head)
        with ExitStack() as st:
            a, mx, rs = (k.sb("l3x_" + n, z, ctx=st) for n, z in (("a", [128, 2, H, T]), ("mx", [128, 2, H]),
                                                                  ("rs", [128, 2, H])))
            turned = k.sb("l3x_turned", [128, 2, H * T], ctx=st)
            bc = lambda m: m.unsqueeze(2).to_broadcast([128, H, T])
            block = st.enter_context(nc.Block())

            @block.scalar
            def _(act):
                with act.Fori(0, N // 256) as i:
                    for j in range(2):
                        act.wait_ge(s["shifted"], i * 2 + (j + 1))
                        nc.scalar.activation(a[:, j], a[:, j], ACT.Exp).then_inc(s["exp"], 1)

            @block.gpsimd
            def _(pool):
                pool.sem_inc(s["kept"], 2)
                with pool.Fori(0, N // 256) as i:
                    for j in range(2):
                        pool.wait_ge(s["turned"], i * 2 + (j + 1))
                        nc.gpsimd.tensor_copy(attT[:, ds(i * 2 + j, 1)].rearrange("p o h s -> p (o h s)"),
                                              turned[:, j]).then_inc(s["kept"], 1)

            @block.vector
            def _(dve):
                with dve.Fori(0, N // 256) as i:
                    step = Steps(dve, s["steps"], i, 8)
                    for j in range(2):
                        step(nc.vector.scalar_tensor_tensor(
                            out=a[:, j], in0=scores[:, ds(i * 2 + j, 1)].rearrange("p o h s -> p (o h) s"),
                            scalar=float((D // H) ** -0.5),
                            in1=k.const("causal").unsqueeze(1).to_broadcast([128, H, T]), op0=ALU.mult, op1=ALU.add))
                        step(nc.vector.tensor_reduce(mx[:, j], a[:, j], AX.X, ALU.max))
                        nc.vector.tensor_tensor(a[:, j], a[:, j], bc(mx[:, j]), ALU.subtract).then_inc(s["shifted"], 1)
                    for j in range(2):
                        dve.wait_ge(s["exp"], i * 2 + (j + 1))
                        step(nc.vector.tensor_reduce(rs[:, j], a[:, j], AX.X, ALU.add))
                        step(nc.vector.reciprocal(rs[:, j], rs[:, j]))
                        nc.vector.tensor_tensor(a[:, j], a[:, j], bc(rs[:, j]), ALU.mult).then_inc(s["att"], 1)
                        dve.wait_ge(s["att"], i * 2 + (j + 1))
                        dve.wait_ge(s["kept"], i * 2 + (j + 1))
                        nc.vector.transpose(turned[:, j], a[:, j].rearrange("p h s -> p (h s)")).then_inc(s["turned"], 1)
                    step.end()
        small_values(k, "l3xv_", w, attT, head, True)


NT = N // 128


def gate_logits(k, nm, w, e):
    nc, mm = k.nc, k.sem(nm + "logits")
    with nc.Block() as block:
        @block.tensor
        def _(pe):
            for t in range(NT):
                ins = nc.tensor.matmul(k.ps[0][:, t * e:(t + 1) * e], k.XN[:, t * 128:(t + 1) * 128], w, start=True,
                                       stop=True)
            ins.then_inc(mm, 1)
            pe.wait_ge(mm, 1)
    return k.ps[0][:, :NT * e].rearrange("p (t e) -> p t e", e=e)


def rows_of(k, nm, cols, rows, e):
    nc, mm, done = k.nc, k.sem(nm + "turn_mm"), k.sem(nm + "turn")
    with nc.Block() as block:
        @block.tensor
        def _(pe):
            for t in range(NT):
                ins = nc.tensor.transpose(k.ps[1 + t // 4][:e, (t % 4) * 128:(t % 4 + 1) * 128], cols[:, t, :],
                                          k.const("ident"))
                if t % 4 == 3:
                    ins.then_inc(mm, 1)

        @block.scalar
        def _(act):
            for c in range(NCH):
                act.wait_ge(mm, c + 1)
                nc.scalar.copy(rows[:e, c * CH:(c + 1) * CH], k.ps[1 + c][:e, :]).then_inc(done, 1)
            act.wait_ge(done, NCH)


def first_max(nc, step, vals, mx, hot, tmp, iota, e):
    bc = lambda m: m.unsqueeze(2).to_broadcast([128, NT, e])
    step(nc.vector.tensor_reduce(mx, vals, AX.X, ALU.max))
    step(nc.vector.tensor_tensor(tmp, vals, bc(mx), ALU.is_lt))
    step(nc.vector.scalar_tensor_tensor(out=tmp, in0=tmp, scalar=float(2 * e), in1=iota, op0=ALU.mult, op1=ALU.add))
    step(nc.vector.tensor_reduce(mx, tmp, AX.X, ALU.min))
    step(nc.vector.tensor_tensor(hot, iota, bc(mx), ALU.is_equal))


def experts(k, nm, e_range, f4, gated, coefT, src, wname, gain):
    nc, ph = k.nc, ExitStack()
    e0, ne = e_range
    lanes = min(2, ne)
    nw = 2 if gated else 1
    wc = nw * f4 * 128 + f4 * 128 + (0 if gated else f4 + 1 + 2)
    erows = coefT.shape[0]
    nb = 2 if gated else 4
    s = {n: k.sem(nm + n) for n in ("in", "hid_mm", "g", "h", "y_mm", "cf_mm", "cf", "t", "x")}
    w_in = [k.sem(nm + f"w_in{j}") for j in range(lanes)]
    with ph:
        w = k.sb(nm + "w", [128, lanes, wc], ctx=ph)
        sel = k.sb(nm + "sel", [erows, lanes, 128], ctx=ph)
        xe = k.sb(nm + "xe", [128, 2, CH], ctx=ph) if gain else None
        gl = k.sb(nm + "gl", [128, 2, CH], ctx=ph) if gated else None
        h = k.sb(nm + "h", [128, 2, f4, CH], ctx=ph)
        cf = k.sb(nm + "cf", [128, 2, CH], ctx=ph)
        t_sb = k.sb(nm + "t", [128, 2, CH], ctx=ph)
        block = ph.enter_context(nc.Block())
        y_ps, cf_ps = k.ps[4:6], k.ps[6:8]
        o2 = nw * f4 * 128
        ob = o2 + f4 * 128
        order = [("h", 0), ("h", 1), ("y", 0), ("h", 2), ("y", 1), ("h", 3), ("y", 2), ("y", 3)]

        def item(i, l, c):
            return i * (lanes * NCH) + (l * NCH + c)

        @block.sync
        def _(sp):
            def fetch(l, e):
                sp.dma_start(w[:, l, :], k.arr[wname][ds(e, 1)].rearrange("o p c -> (o p) c")).then_inc(w_in[l], 16)
                sp.dma_start(sel[:, l, :], k.arr["sel"][:erows, ds((e + e0) * 128, 128)]).then_inc(w_in[l], 16)
            for l in range(lanes):
                fetch(l, l)
            if ne > lanes:
                with sp.Fori(1, ne // lanes) as i:
                    for l in range(lanes):
                        sp.wait_ge(s["x"], i * (2 * NCH) + (l - 1) * NCH)
                        fetch(l, i * lanes + l)

        @block.tensor
        def _(pe):
            pe.sem_inc(s["hid_mm"], 2 * f4)
            pe.sem_inc(s["y_mm"], 2)
            with pe.Fori(0, ne // lanes) as i:
                for l in range(lanes):
                    pe.wait_ge(w_in[l], i * 32 + 32)
                    for what, c in order:
                        m = item(i, l, c)
                        if what == "h":
                            if gain:
                                pe.wait_ge(s["in"], m + 1)
                            rhs = xe[:, c % 2, :] if gain else src[:, c * CH:(c + 1) * CH]
                            for f in range(f4):
                                pe.wait_ge(s["h"], m * f4 + (f + 1))
                                for n in range(nw):
                                    bank = k.ps[((c * f4 + f) % nb) * nw + n]
                                    mm = nc.tensor.matmul(bank[:], w[:, l, (n * f4 + f) * 128:(n * f4 + f + 1) * 128],
                                                          rhs, start=True, stop=True)
                                mm.then_inc(s["hid_mm"], 1)
                        else:
                            pe.wait_ge(s["cf"], m + 1)
                            nc.tensor.matmul(cf_ps[c % 2][:], sel[:, l, :], coefT[:, c * CH:(c + 1) * CH], start=True,
                                             stop=True).then_inc(s["cf_mm"], 1)
                            pe.wait_ge(s["h"], m * f4 + (f4 + nb))
                            pe.wait_ge(s["t"], m + 1)
                            for f in range(f4):
                                mm = nc.tensor.matmul(y_ps[c % 2][:], w[:, l, o2 + f * 128:o2 + (f + 1) * 128],
                                                      h[:, c % 2, f, :], start=(f == 0), stop=(f == f4 - 1))
                            mm.then_inc(s["y_mm"], 1)

        @block.scalar
        def _(act):
            act.sem_inc(s["cf"], 2)
            if not gated:
                act.sem_inc(s["h"], nb)
            with act.Fori(0, ne // lanes) as i:
                for l in range(lanes):
                    if not gated:
                        act.wait_ge(w_in[l], i * 32 + 32)
                    for what, c in order:
                        m = item(i, l, c)
                        if what == "h":
                            for f in range(f4):
                                act.wait_ge(s["hid_mm"], m * f4 + (f + 1 + 2 * f4))
                                if gated:
                                    act.wait_ge(s["h"], m * f4 + (f + 1))
                                    nc.scalar.activation(gl[:, (c * f4 + f) % 2, :], k.ps[((c * f4 + f) % nb) * 2][:],
                                                         ACT.Gelu).then_inc(s["g"], 1)
                                else:
                                    if f == 0:
                                        act.wait_ge(s["y_mm"], m + 1)
                                    nc.scalar.activation(h[:, c % 2, f, :], k.ps[(c * f4 + f) % nb][:], ACT.Relu,
                                                         bias=w[:, l, ob + f:ob + f + 1]).then_inc(s["h"], 1)
                        else:
                            act.wait_ge(s["cf_mm"], m + 1)
                            act.wait_ge(s["t"], m + 1)
                            nc.scalar.copy(cf[:, c % 2, :], cf_ps[c % 2][:]).then_inc(s["cf"], 1)

        @block.vector
        def _(dve):
            dve.sem_inc(s["t"], 2)
            if gated:
                dve.sem_inc(s["h"], nb)
            with dve.Fori(0, ne // lanes) as i:
                for l in range(lanes):
                    if not gated:
                        dve.wait_ge(w_in[l], i * 32 + 32)
                    for what, c in order:
                        m = item(i, l, c)
                        if what == "h":
                            if gain:
                                dve.wait_ge(s["hid_mm"], m * f4 + f4)
                                nc.vector.tensor_scalar(xe[:, c % 2, :], src[:, c * CH:(c + 1) * CH],
                                                        w[:, l, ob + f4 + 1:ob + f4 + 2], w[:, l, ob + f4 + 2:ob + f4 + 3],
                                                        ALU.mult, ALU.add).then_inc(s["in"], 1)
                            if gated:
                                dve.wait_ge(s["y_mm"], m + 1)
                                for f in range(f4):
                                    dve.wait_ge(s["g"], m * f4 + (f + 1))
                                    nc.vector.tensor_tensor(h[:, c % 2, f, :], gl[:, (c * f4 + f) % 2, :],
                                                            k.ps[((c * f4 + f) % nb) * 2 + 1][:],
                                                            ALU.mult).then_inc(s["h"], 1)
                        else:
                            dve.wait_ge(s["y_mm"], m + 3)
                            dve.wait_ge(s["cf"], m + 3)
                            if gated:
                                nc.vector.tensor_tensor(t_sb[:, c % 2, :], y_ps[c % 2][:], cf[:, c % 2, :],
                                                        ALU.mult).then_inc(s["t"], 1)
                            else:
                                nc.vector.scalar_tensor_tensor(
                                    out=t_sb[:, c % 2, :], in0=y_ps[c % 2][:], scalar=w[:, l, ob + f4:ob + f4 + 1],
                                    in1=cf[:, c % 2, :], op0=ALU.add, op1=ALU.mult).then_inc(s["t"], 1)
                            dve.wait_ge(s["t"], m + 3)
                            x = k.X[:, c * CH:(c + 1) * CH]
                            nc.vector.tensor_tensor(x, x, t_sb[:, c % 2, :], ALU.add).then_inc(s["x"], 1)


def add_normed(k, nm):
    nc, done = k.nc, k.sem(nm + "residual")
    with nc.Block() as block:
        @block.vector
        def _(dve):
            nc.vector.tensor_tensor(k.X[:], k.X[:], k.XN[:], ALU.add).then_inc(done, 1)
            dve.wait_ge(done, 1)


def l0_ffn(k):
    nc, ph, e = k.nc, ExitStack(), 8
    s = {n: k.sem("l0f_" + n) for n in ("sig", "steps")}
    with ph:
        xn2 = k.sb("l0f_xn2", [128, N], ctx=ph)
        cen = k.sb("l0f_cen", [128, e], ctx=ph)
        coefT = k.sb("l0f_coefT", [e, N], ctx=ph)
        layer_norm(k, k.XN, xn2)
        load(k, "l0f_", ((cen[:], "l0f_cen"),))
        logits = gate_logits(k, "l0f_", cen[:], e)
        with ExitStack() as st:
            sig, hot, tmp, aff = (k.sb("l0f_" + n, [128, NT, e], ctx=st) for n in ("sig", "hot", "tmp", "aff"))
            mx = k.sb("l0f_mx", [128, NT], ctx=st)
            iota = k.const("iota")[:, :e].unsqueeze(1).to_broadcast([128, NT, e])
            with nc.Block() as block:
                @block.scalar
                def _(act):
                    act.wait_ge(s["steps"], 1)
                    nc.scalar.activation(sig[:], aff[:], ACT.Sigmoid).then_inc(s["sig"], 1)

                @block.vector
                def _(dve):
                    step = Steps(dve, s["steps"])
                    step(nc.vector.tensor_copy(aff[:], logits))
                    first_max(nc, step, aff[:], mx[:], hot[:], tmp[:], iota, e)
                    dve.wait_ge(s["sig"], 1)
                    step(nc.vector.tensor_tensor(hot[:], hot[:], sig[:], ALU.mult))
            rows_of(k, "l0f_", hot, coefT, e)
        experts(k, "l0fe_", (0, e), 4, False, coefT, xn2, "l0f_w", True)
        add_normed(k, "l0f_")


def softmax_rows(k, nm, logits, bias, p, mx, e):
    nc = k.nc
    s = {n: k.sem(nm + n) for n in ("sm_in", "sm_exp", "sm_steps")}
    bc = lambda m: m.unsqueeze(2).to_broadcast([128, NT, e])
    with nc.Block() as block:
        @block.vector
        def _(dve):
            step = Steps(dve, s["sm_steps"])
            if bias is None:
                step(nc.vector.tensor_copy(p, logits))
            else:
                step(nc.vector.tensor_tensor(p, logits, bias.unsqueeze(1).to_broadcast([128, NT, e]), ALU.add))
            step(nc.vector.tensor_reduce(mx, p, AX.X, ALU.max))
            nc.vector.tensor_tensor(p, p, bc(mx), ALU.subtract).then_inc(s["sm_in"], 1)
            dve.wait_ge(s["sm_exp"], 1)
            step(nc.vector.tensor_reduce(mx, p, AX.X, ALU.add))
            step(nc.vector.reciprocal(mx, mx))
            step(nc.vector.tensor_tensor(p, p, bc(mx), ALU.mult))

        @block.scalar
        def _(act):
            act.wait_ge(s["sm_in"], 1)
            nc.scalar.activation(p, p, ACT.Exp).then_inc(s["sm_exp"], 1)


def l2_ffn(k):
    nc, ph, e, cap = k.nc, ExitStack(), 16, N * 2 // 16
    s = {n: k.sem("l2f_" + n) for n in ("ones", "spread", "count", "sum_mm", "found", "thr", "loop", "steps")}
    with ph:
        gw = k.sb("l2f_gw", [128, e], ctx=ph)
        coefT = k.sb("l2f_coefT", [e + 1, N], ctx=ph)
        bits = k.sb("l2f_bits", [128, 32], I32, ctx=ph)
        load(k, "l2f_", ((gw[:], "l2f_gw"), (bits[:], "bits_i")))
        logits = gate_logits(k, "l2f_", gw[:], e)
        with ExitStack() as st:
            p, mx = k.sb("l2f_p", [128, NT, e + 1], ctx=st), k.sb("l2f_mx", [128, NT], ctx=st)
            with nc.Block() as block:
                @block.vector
                def _(dve):
                    nc.vector.memset(p[:], 1.0).then_inc(s["ones"], 1)
                    dve.wait_ge(s["ones"], 1)
            softmax_rows(k, "l2f_", logits, None, p[:, :, :e], mx[:], e)
            rows_of(k, "l2f_", p, coefT, e + 1)
        with ExitStack() as st:
            sc = coefT[:e, :]
            junk, eq, cum, ones = (k.sb("l2f_" + n, [e, N], ctx=st) for n in ("junk", "eq", "cum", "ones"))
            thr, cand, bit = (k.sb("l2f_" + n, [128, 1], I32, ctx=st) for n in ("thr", "cand", "bit"))
            thr_e = k.sb("l2f_thr_e", [e, 1], I32, ctx=st)
            cnt, need, part = (k.sb("l2f_" + n, [n_rows, 1], ctx=st) for n, n_rows in (("cnt", e), ("need", e), ("part", 128)))
            per = 128 // e
            spread, above = (k.sb("l2f_" + n, [128, N // per], ctx=st) for n in ("spread", "above"))
            bitf = k.const("bits")
            with nc.Block() as block:
                @block.sync
                def _(sp):
                    sp.dma_start(spread[:], sc.rearrange("e (s n) -> e s n", s=per)).then_inc(s["spread"], 16)
                    sp.wait_ge(s["found"], 1)
                    sp.dma_start(thr_e[:], thr[0:128:per, :]).then_inc(s["thr"], 16)
                    sp.wait_ge(s["thr"], 16)

                @block.tensor
                def _(pe):
                    with pe.Fori(0, 31) as r:
                        pe.wait_ge(s["count"], r + 1)
                        nc.tensor.matmul(k.ps[7][:, 0:1], k.const("blk8"), part[:], start=True, stop=True
                                         ).then_inc(s["sum_mm"], 1)

                @block.vector
                def _(dve):
                    step = Steps(dve, s["steps"])
                    step(nc.vector.memset(thr[:], 0))
                    step(nc.vector.memset(ones[:], 1.0))
                    dve.wait_ge(s["spread"], 16)
                    with dve.Fori(0, 31) as r:
                        turn = Steps(dve, s["loop"], r, 3)
                        b = r * -1 + 30
                        turn(nc.vector.tensor_tensor(cand[:], thr[:], bits[:, ds(b, 1)], ALU.bitwise_or))
                        nc.vector.tensor_scalar(above[:], spread[:], cand[:].bitcast(F32), 0.0, ALU.is_ge, ALU.add,
                                                accum_out=part[:]).then_inc(s["count"], 1)
                        dve.wait_ge(s["sum_mm"], r + 1)
                        turn(nc.vector.tensor_scalar(bit[:], k.ps[7][:, 0:1], cap - 0.5, bitf[:, ds(b, 1)], ALU.is_ge,
                                                     ALU.mult))
                        turn(nc.vector.tensor_tensor(thr[:], thr[:], bit[:], ALU.bitwise_or))
                        turn.end()
                    dve.sem_inc(s["found"], 1)
                    dve.wait_ge(s["thr"], 16)
                    t = thr_e[:].bitcast(F32)
                    step(nc.vector.tensor_scalar(junk[:], sc, t, 0.0, ALU.is_gt, ALU.add, accum_out=cnt[:]))
                    step(nc.vector.tensor_scalar(need[:], cnt[:], -1.0, float(cap), ALU.mult, ALU.add))
                    step(nc.vector.tensor_scalar(eq[:], sc, t, None, ALU.is_equal))
                    step(nc.vector.tensor_tensor_scan(cum[:], ones[:], eq[:], 0.0, ALU.mult, ALU.add))
                    step(nc.vector.scalar_tensor_tensor(out=eq[:], in0=cum[:], scalar=need[:], in1=eq[:], op0=ALU.is_le,
                                                        op1=ALU.mult))
                    step(nc.vector.tensor_tensor(junk[:], junk[:], eq[:], ALU.add))
                    step(nc.vector.tensor_tensor(sc, sc, junk[:], ALU.mult))
        experts(k, "l2fe_", (0, e), 4, True, coefT, k.XN, "l2f_w", False)
        experts(k, "l2fs_", (e, 1), 2, True, coefT, k.XN, "l2f_s", False)


def sorted_by_expert(k, coefT, top, e, xs):
    nc, ph = k.nc, ExitStack()
    s = {n: k.sem("l3s_" + n) for n in ("bc_mm", "bc", "steps", "start_mm", "rank", "pos_mm", "tok_mm", "tok", "hot",
                                        "sum_mm", "sum", "end")}
    with ph:
        cum, ones, after = (k.sb("l3s_" + n, [e, N], ctx=ph) for n in ("cum", "ones", "after"))
        start, pos = k.sb("l3s_start", [e, 2], ctx=ph), k.sb("l3s_pos", [128, NT], ctx=ph)
        place = k.sb("l3s_place", [128, N], ctx=ph)
        tri = k.sb("l3s_tri", [e, e], ctx=ph)
        tok = k.sb("l3s_tok", [128, NT, D], ctx=ph)
        hot = k.sb("l3s_hot", [128, 2, N], ctx=ph)
        load(k, "l3s_", ((place[:], "places"), (tri[:], "l3f_tri")))
        with nc.Block() as block:
            @block.tensor
            def _(pe):
                for c in range(NCH):
                    nc.tensor.matmul(k.ps[c][:], top[:], coefT[:, c * CH:(c + 1) * CH], start=True,
                                     stop=True).then_inc(s["bc_mm"], 1)
                for t in range(NT):
                    if t % 4 == 0:
                        pe.wait_ge(s["bc"], t // 4 + 1)
                    ins = nc.tensor.transpose(k.ps[t // 4][:, (t % 4) * 128:(t % 4 + 1) * 128],
                                              xs[:, t * 128:(t + 1) * 128], k.const("ident"))
                    if t % 4 == 3:
                        ins.then_inc(s["tok_mm"], 1)
                pe.wait_ge(s["rank"], 1)
                nc.tensor.matmul(k.ps[4][:e, 0:1], tri[:], cum[:, N - 1:N], start=True,
                                 stop=True).then_inc(s["start_mm"], 1)
                pe.wait_ge(s["rank"], 2)
                for t in range(NT):
                    ins = nc.tensor.matmul(k.ps[5][:, t:t + 1], cum[:, t * 128:(t + 1) * 128], k.const("ones", e)[:, 0:1],
                                           start=True, stop=True)
                ins.then_inc(s["pos_mm"], 1)
                pe.wait_ge(s["tok"], NCH)
                for t in range(NT):
                    pe.wait_ge(s["hot"], t + 1)
                    for c in range(NCH):
                        ins = nc.tensor.matmul(k.ps[c][:], tok[:, t, :], hot[:, t % 2, c * CH:(c + 1) * CH],
                                               start=(t == 0), stop=(t == NT - 1))
                    ins.then_inc(s["sum_mm"], 1)

            @block.scalar
            def _(act):
                for c in range(NCH):
                    act.wait_ge(s["tok_mm"], c + 1)
                    nc.scalar.copy(tok[:, c * 4:(c + 1) * 4, :].rearrange("p t d -> p (t d)"),
                                   k.ps[c][:]).then_inc(s["tok"], 1)
                act.wait_ge(s["sum_mm"], NT)
                for c in range(NCH):
                    nc.scalar.copy(xs[:, c * CH:(c + 1) * CH], k.ps[c][:]).then_inc(s["sum"], 1)
                act.wait_ge(s["sum"], NCH)

            @block.vector
            def _(dve):
                step = Steps(dve, s["steps"])
                for c in range(NCH):
                    dve.wait_ge(s["bc_mm"], c + 1)
                    nc.vector.tensor_tensor(xs[:, c * CH:(c + 1) * CH], k.XN[:, c * CH:(c + 1) * CH], k.ps[c][:],
                                            ALU.mult).then_inc(s["bc"], 1)
                route = coefT[:e, :]
                step(nc.vector.memset(ones[:], 1.0))
                nc.vector.tensor_tensor_scan(cum[:], ones[:], route, 0.0, ALU.mult, ALU.add).then_inc(s["rank"], 1)
                dve.wait_ge(s["start_mm"], 1)
                dve.wait_ge(s["rank"], 1)
                step(nc.vector.tensor_copy(start[:, 0:1], k.ps[4][:e, 0:1]))
                step(nc.vector.tensor_tensor(start[:, 1:2], start[:, 0:1], cum[:, N - 1:N], ALU.add))
                step(nc.vector.tensor_scalar(cum[:], cum[:], start[:, 0:1], -1.0, ALU.add, ALU.add))
                nc.vector.tensor_tensor(cum[:], cum[:], route, ALU.mult).then_inc(s["rank"], 1)
                dve.wait_ge(s["rank"], 2)
                step(nc.vector.tensor_scalar(after[:], place[:e, :], start[:, 0:1], None, ALU.is_ge))
                step(nc.vector.scalar_tensor_tensor(out=route, in0=place[:e, :], scalar=start[:, 1:2], in1=after[:],
                                                    op0=ALU.is_lt, op1=ALU.mult))
                dve.wait_ge(s["pos_mm"], 1)
                step(nc.vector.tensor_copy(pos[:], k.ps[5][:, :NT]))
                for t in range(NT):
                    if t >= 2:
                        dve.wait_ge(s["sum_mm"], t - 1)
                    nc.vector.tensor_scalar(hot[:, t % 2, :], place[:], pos[:, t:t + 1], None,
                                            ALU.is_equal).then_inc(s["hot"], 1)


def l3_ffn(k):
    nc, ph, e = k.nc, ExitStack(), 8
    s = {n: k.sem("l3f_" + n) for n in ("steps",)}
    with ph:
        gw = k.sb("l3f_gw", [128, e], ctx=ph)
        bs = k.sb("l3f_bs", [128, e], ctx=ph)
        coefT = k.sb("l3f_coefT", [e + 1, N], ctx=ph)
        top = k.sb("l3f_top", [e + 1, 128], ctx=ph)
        xs = k.sb("l3f_xs", [128, N], ctx=ph)
        load(k, "l3f_", ((gw[:], "l3f_gw"), (bs[:], "l3f_bs"), (top[:], "l3f_top")))
        logits = gate_logits(k, "l3f_", gw[:], e)
        with ExitStack() as st:
            p, tmp = (k.sb("l3f_" + n, [128, NT, e], ctx=st) for n in ("p", "tmp"))
            mx = k.sb("l3f_mx", [128, NT], ctx=st)
            hot = k.sb("l3f_hot", [128, NT, e + 1], ctx=st)
            iota = k.const("iota")[:, :e].unsqueeze(1).to_broadcast([128, NT, e])
            softmax_rows(k, "l3f_", logits, bs[:], p[:], mx[:], e)
            with nc.Block() as block:
                @block.vector
                def _(dve):
                    step = Steps(dve, s["steps"])
                    step(nc.vector.tensor_reduce(hot[:, :, e:e + 1].rearrange("p t o -> p (t o)"), p[:], AX.X, ALU.max))
                    first_max(nc, step, p[:], mx[:], hot[:, :, :e], tmp[:], iota, e)
            rows_of(k, "l3f_", hot, coefT, e + 1)
        sorted_by_expert(k, coefT, top, e, xs)
        experts(k, "l3fe_", (0, e), 1, False, coefT, xs, "l3f_w", False)


def l1_ffn(k):
    nc, ph = k.nc, ExitStack()
    magic = 1.5 * 2.0 ** 23
    s = {n: k.sem("l1f_" + n) for n in ("wq", "w_mm", "wT", "src", "tok_mm", "steps", "xq", "xqT_mm", "xqT", "out_mm",
                                        "out", "turn_mm", "x")}
    with ph:
        wt = k.sb("l1f_wt", [128, D], ctx=ph)
        bias = k.sb("l1f_bias", [128, 1], ctx=ph)
        wsc, am = k.sb("l1f_wsc", [128, 2], ctx=ph), k.sb("l1f_am", [128, 2, 4], ctx=ph)
        wtmp = k.sb("l1f_wtmp", [128, D], ctx=ph)
        wqb, wqT, identb = (k.sb("l1f_" + n, [128, D], BF16, ctx=ph) for n in ("wqb", "wqT", "identb"))
        src, tmp, y = (k.sb("l1f_" + n, [128, CH], ctx=ph) for n in ("src", "tmp", "y"))
        xq, xqT = (k.sb("l1f_" + n, [128, CH], BF16, ctx=ph) for n in ("xq", "xqT"))
        load(k, "l1f_", ((wt[:], "L1_ffn_weight"), (bias[:], "l1f_bias")))
        t3 = lambda a: a.rearrange("p (t d) -> p t d", d=128)
        bc = lambda m: m.unsqueeze(2).to_broadcast([128, 4, 128])
        xqT_ps = k.ps[1][:].bitcast(BF16)
        block = ph.enter_context(nc.Block())

        def rounded(step, out, v):
            step(nc.vector.tensor_scalar(v, v, magic, None, ALU.add))
            step(nc.vector.tensor_scalar(v, v, magic, None, ALU.subtract))
            return nc.vector.tensor_scalar(out, v, 127.0, -128.0, ALU.min, ALU.max)

        @block.vector
        def _(dve):
            step = Steps(dve, s["wq"])
            step(nc.vector.tensor_copy(identb[:], k.const("ident")))
            step(nc.vector.tensor_reduce(wsc[:, 0:1], wt[:], AX.X, ALU.max, apply_absolute_value=True))
            step(nc.vector.tensor_scalar(wsc[:, 0:1], wsc[:, 0:1], 1e-8, 1.0 / 127.0, ALU.max, ALU.mult))
            step(nc.vector.reciprocal(wsc[:, 1:2], wsc[:, 0:1]))
            step(nc.vector.tensor_scalar(wtmp[:], wt[:], wsc[:, 1:2], None, ALU.mult))
            step(rounded(step, wqb[:], wtmp[:]))
            with dve.Fori(0, NCH) as c:
                step = Steps(dve, s["steps"], c, 7)
                dve.wait_ge(s["tok_mm"], c + 1)
                step(nc.vector.tensor_reduce(am[:, 0, :], t3(k.ps[0][:]), AX.X, ALU.max, apply_absolute_value=True))
                step(nc.vector.tensor_scalar(am[:, 0, :], am[:, 0, :], 1e-8, 1.0 / 127.0, ALU.max, ALU.mult))
                step(nc.vector.reciprocal(am[:, 1, :], am[:, 0, :]))
                step(nc.vector.tensor_tensor(t3(tmp[:]), t3(k.ps[0][:]), bc(am[:, 1, :]), ALU.mult))
                rounded(step, xq[:], tmp[:]).then_inc(s["xq"], 1)
                dve.wait_ge(s["out_mm"], c + 1)
                nc.vector.tensor_tensor(t3(y[:]), t3(k.ps[2][:]), bc(am[:, 0, :]), ALU.mult).then_inc(s["out"], 1)
                dve.wait_ge(s["turn_mm"], c + 1)
                step(nc.vector.tensor_scalar(tmp[:], k.ps[3][:], wsc[:, 0:1], bias[:], ALU.mult, ALU.add))
                x = k.X[:, ds(c * CH, CH)]
                nc.vector.tensor_tensor(x, x, tmp[:], ALU.add).then_inc(s["x"], 1)
                step.end()

        @block.tensor
        def _(pe):
            pe.wait_ge(s["wq"], 8)
            nc.tensor.transpose(xqT_ps[:, :D], wqb[:], identb[:]).then_inc(s["w_mm"], 1)
            with pe.Fori(0, NCH) as c:
                pe.wait_ge(s["src"], c + 1)
                for t in range(4):
                    ins = nc.tensor.transpose(k.ps[0][:, t * 128:(t + 1) * 128], src[:, t * 128:(t + 1) * 128],
                                              k.const("ident"))
                ins.then_inc(s["tok_mm"], 1)
                pe.wait_ge(s["xq"], c + 1)
                pe.wait_ge(s["wT"], 1)
                for t in range(4):
                    ins = nc.tensor.transpose(xqT_ps[:, t * 128:(t + 1) * 128], xq[:, t * 128:(t + 1) * 128], identb[:])
                ins.then_inc(s["xqT_mm"], 1)
                pe.wait_ge(s["xqT"], c + 1)
                for t in range(4):
                    ins = nc.tensor.matmul(k.ps[2][:, t * 128:(t + 1) * 128], xqT[:, t * 128:(t + 1) * 128], wqT[:],
                                           start=True, stop=True)
                ins.then_inc(s["out_mm"], 1)
                pe.wait_ge(s["out"], c + 1)
                for t in range(4):
                    ins = nc.tensor.transpose(k.ps[3][:, t * 128:(t + 1) * 128], y[:, t * 128:(t + 1) * 128],
                                              k.const("ident"))
                ins.then_inc(s["turn_mm"], 1)

        @block.scalar
        def _(act):
            act.wait_ge(s["w_mm"], 1)
            nc.scalar.copy(wqT[:], xqT_ps[:, :D]).then_inc(s["wT"], 1)
            act.sem_inc(s["x"], 1)
            with act.Fori(0, NCH) as c:
                act.wait_ge(s["x"], c + 1)
                nc.scalar.copy(src[:], k.XN[:, ds(c * CH, CH)]).then_inc(s["src"], 1)
                act.wait_ge(s["xqT_mm"], c + 1)
                nc.scalar.copy(xqT[:], xqT_ps[:, :CH]).then_inc(s["xqT"], 1)


def l2_attn(k):
    nc, ph, hp, w2 = k.nc, ExitStack(), H // 2, 1024
    s = {n: k.sem("l2a_" + n) for n in ("src", "v_mm", "v", "p_mm", "neg", "exp", "relu", "phi", "a_mm", "a", "y_mm", "rec",
                                        "quot", "turn_mm", "ones", "y", "o_mm", "x", "steps")}
    with ph:
        wq, wk, wv = (k.sb("l2a_" + n, [128, w2], ctx=ph) for n in ("wq", "wk", "wv"))
        wo = k.sb("l2a_wo", [128, hp, D], ctx=ph)
        bq, bk = k.sb("l2a_bq", [128, hp], ctx=ph), k.sb("l2a_bk", [128, hp], ctx=ph)
        bv, bo = k.sb("l2a_bv", [128, w2], ctx=ph), k.sb("l2a_bo", [128, 1], ctx=ph)
        src = k.sb("l2a_src", [128, CH], ctx=ph)
        v = k.sb("l2a_v", [128, 4, H, 65], ctx=ph)
        quot, rden = k.sb("l2a_quot", [128, 2, 4, 2, 64], ctx=ph), k.sb("l2a_rden", [128, 8], ctx=ph)
        neg, ex, pos, phi = (k.sb("l2a_" + n, [128, 2, 2, CH], ctx=ph) for n in ("neg", "ex", "pos", "phi"))
        a = k.sb("l2a_a", [128, 2, 2, CH], ctx=ph)
        rec, y = k.sb("l2a_rec", [128, CH], ctx=ph), k.sb("l2a_y", [128, 2, CH], ctx=ph)
        load(k, "l2a_", ((wq[:], "l2a_wq"), (wk[:], "l2a_wk"), (wv[:], "l2a_wv"), (wo[:], "l2a_wo"), (bq[:], "l2a_bq"),
                         (bk[:], "l2a_bk"), (bv[:], "l2a_bv"), (bo[:], "l2a_bo")))
        p_ps, a_ps, nd_ps, o_ps, turn_ps = k.ps[0:2], k.ps[2:4], k.ps[4:6], k.ps[6], k.ps[7]
        v_ps = k.ps[2:6]
        block = ph.enter_context(nc.Block())

        @block.tensor
        def _(pe):
            with pe.Fori(0, NCH) as c:
                pe.wait_ge(s["src"], c + 1)
                for t in range(4):
                    for n in range(2):
                        m = t * 2 + n
                        if m >= 4:
                            pe.wait_ge(s["v"], c * 8 + (m - 2))
                        nc.tensor.matmul(v_ps[m % 4][:], src[:, t * 128:(t + 1) * 128], wv[:, n * 512:(n + 1) * 512], start=True,
                                         stop=True).then_inc(s["v_mm"], 1)
                for n in range(hp + 4):
                    if n < hp:
                        pe.wait_ge(s["relu"], c * 16 + (n * 2 + 2))
                        pe.wait_ge(s["neg"], c * 16 + (n * 2 + 2))
                        nc.tensor.matmul(p_ps[0][:], wq[:, n * 128:(n + 1) * 128], src[:], start=True,
                                         stop=True).then_inc(s["p_mm"], 1)
                        nc.tensor.matmul(p_ps[1][:], wk[:, n * 128:(n + 1) * 128], src[:], start=True,
                                         stop=True).then_inc(s["p_mm"], 1)
                    m = n - 1
                    if 0 <= m < hp:
                        if m == 0:
                            pe.wait_ge(s["v"], c * 8 + 9)
                        pe.wait_ge(s["phi"], c * 16 + (m * 2 + 2))
                        pe.wait_ge(s["a"], c * 16 + (m * 2 + 2))
                        for h in range(2):
                            r = slice(h * 64, h * 64 + 64)
                            for t in range(4):
                                cols = slice(t * 128, t * 128 + 128)
                                mm = nc.tensor.matmul(a_ps[h][:, cols], phi[r, m % 2, 1, cols], phi[r, m % 2, 0, cols],
                                                      start=True, stop=True)
                        mm.then_inc(s["a_mm"], 1)
                    m = n - 2
                    if 0 <= m < hp:
                        pe.wait_ge(s["a"], c * 16 + (m * 2 + 4))
                        pe.wait_ge(s["quot"], c * 16 + (m * 2 + 2))
                        for t in range(4):
                            for h in range(2):
                                mm = nc.tensor.matmul(nd_ps[t // 2][:, (t % 2 * 2 + h) * 65:(t % 2 * 2 + h + 1) * 65],
                                                      a[:, m % 2, h, t * 128:t * 128 + 128], v[:, t, 2 * m + h, :],
                                                      start=True, stop=True)
                        mm.then_inc(s["y_mm"], 1)
                    m = n - 3
                    if 0 <= m < hp:
                        pe.wait_ge(s["quot"], c * 16 + (m * 2 + 4))
                        pe.wait_ge(s["y"], c * 8 + (m + 1))
                        for t in range(4):
                            mm = nc.tensor.transpose(turn_ps[:, t * 128:(t + 1) * 128],
                                                     quot[:, m % 2, t].rearrange("p h d -> p (h d)"), k.const("ident"))
                        mm.then_inc(s["turn_mm"], 1)
                    m = n - 4
                    if 0 <= m < hp:
                        pe.wait_ge(s["y"], c * 8 + (m + 2))
                        if m == 0:
                            pe.wait_ge(s["x"], c + 1)
                        mm = nc.tensor.matmul(o_ps[:], wo[:, m, :], y[:, m % 2, :], start=(m == 0), stop=(m == hp - 1))
                mm.then_inc(s["o_mm"], 1)

        @block.scalar
        def _(act):
            act.sem_inc(s["relu"], 2)
            with act.Fori(0, NCH) as c:
                act.wait_ge(s["x"], c + 1)
                nc.scalar.copy(src[:], k.XN[:, ds(c * CH, CH)]).then_inc(s["src"], 1)
                for n in range(hp + 3):
                    for j in range(2 if n < hp else 0):
                        m = c * 16 + (n * 2 + j)
                        act.wait_ge(s["neg"], m + 3)
                        act.wait_ge(s["a_mm"], c * 8 + (n + 1))
                        nc.scalar.activation(pos[:, n % 2, j, :], p_ps[j][:], ACT.Relu,
                                             bias=(bq, bk)[j][:, n:n + 1]).then_inc(s["relu"], 1)
                        nc.scalar.activation(ex[:, n % 2, j, :], neg[:, n % 2, j, :], ACT.Exp).then_inc(s["exp"], 1)
                    if n >= 3:
                        act.wait_ge(s["turn_mm"], c * 8 + (n - 2))
                        nc.scalar.copy(y[:, (n - 3) % 2, :], turn_ps[:]).then_inc(s["y"], 1)

        @block.gpsimd
        def _(pool):
            with pool.Fori(0, NCH) as c:
                for n in range(hp):
                    for j in range(2):
                        m = c * 16 + (n * 2 + j)
                        pool.wait_ge(s["exp"], m + 1)
                        pool.wait_ge(s["relu"], m + 3)
                        pool.wait_ge(s["a_mm"], c * 8 + (n + 1))
                        nc.gpsimd.tensor_tensor(phi[:, n % 2, j, :], pos[:, n % 2, j, :], ex[:, n % 2, j, :],
                                                ALU.add).then_inc(s["phi"], 1)

        @block.vector
        def _(dve):
            for n, z in (("v", 1), ("neg", 2), ("a", 2), ("y", 1), ("quot", 2), ("x", 1), ("a_mm", 2)):
                dve.sem_inc(s[n], z)
            nc.vector.memset(v[:, :, :, 64:65], 1.0).then_inc(s["ones"], 1)
            dve.wait_ge(s["ones"], 1)
            blk = k.const("blk32").unsqueeze(1).to_broadcast([128, 4, 128])
            with dve.Fori(0, NCH) as c:
                step = Steps(dve, s["steps"], c, 2 * hp + 1)
                for t in range(4):
                    for n in range(2):
                        dve.wait_ge(s["v_mm"], c * 8 + (t * 2 + n + 1))
                        heads = lambda x: x.rearrange("p (h d) -> p h d", d=64)
                        nc.vector.tensor_tensor(v[:, t, 8 * n:8 * n + 8, :64], heads(v_ps[(t * 2 + n) % 4][:]),
                                                heads(bv[:, n * 512:(n + 1) * 512]), ALU.add).then_inc(s["v"], 1)
                for n in range(hp + 2):
                    if n < hp:
                        for j in range(2):
                            dve.wait_ge(s["p_mm"], c * 16 + (n * 2 + j + 1))
                            if n >= 2:
                                dve.wait_ge(s["exp"], c * 16 + ((n - 2) * 2 + j + 1))
                            nc.vector.tensor_scalar(neg[:, n % 2, j, :], p_ps[j][:], (bq, bk)[j][:, n:n + 1], 0.0, ALU.add,
                                                    ALU.min).then_inc(s["neg"], 1)
                    m = n - 1
                    if 0 <= m < hp:
                        dve.wait_ge(s["a_mm"], c * 8 + (m + 3))
                        for h in range(2):
                            nc.vector.tensor_tensor(a[:, m % 2, h, :].rearrange("p (t l) -> p t l", t=4),
                                                    a_ps[h][:].rearrange("p (t l) -> p t l", t=4), blk,
                                                    ALU.mult).then_inc(s["a"], 1)
                    m = n - 2
                    if 0 <= m < hp:
                        dve.wait_ge(s["y_mm"], c * 8 + (m + 1))
                        nd = [b[:, :260].rearrange("p (x d) -> p x d", d=65) for b in nd_ps]
                        for g in range(2):
                            step(nc.vector.tensor_scalar(rden[:, 4 * g:4 * g + 4], nd[g][:, :, 64], 1e-6, None, ALU.add))
                        nc.vector.reciprocal(rden[:], rden[:]).then_inc(s["rec"], 1)
                        dve.wait_ge(s["rec"], c * 8 + (m + 1))
                        for g in range(2):
                            nc.vector.tensor_tensor(quot[:, m % 2, 2 * g:2 * g + 2].rearrange("p t h d -> p (t h) d"),
                                                    nd[g][:, :, :64],
                                                    rden[:, 4 * g:4 * g + 4].unsqueeze(2).to_broadcast([128, 4, 64]),
                                                    ALU.mult).then_inc(s["quot"], 1)
                dve.wait_ge(s["o_mm"], c + 1)
                step(nc.vector.tensor_scalar(rec[:], o_ps[:], bo[:], None, ALU.add))
                x = k.X[:, ds(c * CH, CH)]
                nc.vector.tensor_tensor(x, x, rec[:], ALU.add).then_inc(s["x"], 1)
                step.end()


def l3_attn(k):
    nc, ph = k.nc, ExitStack()
    s = {n: k.sem("l3a_" + n) for n in ("src", "p_mm", "neg", "exp", "relu", "phi", "v", "kv_mm", "kv", "y_mm", "rec", "y",
                                        "o_mm", "x", "steps")}
    with ph:
        w = k.sb("l3a_w", [128, 4, D], ctx=ph)
        src = k.sb("l3a_src", [128, CH], ctx=ph)
        neg, pos, phi = (k.sb("l3a_" + n, [128, 2, CH], ctx=ph) for n in ("neg", "pos", "phi"))
        v = k.sb("l3a_v", [128, 4, 2 * D], ctx=ph)
        kv = k.sb("l3a_kv", [128, 4, 2 * D], ctx=ph)
        rec, y = k.sb("l3a_rec", [128, CH], ctx=ph), k.sb("l3a_y", [128, CH], ctx=ph)
        load(k, "l3a_", ((w[:], "l3a_w"),))
        q_ps, k_ps, v_ps, kv_ps, num_ps, den_ps = k.ps[0], k.ps[1], k.ps[2], k.ps[2:6], k.ps[6], k.ps[7]
        o_ps = k.ps[0]
        block = ph.enter_context(nc.Block())

        @block.tensor
        def _(pe):
            with pe.Fori(0, NCH) as c:
                pe.wait_ge(s["src"], c + 1)
                nc.tensor.matmul(q_ps[:], w[:, 0, :], src[:], start=True, stop=True).then_inc(s["p_mm"], 1)
                for n, bank in ((1, k_ps), (2, v_ps)):
                    for t in range(4):
                        mm = nc.tensor.matmul(bank[:, t * D:(t + 1) * D], src[:, t * 128:(t + 1) * 128], w[:, n, :],
                                              start=True, stop=True)
                    mm.then_inc(s["p_mm"], 1)
                pe.wait_ge(s["phi"], c * 2 + 2)
                pe.wait_ge(s["v"], c + 2)

                def out(n):
                    pe.wait_ge(s["kv"], c * 16 + (n + 5))
                    for j, bank in enumerate((num_ps, den_ps)):
                        ins = nc.tensor.matmul(bank[:, n * T:(n + 1) * T], kv[:, n % 4, j * D:(j + 1) * D],
                                               phi[:, 0, n * T:(n + 1) * T], start=True, stop=True)
                    ins.then_inc(s["y_mm"], 1)

                for n in range(16):
                    r = slice((n % 4) * T, (n % 4 + 1) * T)
                    pe.wait_ge(s["kv"], c * 16 + (n + 1))
                    nc.tensor.matmul(kv_ps[n % 4][:, :2 * D], phi[r, 1, (n // 4) * D:(n // 4 + 1) * D], v[r, n // 4, :],
                                     start=True, stop=True).then_inc(s["kv_mm"], 1)
                    if n >= 2:
                        out(n - 2)
                out(14)
                out(15)
                pe.wait_ge(s["y"], c + 1)
                nc.tensor.matmul(o_ps[:], w[:, 3, :], y[:], start=True, stop=True).then_inc(s["o_mm"], 1)

        @block.scalar
        def _(act):
            with act.Fori(0, NCH) as c:
                act.wait_ge(s["x"], c + 1)
                nc.scalar.copy(src[:], k.XN[:, ds(c * CH, CH)]).then_inc(s["src"], 1)
                for j, bank in enumerate((q_ps, k_ps)):
                    act.wait_ge(s["neg"], c * 2 + (j + 1))
                    nc.scalar.activation(pos[:, j, :], bank[:], ACT.Relu).then_inc(s["relu"], 1)
                    nc.scalar.activation(neg[:, j, :], neg[:, j, :], ACT.Exp).then_inc(s["exp"], 1)

        @block.gpsimd
        def _(pool):
            with pool.Fori(0, NCH) as c:
                for j in range(2):
                    pool.wait_ge(s["exp"], c * 2 + (j + 1))
                    pool.wait_ge(s["relu"], c * 2 + (j + 1))
                    nc.gpsimd.tensor_tensor(phi[:, j, :], pos[:, j, :], neg[:, j, :], ALU.add).then_inc(s["phi"], 1)

        @block.vector
        def _(dve):
            dve.sem_inc(s["x"], 1)
            dve.sem_inc(s["kv"], 4)
            nc.vector.memset(v[:], 1.0).then_inc(s["v"], 1)
            dve.wait_ge(s["v"], 1)
            blk = k.const("blk8").unsqueeze(1).to_broadcast([128, 2, D])
            with dve.Fori(0, NCH) as c:
                step = Steps(dve, s["steps"], c, 1)
                for j, bank in enumerate((q_ps, k_ps)):
                    dve.wait_ge(s["p_mm"], c * 3 + (j + 1))
                    nc.vector.tensor_scalar(neg[:, j, :], bank[:], 0.0, None, ALU.min).then_inc(s["neg"], 1)
                dve.wait_ge(s["p_mm"], c * 3 + 3)
                nc.vector.tensor_copy(v[:, :, :D], v_ps[:].rearrange("p (t d) -> p t d", d=D)).then_inc(s["v"], 1)
                for n in range(16):
                    dve.wait_ge(s["kv_mm"], c * 16 + (n + 1))
                    if n >= 4:
                        dve.wait_ge(s["y_mm"], c * 16 + (n - 3))
                    nc.vector.tensor_tensor(kv[:, n % 4, :].rearrange("p (j d) -> p j d", j=2),
                                            kv_ps[n % 4][:, :2 * D].rearrange("p (j d) -> p j d", j=2), blk,
                                            ALU.mult).then_inc(s["kv"], 1)
                dve.wait_ge(s["y_mm"], c * 16 + 16)
                step(nc.vector.tensor_scalar(rec[:], den_ps[:], 1e-6, None, ALU.add))
                nc.vector.reciprocal(rec[:], rec[:]).then_inc(s["rec"], 1)
                dve.wait_ge(s["rec"], c + 1)
                nc.vector.tensor_tensor(y[:], num_ps[:], rec[:], ALU.mult).then_inc(s["y"], 1)
                dve.wait_ge(s["o_mm"], c + 1)
                x = k.X[:, ds(c * CH, CH)]
                nc.vector.tensor_tensor(x, x, o_ps[:], ALU.add).then_inc(s["x"], 1)
                step.end()


def context_attention(k, nm, queries, u_out, project=None):
    nc, ph = k.nc, ExitStack()
    s = {n: k.sem(nm + n) for n in ("qx", "s_mm", "mx", "exp", "rec", "p", "t_mm", "pt", "u_mm", "u", "own", "o", "kv_mm",
                                    "kv", "mask", "pad")}
    ctx_in = [k.sem(nm + f"ctx_in{j}") for j in range(2)]
    mask_in = k.sem(nm + "mask_in")
    val_in = [k.sem(nm + f"val_in{j}") for j in range(2)]
    turns = B // 2
    with ph:
        ctxT = k.sb(nm + "ctxT", [128, 2, SP2], ctx=ph)
        vals = k.sb(nm + "vals", [KC, 2, NKC, D], ctx=ph)
        qx = k.sb(nm + "qx", [128, 2, H, T], ctx=ph)
        p = k.sb(nm + "p", [128, 2, SP2], ctx=ph)
        pt = k.sb(nm + "pt", [KC, 2, NKC, H * T], ctx=ph)
        col = k.sb(nm + "col", [128, 3, 4], ctx=ph)
        if project:
            keys = k.sb(nm + "keys", [128, 2, SP2], ctx=ph)
            mask_i = k.sb(nm + "mask_i", [1, B * SP2], I32, ctx=ph)
            mask = k.sb(nm + "mask", [1, 2, SP2], BF16, ctx=ph)
            one = k.sb(nm + "one", [1, 128], BF16, ctx=ph)
            own = k.sb(nm + "own", [128, 2, 4, T], ctx=ph)
            o = k.sb(nm + "o", [128, 2, T], ctx=ph)
        else:
            keys = ctxT
        s_ps, t_ps, u_ps, k_ps, v_ps = k.ps[0:2], k.ps[2:4], k.ps[4:6], k.ps[6], k.ps[7]
        block = ph.enter_context(nc.Block())

        def turns_of(eng, first, body):
            first()
            with eng.Fori(0, turns - 1) as i:
                for j in range(8):
                    body(i, j, lambda jj: True)
            for j in range(8):
                body(turns - 1, j, lambda jj: jj < 8)

        @block.sync
        def _(sp):
            def fetch(l, g):
                sp.dma_start(ctxT[:, l, :], k.arr["ctxT"][:, ds(g * SP2, SP2)]).then_inc(ctx_in[l], 16)

            def fetch_rows(l, g):
                sp.dma_start(vals[:, l], k.arr["ctx_rows"][ds(g, 1)].rearrange("o p c d -> (o p) c d")
                             ).then_inc(val_in[l], 16)

            if project:
                sp.dma_start(mask_i[:], k.arr["ctx_mask"]).then_inc(mask_in, 16)
            for l in range(2):
                fetch(l, l)
                if not project:
                    fetch_rows(l, l)
            with sp.Fori(1, turns) as i:
                for l in range(2):
                    if project:
                        sp.wait_ge(s["kv_mm"], i * 4 + 2 * l)
                    else:
                        sp.wait_ge(s["s_mm"], i * 8 + (l * 4 + 4))
                    fetch(l, i * 2 + l)
                    if not project:
                        sp.wait_ge(s["u_mm"], i * 2 + (l + 1))
                        fetch_rows(l, i * 2 + l)

        @block.gpsimd
        def _(pool):
            with pool.Fori(0, turns) as i:
                for l in range(2):
                    pool.wait_ge(s["s_mm"], i * 8 + (l * 4 + 4))
                    queries(i * 2 + l, qx[:, l]).then_inc(s["qx"], 1)

        @block.tensor
        def _(pe):
            pe.sem_inc(s["s_mm"], 8)
            pe.sem_inc(s["t_mm"], 2)
            pe.sem_inc(s["u_mm"], 2)
            if project:
                pe.sem_inc(s["kv_mm"], 2)

            def make_kv(i, l):
                g = i * 2 + l
                sl = l % 2
                pe.wait_ge(ctx_in[sl], (i + l // 2) * 16 + 16)
                pe.wait_ge(s["kv"], g * 2 + 1)
                nc.tensor.matmul(k_ps[:, :SP2], project["k"], ctxT[:, sl, :], start=True, stop=True
                                 ).then_inc(s["kv_mm"], 1)
                pe.wait_ge(s["kv"], g * 2 + 2)
                for c in range(NKC):
                    mm = nc.tensor.matmul(v_ps[:KC, c * D:(c + 1) * D], ctxT[:, sl, c * KC:(c + 1) * KC], project["v"],
                                          start=True, stop=True)
                mm.then_inc(s["kv_mm"], 1)

            def score(i, j):
                n, l, sl = i * 8 + j, j // 4, (j // 4) % 2
                if j % 4 == 0:
                    pe.wait_ge(s["qx"], i * 2 + (l + 1))
                    if project:
                        pe.wait_ge(s["kv"], (i * 2 + l) * 2 + 3)
                        pe.wait_ge(s["mask"], i * 2 + (l + 2))
                    else:
                        pe.wait_ge(ctx_in[sl], (i + l // 2) * 16 + 16)
                pe.wait_ge(s["exp"], n + 1)
                q = qx[:, sl].rearrange("p h q -> p (h q)")[:, (j % 4) * 128:(j % 4 + 1) * 128]
                mm = nc.tensor.matmul(s_ps[j % 2][:, :S2], q, keys[:, sl, :S2], start=True, stop=not project)
                if project:
                    mm = nc.tensor.matmul(s_ps[j % 2][:, :S2], one[:], mask[:, sl, :S2], start=False, stop=True)
                mm.then_inc(s["s_mm"], 1)
                if project and j % 4 == 2:
                    return l + 1
                return None

            def turn(i, j):
                n = i * 8 + j
                pe.wait_ge(s["p"], n + 1)
                pe.wait_ge(s["pt"], n + 1)
                for c in range(NKC):
                    mm = nc.tensor.transpose(t_ps[j % 2][:KC, c * 128:(c + 1) * 128], p[:, j % 2, c * KC:(c + 1) * KC],
                                             k.const("ident"))
                mm.then_inc(s["t_mm"], 1)

            def first():
                if project:
                    make_kv(0, 0)
                score(0, 0)
                score(0, 1)
                turn(0, 0)
                nxt = score(0, 2)
                if nxt is not None:
                    make_kv(0, nxt)

            def body(i, j, there):
                if there(j + 3):
                    nxt = score(i, j + 3)
                    if nxt is not None and there(nxt * 4):
                        make_kv(i, nxt)
                if there(j + 1):
                    turn(i, j + 1)
                if j % 4 == 3:
                    l = j // 4
                    g = i * 2 + l
                    pe.wait_ge(s["pt"], i * 8 + (j + 3))
                    pe.wait_ge(s["u"], g + 1)
                    if project:
                        pe.wait_ge(s["kv"], g * 2 + 4)
                    else:
                        pe.wait_ge(val_in[l], i * 16 + 16)
                    for c in range(NKC):
                        if project:
                            for f in range(4):
                                mm = nc.tensor.matmul(u_ps[l][32 * f:32 * f + 32, :128], vals[:, l, c, 32 * f:32 * f + 32],
                                                      pt[:, l, c, 128 * f:128 * f + 128], start=(c == 0),
                                                      stop=(c == NKC - 1))
                        else:
                            mm = nc.tensor.matmul(u_ps[l][:], vals[:, l, c, :], pt[:, l, c, :], start=(c == 0),
                                                  stop=(c == NKC - 1))
                    mm.then_inc(s["u_mm"], 1)

            turns_of(pe, first, body)

        def take_turned(eng, copy, i, j):
            l = j // 4
            eng.wait_ge(s["t_mm"], i * 8 + (j + 3))
            if j % 4 == 0:
                eng.wait_ge(s["u_mm"], i * 2 + (l + 1))
            copy(pt[:, l, :, (j % 4) * 128:(j % 4 + 1) * 128],
                 t_ps[j % 2][:KC, :NKC * 128].rearrange("p (c r) -> p c r", c=NKC)).then_inc(s["pt"], 1)

        @block.scalar
        def _(act):
            act.sem_inc(s["exp"], 2)
            act.sem_inc(s["pt"], 2)
            if project:
                act.sem_inc(s["kv"], 2)
            else:
                act.sem_inc(s["u"], 2)

            def take_keys(i, l):
                g = i * 2 + l
                act.wait_ge(s["kv_mm"], g * 2 + 3)
                act.wait_ge(s["s_mm"], g * 4 + 4)
                nc.scalar.activation(keys[:, l % 2, :], k_ps[:, :SP2], ACT.Identity, bias=project["kb"]
                                     ).then_inc(s["kv"], 1)

            def take_values(i, l):
                g = i * 2 + l
                act.wait_ge(s["kv_mm"], g * 2 + 4)
                act.wait_ge(s["u_mm"], g + 1)
                nc.scalar.copy(vals[:, l % 2].rearrange("p c d -> p (c d)"), v_ps[:KC, :NKC * D]).then_inc(s["kv"], 1)

            def exp(i, j):
                n = i * 8 + j
                act.wait_ge(s["mx"], n + 1)
                act.wait_ge(s["t_mm"], n + 1)
                nc.scalar.activation(p[:, j % 2, :S2], s_ps[j % 2][:, :S2], ACT.Exp, bias=col[:, 0, j % 4:j % 4 + 1],
                                     accum_out=col[:, 1, j % 4:j % 4 + 1]).then_inc(s["exp"], 1)
                if project and j % 4 == 1:
                    return j // 4 + 1
                return None

            def first():
                act.wait_ge(s["pad"], 1)
                if project:
                    take_keys(0, 0)
                    take_values(0, 0)
                for j in range(2):
                    nxt = exp(0, j)
                if nxt is not None:
                    take_keys(0, nxt)

            def body(i, j, there):
                take_turned(act, nc.scalar.copy, i, j)
                if there(j + 2):
                    nxt = exp(i, j + 2)
                    if nxt is not None and there(nxt * 4):
                        take_keys(i, nxt)
                if project and j % 4 == 0 and there(j + 4):
                    take_values(i, j // 4 + 1)
                if not project and j % 4 == 3:
                    l = j // 4
                    act.wait_ge(s["u_mm"], i * 2 + (l + 3))
                    u_out(nc.scalar, u_ps[l], i * 2 + l).then_inc(s["u"], 1)

            turns_of(act, first, body)

        @block.vector
        def _(dve):
            if project:
                dve.sem_inc(s["u"], 2)
                nc.vector.memset(one[:], 1.0).then_inc(s["mask"], 1)
                dve.wait_ge(mask_in, 16)
            nc.vector.memset(p[:, :, S2:], 0.0).then_inc(s["pad"], 1)

            def make_mask(i, l):
                sl = l % 2
                dve.wait_ge(s["s_mm"], (i * 2 + l) * 4 + 4)
                nc.vector.tensor_scalar(mask[:, sl, :], mask_i[:, ds((i * 2 + l) * SP2, SP2)], 0.0, NEG, ALU.is_gt, ALU.mult
                                        ).then_inc(s["mask"], 1)

            def maximum(i, j):
                dve.wait_ge(s["s_mm"], i * 8 + (j + 9))
                nc.vector.tensor_reduce(col[:, 0, j % 4:j % 4 + 1], s_ps[j % 2][:, :S2], AX.X, ALU.max, negate=True
                                        ).then_inc(s["mx"], 1)
                if project and j % 4 == 0:
                    return j // 4 + 1
                return None

            def normalize(i, j):
                n = i * 8 + j
                dve.wait_ge(s["exp"], n + 3)
                r = col[:, 2, j % 4:j % 4 + 1]
                nc.vector.reciprocal(r, col[:, 1, j % 4:j % 4 + 1]).then_inc(s["rec"], 1)
                dve.wait_ge(s["rec"], n + 1)
                nc.vector.tensor_scalar(p[:, j % 2, :], p[:, j % 2, :], r, None, ALU.mult).then_inc(s["p"], 1)

            def gather(i, l):
                g = i * 2 + l
                dve.wait_ge(s["u_mm"], g + 3)
                nc.vector.tensor_tensor(own[:, l], u_ps[l][:, :128].rearrange("p (h q) -> p h q", h=4),
                                        k.const("hmask4").unsqueeze(2).to_broadcast([128, 4, T]), ALU.mult
                                        ).then_inc(s["u"], 1)
                dve.wait_ge(s["u"], g + 3)
                nc.vector.tensor_reduce(o[:, l, :], own[:, l].rearrange("p h q -> p q h"), AX.X, ALU.add
                                        ).then_inc(s["own"], 1)
                dve.wait_ge(s["own"], g + 1)
                x = k.X[:, ds(g * T, T)]
                nc.vector.scalar_tensor_tensor(out=x, in0=o[:, l, :], scalar=project["vb"], in1=x, op0=ALU.add, op1=ALU.add
                                               ).then_inc(s["o"], 1)

            def first():
                if project:
                    make_mask(0, 0)
                for j in range(2):
                    nxt = maximum(0, j)
                    if nxt is not None:
                        make_mask(0, nxt)
                normalize(0, 0)

            def body(i, j, there):
                if there(j + 2):
                    nxt = maximum(i, j + 2)
                    if nxt is not None and there(nxt * 4):
                        make_mask(i, nxt)
                if there(j + 1):
                    normalize(i, j + 1)
                if not project:
                    return
                if j == 4:
                    gather(i, 0)
                elif j == 7:
                    gather(i, 1)

            turns_of(dve, first, body)


def l1_xattn(k):
    nc, ph, hp = k.nc, ExitStack(), H // 2
    s = {n: k.sem("l1x_" + n) for n in ("w_mm", "w", "b_mm", "b", "q_mm", "q", "o_mm", "x")}
    with ph:
        wqk, wvo = (k.sb("l1x_" + n, [128, H, D], ctx=ph) for n in ("wqk", "wvo"))
        bqk, bo = k.sb("l1x_bqk", [128, H], ctx=ph), k.sb("l1x_bo", [128, 2], ctx=ph)
        qt = k.sb("l1x_qt", [128, H, N], ctx=ph)
        with ExitStack() as st:
            wq, wk, wv, wo = (k.sb("l1x_" + n, [128, hp, D], ctx=st) for n in ("wq", "wk", "wv", "wo"))
            bq, bv = (k.sb("l1x_" + n, [128, hp], ctx=st) for n in ("bq", "bv"))
            load(k, "l1xw_", ((wq[:], "l1x_wq"), (wk[:], "l1x_wk"), (wv[:], "l1x_wv"), (wo[:], "l1x_wo"),
                             (bq[:], "l1x_bq"), (bv[:], "l1x_bv"), (bo[:, 0:1], "l1x_bo")))
            with nc.Block() as block:
                @block.tensor
                def _(pe):
                    for h in range(H):
                        r = slice(64 * (h % 2), 64 * (h % 2) + 64)
                        for j, (a, b) in enumerate(((wq, wk), (wv, wo))):
                            m = 2 * h + j
                            if m >= 4:
                                pe.wait_ge(s["w"], m - 3)
                            nc.tensor.matmul(k.ps[m % 4][:, :D], a[r, h // 2, :], b[r, h // 2, :], start=True, stop=True
                                             ).then_inc(s["w_mm"], 1)
                        ins = nc.tensor.matmul(k.ps[4 + h % 2][:, h:h + 1], wk[r, h // 2, :], bq[r, h // 2:h // 2 + 1],
                                               start=True, stop=True)
                    for j in range(hp):
                        ins = nc.tensor.matmul(k.ps[6][:, 0:1], wo[:, j, :], bv[:, j:j + 1], start=(j == 0),
                                               stop=(j == hp - 1))
                    ins.then_inc(s["b_mm"], 1)

                @block.scalar
                def _(act):
                    for m in range(2 * H):
                        act.wait_ge(s["w_mm"], m + 1)
                        nc.scalar.copy((wqk, wvo)[m % 2][:, m // 2, :], k.ps[m % 4][:, :D]).then_inc(s["w"], 1)

                @block.vector
                def _(dve):
                    dve.wait_ge(s["b_mm"], 1)
                    for j in range(2):
                        nc.vector.tensor_copy(bqk[:].rearrange("p (h j) -> p j h", j=2)[:, j, :],
                                              k.ps[4 + j][:, :H].rearrange("p (h j) -> p j h", j=2)[:, j, :]
                                              ).then_inc(s["b"], 1)
                    nc.vector.tensor_tensor(bo[:, 1:2], bo[:, 0:1], k.ps[6][:, 0:1], ALU.add).then_inc(s["b"], 1)
        with nc.Block() as block:
            @block.tensor
            def _(pe):
                with pe.Fori(0, NCH) as c:
                    for h in range(H):
                        pe.wait_ge(s["q"], c * H + (h + 1))
                        nc.tensor.matmul(k.ps[h % 8][:], wqk[:, h, :], k.XN[:, ds(c * CH, CH)], start=True, stop=True
                                         ).then_inc(s["q_mm"], 1)

            @block.vector
            def _(dve):
                dve.sem_inc(s["q"], 8)
                with dve.Fori(0, NCH) as c:
                    for h in range(H):
                        dve.wait_ge(s["q_mm"], c * H + (h + 1))
                        nc.vector.tensor_scalar(qt[:, h, ds(c * CH, CH)], k.ps[h % 8][:], bqk[:, h:h + 1], 0.125, ALU.add,
                                                ALU.mult).then_inc(s["q"], 1)

        def queries(g, dst):
            return nc.gpsimd.tensor_copy(dst, qt[:, :, ds(g * T, T)])

        def u_out(act, bank, g):
            return act.copy(qt[:, :, ds(g * T, T)], bank[:].rearrange("p (h q) -> p h q", h=H))

        context_attention(k, "l1xc_", queries, u_out)
        with nc.Block() as block:
            @block.tensor
            def _(pe):
                with pe.Fori(0, NCH) as c:
                    pe.wait_ge(s["x"], c + 1)
                    for h in range(H):
                        mm = nc.tensor.matmul(k.ps[0][:], wvo[:, h, :], qt[:, h, ds(c * CH, CH)], start=(h == 0),
                                              stop=(h == H - 1))
                    mm.then_inc(s["o_mm"], 1)

            @block.vector
            def _(dve):
                dve.sem_inc(s["x"], 1)
                with dve.Fori(0, NCH) as c:
                    dve.wait_ge(s["o_mm"], c + 1)
                    x = k.X[:, ds(c * CH, CH)]
                    nc.vector.scalar_tensor_tensor(out=x, in0=k.ps[0][:], scalar=bo[:, 1:2], in1=x, op0=ALU.add,
                                                   op1=ALU.add).then_inc(s["x"], 1)


def l2_xattn(k):
    nc, ph = k.nc, ExitStack()
    s = {n: k.sem("l2x_" + n) for n in ("q_mm", "q")}
    with ph:
        w = k.sb("l2x_w", [128, 3, D], ctx=ph)
        b = k.sb("l2x_b", [128, 3], ctx=ph)
        q = k.sb("l2x_q", [128, N], ctx=ph)
        load(k, "l2x_", ((w[:], "l2x_w"), (b[:], "l2x_b")))
        with nc.Block() as block:
            @block.tensor
            def _(pe):
                for c in range(NCH):
                    nc.tensor.matmul(k.ps[c][:], w[:, 0, :], k.XN[:, c * CH:(c + 1) * CH], start=True, stop=True
                                     ).then_inc(s["q_mm"], 1)

            @block.vector
            def _(dve):
                for c in range(NCH):
                    dve.wait_ge(s["q_mm"], c + 1)
                    nc.vector.tensor_scalar(q[:, c * CH:(c + 1) * CH], k.ps[c][:], b[:, 0:1],
                                            float(1.0 / np.sqrt(np.float32(D // H))), ALU.add, ALU.mult
                                            ).then_inc(s["q"], 1)

        def queries(g, dst):
            return nc.gpsimd.tensor_tensor(dst, q[:, ds(g * T, T)].unsqueeze(1).to_broadcast([128, H, T]),
                                           k.const("hmask").unsqueeze(2).to_broadcast([128, H, T]), ALU.mult)

        context_attention(k, "l2xc_", queries, None,
                          {"k": w[:, 1, :], "v": w[:, 2, :], "kb": b[:, 1:2], "vb": b[:, 2:3]})


DELTA_STEPS_DVE, DELTA_STEPS_POOL = 59, 18
LEVELS = 5

def l1_attn(k):
    nc, ph, hp = k.nc, ExitStack(), H // 2
    slot = lambda h: hp * (h % 2) + h // 2
    names = ("src", "pj_mm", "q", "k", "ksq", "gate", "nb_mm", "nrm", "bg", "small", "bc_mm", "kn", "v_mm", "v",
             "rowS", "rowR", "mS_mm", "mS", "mR_mm", "mR", "back", "wideM", "wideX", "y_mm", "y", "z_mm", "t", "u_mm", "u",
             "p_mm", "r", "y2_mm", "y2", "z2_mm", "t2", "wr_mm", "wr", "o_mm", "o", "out_mm", "x", "dve", "p1", "pool", "zero",
             "seen", "ready", "diagS", "diagR", "chain")
    s = {n: k.sem("l1d_" + n) for n in names}
    add_normed(k, "l1d_")
    with ph:
        sb = lambda n, shape, dt=F32: k.sb("l1d_" + n, shape, dt, ctx=ph)
        lncol = sb("lncol", [128, 2])
        load(k, "l1d_l", ((lncol[:], "l1d_ln"),))
        layer_norm(k, k.XN, k.XN, (lncol[:, 0:1], lncol[:, 1:2]))
        wp = sb("wp", [128, 4, 1024])
        wv, wo, wbg = sb("wv", [128, 1024]), sb("wo", [128, hp, D]), sb("wbg", [128, 2, H])
        abias, bgcol = sb("abias", [128, 2, hp]), sb("bgcol", [H, 2])
        hsum, hsel = sb("hsum", [128, hp, H]), sb("hsel", [128, hp, 128])
        lmask, imask = sb("lmask", [128, LEVELS, T // 2], I32), sb("imask", [128, T], I32)
        src = sb("src", [128, 128])
        small = sb("small", [128, 3, 128])
        a, ar, sx, sxr = (sb(n, [128, 1024]) for n in ("a", "ar", "sx", "sxr"))
        px_xi = sb("px_xi", [128, T * (T + 1)])
        kn3 = sb("kn3", [128, 3, hp, 128])
        cols = sb("cols", [128, 2, 2, 1024])
        rows0, rows1 = sb("rows0", [128, 32, 112]), sb("rows1", [128, 32, 80])
        ms, mr, ll = sb("ms", [128, H, 3, T]), sb("mr", [128, H, 2, T]), sb("ll", [128, 2, H, T // 2])
        wideM = sb("wideM", [128, 5, H, 128])
        wideX = sb("wideX", [128, 2 * H, 128])
        v, u, rd = (sb(n, [128, 1024]) for n in ("v", "u", "rd"))
        ya = sb("ya", [128, T * (T + 1)])
        kk, ksq = (cols[:, n, 0, :].rearrange("p (h t) -> p h t", h=hp) for n in range(2))
        tmp = rows1[:].rearrange("p g w -> p (g w)")
        wmat = tmp[:, 1024:1088]
        nrm, tb, lt, kc = small[:H, 0, :], ya, ya, rd
        px, xi = px_xi[:, :1024], px_xi
        load(k, "l1d_", ((wp[:], "l1d_wp"), (wv[:], "l1d_wv"), (wo[:], "l1d_wo"), (wbg[:], "l1d_wbg"),
                         (abias[:], "l1d_ab"), (bgcol[:], "l1d_bg"), (hsum[:], "l1d_hsum"), (hsel[:], "l1d_hsel"),
                         (lmask[:], "l1d_lmask"), (imask[:], "l1d_imask")))
        g32 = lambda x: x.rearrange("p (g t) -> p g t", t=T)
        kn, kb, kg = (kn3[:, n].rearrange("p h t -> p (h t)") for n in range(3))
        q = rows0[:, :, 32:64]
        row_r = [(rows0, rows1)[l][:, :, 0:32] for l in range(2)]
        row_s = [rows0[:, :, 64:112], rows1[:, :, 32:80]]
        halves = lambda x, m, up: x.rearrange("p g (n two m) -> p g n two m", two=2, m=m)[:, :, :, up, :]
        row = lambda rows, f, m: rows[:, :, 16 * f:16 * f + 16].rearrange("p g (n m) -> p g n m", m=m)
        last = lambda x, m: x[:, :, :, m - 1:m].to_broadcast([128, 32, 16 // m, m])
        ones = lambda m: k.const("ones")[:, 0:1].unsqueeze(2).unsqueeze(3).to_broadcast([128, 32, 16 // m, m])
        first = lambda i: isinstance(i, int) and i == 0
        block = ph.enter_context(nc.Block())

        @block.scalar
        def _(act):
            copy = nc.scalar.copy

            def project(i):
                if not first(i):
                    act.wait_ge(s["v_mm"], i * 2)
                copy(src[:], k.XN[:, ds(i * 128, 128)]).then_inc(s["src"], 1)
                if not first(i):
                    for j in range(2):
                        copy(v[:, j * 512:(j + 1) * 512], k.ps[4 + j][:]).then_inc(s["v"], 1)
                for j in range(2):
                    act.wait_ge(s["pj_mm"], i * 8 + (j + 1))
                    copy(q[:, 16 * j:16 * j + 16, :], k.ps[6 + j][:].rearrange("p (g t) -> p g t", t=T)).then_inc(s["q"], 1)
                for j in range(2):
                    act.wait_ge(s["pj_mm"], i * 8 + (j + 3))
                    flat = lambda x: x[:, 4 * j:4 * j + 4, :].rearrange("p h t -> p (h t)")
                    copy(flat(kk), k.ps[4 + j][:]).then_inc(s["k"], 1)
                    nc.scalar.activation(flat(ksq), k.ps[4 + j][:], ACT.Square).then_inc(s["ksq"], 1)
                for n, x in enumerate((a, ar)):
                    for p in range(hp):
                        if p % 4 == 0:
                            act.wait_ge(s["pj_mm"], i * 8 + (5 + 2 * n + p // 4))
                        nc.scalar.activation(x[:, p * 128:(p + 1) * 128],
                                             k.ps[6 - 2 * n + p // 4][:, (p % 4) * 128:(p % 4 + 1) * 128], ACT.Sigmoid,
                                             bias=abias[:, n, p:p + 1]).then_inc(s["gate"], 1)
                act.wait_ge(s["nb_mm"], i + 1)
                for j in range(2):
                    nc.scalar.activation(small[:H, 1 + j, :], k.ps[6][:H, j * 128:(j + 1) * 128], ACT.Sigmoid,
                                         bias=bgcol[:, j:j + 1]).then_inc(s["bg"], 1)
                nc.scalar.activation(nrm, k.ps[7][:H, :128], ACT.Sqrt).then_inc(s["nrm"], 1)

            def widen(i):
                act.wait_ge(s["mS"], i * 5 + 5)
                act.wait_ge(s["mR"], i * 5 + 5)
                for b in range(TB):
                    rows, c = slice(b * T, b * T + T), slice(b * T, b * T + T)
                    up = slice(b * T + T // 2, b * T + T)
                    copy(wideM[rows, 0:2, :, c], ms[rows, :, 1:3, :].rearrange("p h f t -> p f h t")).then_inc(s["wideM"], 1)
                    copy(wideM[rows, 2, :, c], mr[rows, :, 1, :]).then_inc(s["wideM"], 1)
                    copy(wideM[rows, 3:5, :, up], ll[rows]).then_inc(s["wideM"], 1)
                act.wait_ge(s["back"], i + 1)
                for b in range(TB):
                    rows = slice(b * T, b * T + T)
                    copy(wideX[rows, :, b * T:b * T + T], kc[rows, :T * T].rearrange("p (t c) -> p c t", t=T)
                         ).then_inc(s["wideX"], 1)

            def chain(i):
                def out(mm, dst, bank, done):
                    for j in range(2):
                        act.wait_ge(s[mm], i * 2 + (j + 1))
                        copy(dst[:, j * 512:(j + 1) * 512], k.ps[bank + j][:]).then_inc(s[done], 1)
                out("y_mm", ya, 4, "y")
                out("u_mm", u, 4, "u")
                out("y2_mm", ya, 4, "y2")
                out("wr_mm", ya, 4, "wr")
                out("o_mm", rd, 6, "o")

            act.wait_ge(s["zero"], 7)
            project(0)
            project(1)
            widen(0)
            with act.Fori(1, NT - 1) as i:
                chain(i - 1)
                project(i + 1)
                widen(i)
            chain(NT - 2)
            for j in range(2):
                act.wait_ge(s["v_mm"], (NT - 1) * 2 + (j + 1))
                copy(v[:, j * 512:(j + 1) * 512], k.ps[4 + j][:]).then_inc(s["v"], 1)
            widen(NT - 1)
            chain(NT - 1)

        @block.tensor
        def _(pe):
            def project(i):
                pe.wait_ge(s["src"], i + 1)
                for n in range(4):
                    b0 = 6 - 2 * (n % 2)
                    if n == 1 and not first(i):
                        pe.wait_ge(s["v"], i * 2)
                    if n == 2:
                        pe.wait_ge(s["q"], i * 2 + 2)
                    if n == 3:
                        pe.wait_ge(s["ksq"], i * 2 + 2)
                    for j in range(2):
                        for e in range(4):
                            c = (4 * j + e) * 128
                            mm = nc.tensor.matmul(k.ps[b0 + j][:, e * 128:(e + 1) * 128], wp[:, n, c:c + 128], src[:],
                                                  start=True, stop=True)
                        mm.then_inc(s["pj_mm"], 1)
                pe.wait_ge(s["gate"], i * 16 + 8)
                for j in range(2):
                    nc.tensor.matmul(k.ps[6][:H, j * 128:(j + 1) * 128], wbg[:, j, :], src[:], start=True, stop=True)
                for p in range(hp):
                    mm = nc.tensor.matmul(k.ps[7][:H, :128], hsum[:, p, :], ksq[:, p, :], start=(p == 0),
                                          stop=(p == hp - 1))
                mm.then_inc(s["nb_mm"], 1)
                pe.wait_ge(s["gate"], i * 16 + 16)
                pe.wait_ge(s["small"], i + 1)
                for p in range(hp):
                    if p >= 4:
                        pe.wait_ge(s["kn"], i * 8 + (p - 3))
                    nc.tensor.matmul(k.ps[4 + p % 4][:, :384], hsel[:, p, :], small[:].rearrange("p n t -> p (n t)"),
                                     start=True, stop=True).then_inc(s["bc_mm"], 1)

            def fill(bank0, key, rows, w, sem, banks=1):
                pe.sem_inc(s["ready"], 1)
                per = hp // banks
                for e in range(hp):
                    for b in range(TB):
                        for pr in range(2):
                            rr = slice(64 * pr, 64 * pr + 64)
                            mm = nc.tensor.matmul(k.ps[bank0 + pr + e // per * 2][b * T:b * T + T,
                                                                                  e % per * w:(e % per + 1) * w],
                                                  key[rr, e * 128 + b * T:e * 128 + b * T + T],
                                                  rows[rr, e * TB + b, :], start=True, stop=True)
                mm.then_inc(sem, 1)

            def fill_s(i, lv):
                if not (first(i) and lv == 0):
                    pe.wait_ge(s["mS"], i * LEVELS + lv)
                pe.wait_ge(s["rowS"], i * LEVELS + (lv + 1))
                if lv == 0:
                    if not first(i):
                        pe.wait_ge(s["mR"], i * LEVELS)
                    pe.wait_ge(s["q"], i * 2 + 2)
                    fill(0, kb, rows0[:, :, 32:112], 80, s["mS_mm"], 2)
                else:
                    fill(0, cols[:, 0, lv % 2], row_s[lv % 2], 48, s["mS_mm"])

            def fill_r(i, lv):
                if lv == 0:
                    pe.wait_ge(s["mS"], i * LEVELS + 1)
                else:
                    pe.wait_ge(s["mR"], i * LEVELS + lv)
                pe.wait_ge(s["rowR"], i * LEVELS + (lv + 1))
                if lv == 0:
                    fill(2, kg, rows0[:, :, 0:64], 64, s["mR_mm"])
                else:
                    fill(2, cols[:, 1, lv % 2], row_r[lv % 2], 32, s["mR_mm"])

            def chain(i, n):
                def apply(bank0, mm_sem, lhs, rhs, needs):
                    pe.wait_ge(s[needs], i * 2 + 2)
                    for h in range(H):
                        for b in range(TB):
                            c = slice(b * T, b * T + T)
                            mm = nc.tensor.matmul(k.ps[bank0 + h // 8][c, (h % 8) * 64:(h % 8 + 1) * 64], lhs(h)[:, c],
                                                  rhs[:, h * 64:(h + 1) * 64], start=True, stop=True)
                        if h % 8 == 7:
                            mm.then_inc(s[mm_sem], 1)

                wide = lambda j: (lambda h: wideM[:, j, slot(h), :])
                inv = lambda j: (lambda h: wideX[:, j * H + slot(h), :])
                if n == 0:
                    pe.wait_ge(s["wideM"], i * 12 + 12)
                    pe.wait_ge(s["wideX"], i * 4 + 4)
                    apply(4, "y_mm", inv(0), v, "v")
                elif n == 1:
                    apply(6, "z_mm", wide(3), ya, "y")
                elif n == 2:
                    apply(4, "u_mm", inv(0), tb, "t")
                elif n == 3:
                    apply(6, "p_mm", wide(0), u, "u")
                elif n == 4:
                    apply(4, "y2_mm", inv(1), rd, "r")
                elif n == 5:
                    apply(6, "z2_mm", wide(4), ya, "y2")
                elif n == 6:
                    apply(4, "wr_mm", inv(1), tb, "t2")
                elif n == 7:
                    pe.wait_ge(s["wr"], i * 2 + 2)
                    for h in range(H):
                        out = k.ps[6 + h // 8][64 * (h % 2):64 * (h % 2) + 64, (h // 2 % 4) * 128:(h // 2 % 4 + 1) * 128]
                        nc.tensor.matmul(out, u[:, h * 64:(h + 1) * 64], wideM[:, 1, slot(h), :], start=True, stop=False)
                        mm = nc.tensor.matmul(out, ya[:, h * 64:(h + 1) * 64], wideM[:, 2, slot(h), :], start=False, stop=True)
                        if h % 8 == 7:
                            mm.then_inc(s["o_mm"], 1)
                else:
                    pe.wait_ge(s["o"], i * 2 + 2)
                    for p in range(hp):
                        mm = nc.tensor.matmul(k.ps[4][:, :128], wo[:, p, :], rd[:, p * 128:(p + 1) * 128], start=(p == 0),
                                              stop=(p == hp - 1))
                    mm.then_inc(s["out_mm"], 1)

            def levels(i):
                step = (lambda n: None) if first(i) else (lambda n: chain(i - 1, n))
                pe.wait_ge(s["kn"], i * 8 + 8)
                step(0)
                for lv in range(LEVELS):
                    fill_s(i, lv)
                    if lv < LEVELS - 1:
                        step(2 * lv + 1)
                    fill_r(i, lv)
                    if lv < LEVELS - 1:
                        step(2 * lv + 2)
                if not first(i):
                    pe.wait_ge(s["x"], i)
                for j in range(2):
                    nc.tensor.matmul(k.ps[4 + j][:], src[:], wv[:, j * 512:(j + 1) * 512], start=True, stop=True
                                     ).then_inc(s["v_mm"], 1)

            project(0)
            levels(0)
            project(1)
            with pe.Fori(1, NT - 1) as i:
                levels(i)
                project(i + 1)
            levels(NT - 1)
            for n in range(9):
                chain(NT - 1, n)

        @block.gpsimd
        def _(pool):
            tt = nc.gpsimd.tensor_tensor
            with pool.Fori(0, NT) as i:
                step = Steps(pool, s["pool"], i, DELTA_STEPS_POOL)
                pool.wait_ge(s["gate"], i * 16 + 16)
                pool.wait_ge(s["kn"], i * 8 + 8)
                for lv in range(LEVELS):
                    m, buf = 1 << lv, lv % 2
                    g, half = g32(ar[:]), (lambda x, up: halves(x, m, up))
                    if lv >= 2:
                        pool.wait_ge(s["mR_mm"], i * LEVELS + (lv - 1))
                    if lv >= 1:
                        step(tt(half(g32(cols[:, 1, buf]), 0), half(g32(kg), 0), half(g32(sxr[:]), 0), ALU.mult))
                    step(tt(row(row_r[buf], 0, m), half(g32(kn), 1), half(g, 1), ALU.mult))
                    tt(row(row_r[buf], 1, m), half(q, 1), half(g, 1), ALU.mult).then_inc(s["rowR"], 1)
                    pool.wait_ge(s["rowR"], i * LEVELS + (lv + 1))
                    if lv == LEVELS - 1:
                        break
                    if lv == 0:
                        step(tt(half(g32(sxr[:]), 0), half(g, 1), ones(m), ALU.mult))
                        step(tt(half(g32(sxr[:]), 1), ones(m), ones(m), ALU.mult))
                    else:
                        step(tt(half(g32(sxr[:]), 0), half(g32(sxr[:]), 0), last(half(g, 1), m), ALU.mult))
                    step(tt(half(g, 1), half(g, 1), last(half(g, 0), m), ALU.mult))
                step.end()

        @block.vector
        def _(dve):
            tt, vc = nc.vector.tensor_tensor, nc.vector
            for x in (wideM, wideX, ms, mr, ll, cols, small):
                vc.memset(x[:], 0.0).then_inc(s["zero"], 1)
            dve.wait_ge(s["zero"], 7)

            def project(i):
                step = Steps(dve, s["p1"], i, 2)
                dve.wait_ge(s["nrm"], i + 1)
                dve.wait_ge(s["bg"], i * 2 + 2)
                step(vc.tensor_scalar(nrm, nrm, 1e-12, None, ALU.max))
                step(vc.reciprocal(nrm, nrm))
                tt(small[:H, 1:3, :], small[:H, 1:3, :], small[:H, 0:1, :].to_broadcast([H, 2, 128]), ALU.mult
                   ).then_inc(s["small"], 1)
                dve.wait_ge(s["k"], i * 2 + 2)
                for p in range(hp):
                    dve.wait_ge(s["bc_mm"], i * 8 + (p + 1))
                    tt(kn3[:, :, p, :], k.ps[4 + p % 4][:, :384].rearrange("p (n t) -> p n t", n=3),
                       kk[:, p:p + 1, :].to_broadcast([128, 3, 128]), ALU.mult).then_inc(s["kn"], 1)
                dve.wait_ge(s["kn"], i * 8 + 8)
                step.end()

            def rows(i, lv, step):
                m, buf = 1 << lv, lv % 2
                g, half = g32(a[:]), (lambda x, up: halves(x, m, up))
                sx_, px_ = g32(sx[:]), g32(px)
                if lv >= 2:
                    dve.wait_ge(s["mS_mm"], i * LEVELS + (lv - 1))
                if lv >= 1:
                    step(tt(half(g32(cols[:, 0, buf]), 0), half(g32(kb), 0), half(sx_, 0), ALU.mult))
                step(tt(row(row_s[buf], 0, m), half(g32(kn), 1), half(g, 1), ALU.mult))
                if lv == 0:
                    step(vc.tensor_copy(row(row_s[buf], 1, m), half(g32(kn), 1)))
                else:
                    step(tt(row(row_s[buf], 1, m), half(g32(kn), 1), half(px_, 1), ALU.mult))
                tt(row(row_s[buf], 2, m), half(q, 1), half(g, 1), ALU.mult).then_inc(s["rowS"], 1)
                dve.wait_ge(s["rowS"], i * LEVELS + (lv + 1))
                if lv == LEVELS - 1:
                    return
                if lv == 0:
                    step(vc.tensor_copy(half(sx_, 0), half(g, 1)))
                    step(vc.tensor_scalar(half(sx_, 1), half(g, 1), 0.0, 1.0, ALU.mult, ALU.add))
                    step(vc.tensor_scalar(half(px_, 0), half(g, 1), 0.0, 1.0, ALU.mult, ALU.add))
                    step(vc.tensor_copy(half(px_, 1), half(g, 0)))
                else:
                    step(tt(half(sx_, 0), half(sx_, 0), last(half(g, 1), m), ALU.mult))
                    step(tt(half(px_, 1), half(px_, 1), last(half(g, 0), m), ALU.mult))
                step(tt(half(g, 1), half(g, 1), last(half(g, 0), m), ALU.mult))

            def cut(x, m):
                return x.rearrange("p h f (n two m) -> p (h f) n two m", two=2, m=m)[:, :, :, 1, :]

            def mask(lv, f):
                m = 1 << lv
                return lmask[:, lv].rearrange("p (n m) -> p n m", m=m).unsqueeze(1).to_broadcast([128, hp * f, 16 // m, m])

            diag = imask[:].unsqueeze(1).to_broadcast([128, hp, T])
            top = lmask[:, LEVELS - 1].unsqueeze(1).to_broadcast([128, hp, T // 2])

            odd = lambda x: x.rearrange("p h f (n two) -> p h f n two", two=2)[:, :, :, :, 1]
            below = lambda h, f: lmask[:, 0].unsqueeze(1).unsqueeze(2).to_broadcast([128, h, f, T // 2])

            def keep_s(i, lv):
                dve.wait_ge(s["mS_mm"], i * LEVELS + (lv + 1))
                dve.sem_inc(s["seen"], 1)
                if lv == 0:
                    hh = hp // 2
                    part = [k.ps[n][:, :hh * 80].rearrange("p (h x) -> p h x", h=hh) for n in range(4)]
                    hs = [slice(hp * (n % 2) + hh * (n // 2), hp * (n % 2) + hh * (n // 2) + hh) for n in range(4)]
                    for n in range(4):
                        vc.copy_predicated(ms[:, hs[n], 2, :], diag[:, :hh], part[n][:, :, :T]).then_inc(s["diagS"], 1)
                    dve.wait_ge(s["diagS"], i * 4 + 4)
                    dve.sem_inc(s["seen"], 1)
                    for n in range(4):
                        ins = vc.copy_predicated(odd(ms[:, hs[n]]), below(hh, 3),
                                                 part[n][:, :, T:].rearrange("p h (f t) -> p h f t", f=3))
                    ins.then_inc(s["mS"], 1)
                    return
                for pr in range(2):
                    hs, bank, m = slice(hp * pr, hp * pr + hp), k.ps[pr], 1 << lv
                    if lv < LEVELS - 1:
                        ins = vc.copy_predicated(cut(ms[:, hs], m), mask(lv, 3),
                                                 bank[:, :384].rearrange("p (x n m) -> p x n m", x=24, m=m))
                    else:
                        part = bank[:, :384].rearrange("p (h f t) -> p h f t", h=hp, f=3)
                        vc.copy_predicated(ll[:, 0, hs, :], top, part[:, :, 0, :])
                        vc.copy_predicated(ms[:, hs, 1, 16:], top, part[:, :, 1, :])
                        ins = vc.copy_predicated(ms[:, hs, 2, 16:], top, part[:, :, 2, :])
                ins.then_inc(s["mS"], 1)

            def keep_r(i, lv):
                dve.wait_ge(s["mR_mm"], i * LEVELS + (lv + 1))
                dve.sem_inc(s["seen"], 1)
                m, hs = 1 << lv, [slice(hp * pr, hp * pr + hp) for pr in range(2)]
                if lv == 0:
                    part = [k.ps[2 + pr][:].rearrange("p (h x) -> p h x", h=hp) for pr in range(2)]
                    for pr in range(2):
                        vc.copy_predicated(mr[:, hs[pr], 1, :], diag, part[pr][:, :, 32:]).then_inc(s["diagR"], 1)
                    dve.wait_ge(s["diagR"], i * 2 + 2)
                    dve.sem_inc(s["seen"], 1)
                    for pr in range(2):
                        ins = vc.copy_predicated(odd(mr[:, hs[pr]]), below(hp, 2),
                                                 part[pr][:, :, :32].rearrange("p h (f t) -> p h f t", f=2))
                    ins.then_inc(s["mR"], 1)
                    return
                for pr in range(2):
                    bank = k.ps[2 + pr]
                    if lv < LEVELS - 1:
                        ins = vc.copy_predicated(cut(mr[:, hs[pr]], m), mask(lv, 2),
                                                 bank[:, :256].rearrange("p (x n m) -> p x n m", x=16, m=m))
                    else:
                        part = bank[:, :256].rearrange("p (h f t) -> p h f t", h=hp, f=2)
                        vc.copy_predicated(ll[:, 1, hs[pr], :], top, part[:, :, 0, :])
                        ins = vc.copy_predicated(mr[:, hs[pr], 1, 16:], top, part[:, :, 1, :])
                ins.then_inc(s["mR"], 1)

            def minus(i, mm, dst, base, done):
                for j in range(2):
                    dve.wait_ge(s[mm], i * 2 + (j + 1))
                    c = slice(j * 512, j * 512 + 512)
                    tt(dst[:, c], base[:, c], k.ps[6 + j][:], ALU.subtract).then_inc(s[done], 1)

            def chain(i, n):
                if n == 0:
                    minus(i, "z_mm", tb, v, "t")
                elif n == 1:
                    minus(i, "p_mm", rd, v, "chain")
                    dve.wait_ge(s["chain"], i * 2 + 2)
                    for j in range(2):
                        c = slice(j * 512, j * 512 + 512)
                        vc.tensor_scalar(rd[:, c], rd[:, c], 1.0, -1.0, ALU.min, ALU.max).then_inc(s["r"], 1)
                elif n == 2:
                    minus(i, "z2_mm", tb, rd, "t2")
                else:
                    dve.wait_ge(s["out_mm"], i + 1)
                    x = k.X[:, ds(i * 128, 128)]
                    tt(x, x, k.ps[4][:, :128], ALU.add).then_inc(s["x"], 1)

            def levels(i, step):
                rows(i, 0, step)
                for lv in range(LEVELS):
                    if lv + 1 < LEVELS:
                        rows(i, lv + 1, step)
                    if lv == 0 and not first(i):
                        dve.wait_ge(s["wideM"], i * 12)
                    keep_s(i, lv)
                    if lv < 3 and not first(i):
                        chain(i - 1, lv)
                    keep_r(i, lv)
                    if lv == 3 and not first(i):
                        chain(i - 1, 3)
                dve.wait_ge(s["mS"], i * 5 + 5)
                dve.wait_ge(s["mR"], i * 5 + 5)

            def blocks(x, m):
                return (x.rearrange("p (n x) -> p n x", x=2 * m * (T + 1))[:, :, :2 * m * T]
                        .rearrange("p n (r c) -> p n r c", c=T))

            def inverse(i, step):
                for j, mat in enumerate((ms, mr)):
                    step(vc.tensor_copy(kc[:, :T * T].rearrange("p (t c) -> p c t", t=T)[:, j * H:(j + 1) * H, :], mat[:, :, 0, :]))
                step(vc.transpose(lt[:, :T * T], kc[:, :T * T]))
                step(vc.tensor_scalar(xi[:, :T * T], lt[:, :T * T], -1.0, None, ALU.mult))
                step(vc.memset(xi[:, 0:T * T:T + 1], 1.0))
                for m in (2, 4, 8):
                    nb, lb, xb = T // (2 * m), blocks(lt, m), blocks(xi, m)
                    lo, hi = slice(0, m), slice(m, 2 * m)
                    t5 = tmp[:, :nb * m * m * m].rearrange("p (n r c k) -> p n r c k", n=nb, r=m, c=m)
                    w4 = wmat[:, :m * m].rearrange("p (r c) -> p r c", r=m) if m == 8 else \
                        wmat[:, :nb * m * m].rearrange("p (n r c) -> p n r c", n=nb, r=m)
                    if m == 8:
                        for n in range(nb):
                            t4 = t5[:, 0]
                            left = lambda x: x.unsqueeze(2).to_broadcast([128, m, m, m])
                            right = lambda x: x.rearrange("p k c -> p c k").unsqueeze(1).to_broadcast([128, m, m, m])
                            step(tt(t4, left(lb[:, n, hi, lo]), right(xb[:, n, lo, lo]), ALU.mult))
                            step(vc.tensor_reduce(w4, t4, AX.X, ALU.add))
                            step(tt(t4, left(xb[:, n, hi, hi]), right(w4), ALU.mult))
                            step(vc.tensor_reduce(xb[:, n, hi, lo], t4, AX.X, ALU.add, negate=True))
                        continue
                    flat = tmp[:, :nb * m * m * m].rearrange("p (x k) -> p x k", k=m)
                    right = lambda x: x.rearrange("p n k c -> p n c k")
                    left = lambda x, r: x[:, :, r:r + 1, :].to_broadcast([128, nb, m, m])
                    for r in range(m):
                        step(tt(t5[:, :, r], left(lb[:, :, hi, lo], r), right(xb[:, :, lo, lo]), ALU.mult))
                    step(vc.tensor_reduce(wmat[:, :nb * m * m], flat, AX.X, ALU.add))
                    for r in range(m):
                        step(tt(t5[:, :, r], left(xb[:, :, hi, hi], r), right(w4), ALU.mult))
                    step(vc.tensor_reduce(wmat[:, :nb * m * m], flat, AX.X, ALU.add, negate=True))
                    step(vc.tensor_copy(xb[:, :, hi, lo], w4))
                vc.transpose(kc[:, :T * T], xi[:, :T * T]).then_inc(s["back"], 1)

            def body(i):
                step = Steps(dve, s["dve"], i, DELTA_STEPS_DVE)
                levels(i, step)
                inverse(i, step)
                step.end()

            project(0)
            body(0)
            project(1)
            with dve.Fori(1, NT - 1) as i:
                body(i)
                project(i + 1)
            body(NT - 1)
            for n in range(4):
                chain(NT - 1, n)
            dve.wait_ge(s["x"], NT)


SUBLAYERS = {4: l1_attn, 3: l1_xattn, 6: l2_xattn, 0: l0_xattn, 1: l0_attn, 2: l0_ffn, 5: l1_ffn, 7: l2_attn, 10: l3_attn, 8: l2_ffn, 9: l3_xattn, 11: l3_ffn}


def program(nc, arr, out):
    ctx = ExitStack()
    with ctx:
        k = Core(nc, ctx, arr, out)
        load_state(k)
        for p in PHASES:
            before = nc.snapshot_sems()
            layer_norm(k, k.X, k.XN)
            SUBLAYERS[p](k)
            nc.clear_and_free_semaphores(nc.allocated_since(before))
            nc.all_engine_barrier()
        store_state(k)


def laid_out(a):
    f = lambda v: np.ascontiguousarray(v)
    ctx = a["ctx_1024"]
    pad = np.concatenate([ctx, np.zeros((B, SP2 - S2, D), ctx.dtype)], 1)
    m = a["mask_1xSxS2_ff0"][0]
    mpad = np.concatenate([m, np.zeros((T, SP2 - S2), m.dtype)], 1)
    r = {
        "xT": f(a["x"].reshape(N, D).T),
        "consts": constants(),
        "ctxT": f(pad.transpose(2, 0, 1).reshape(D, B * SP2)),
        "l0x_mask": f(mpad.T.reshape(NKC, KC, T).transpose(1, 0, 2)),
        "l0x_bcol": f(np.stack([a["L0_xattn_bias_q"], a["L0_xattn_bias_k"]], 1)),
        "l0x_bv": f(np.tile(a["L0_xattn_bias_v"].reshape(1, 1, D), (KC, NKC, 1))),
    }
    wq, wk, wv = np.split(a["L0_attn_Wqkv"], 3, 1)
    swap = np.arange(D) ^ 1
    r["l0a_w"] = f(np.stack([wq, wq[:, swap], wk, wk[:, swap], wv], 1))
    r["L0_attn_Wproj"] = f(a["L0_attn_Wproj"])
    r["l0a_cw"] = f(np.tile(np.concatenate([np.zeros(1, np.float32), a["L0_attn_cascade_w"]]), (128, 1)))
    r["ctx_head"] = f(ctx[:, :T].reshape(N, D).T)
    L = lambda n: a["L3_xattn_" + n]
    r["l3x_w"] = f(np.stack([L("Wq").T, L("Wf")[:D].T, L("Wf")[D:].T, L("Wp").T], 1))
    r["l3x_A"] = f(np.stack([L("Aq").T, L("Af").T, L("Ap").T], 1))
    r["l3x_B"] = f(np.stack([L("Bq").T, L("Bf")[:D].T, L("Bf")[D:].T, L("Bp").T], 1))
    r["l3x_bcol"] = f(np.stack([L("bq"), L("bf")[:D], L("bp")], 1))
    r["l3x_bv"] = f(L("bf")[D:].reshape(1, D))
    def expert_pack(up, down, cols):
        e, d, ff = down.shape
        return f(np.concatenate([u.transpose(0, 2, 1) for u in up]
                                + [down.transpose(0, 2, 1).reshape(e, ff // 128, 128, d).transpose(0, 2, 1, 3)
                                   .reshape(e, 128, ff)] + cols, 2))

    G = lambda n: a["L0_ffn_" + n]
    r["l0f_cen"] = f(G("centroids").T)
    r["l0f_w"] = expert_pack([G("w1")], G("w2"), [G("b1").reshape(8, 4, 128).transpose(0, 2, 1)]
                             + [G(n)[:, :, None] for n in ("b2", "ln_g", "ln_b")])
    r["sel"] = np.repeat(np.eye(17, dtype=np.float32), 128, 1)
    r["bits_i"] = np.tile((np.int64(1) << np.arange(32)).astype(np.uint32).view(np.int32), (128, 1))
    G2 = lambda n: a["L2_ffn_" + n]
    r["l2f_gw"] = f(G2("gate_w").T)
    r["l2f_w"] = expert_pack([G2("Wg"), G2("Wu")], G2("Wd"), [])
    r["l2f_s"] = expert_pack([G2("Sg")[None], G2("Su")[None]], G2("Sd")[None], [])
    G3 = lambda n: a["L3_ffn_" + n]
    r["places"] = np.tile(np.arange(N, dtype=np.float32), (128, 1))
    r["l3f_tri"] = np.triu(np.ones((8, 8), np.float32), 1)
    r["l3f_gw"] = f(G3("Ws").T)
    r["l3f_bs"] = f(np.tile(G3("bs")[None], (128, 1)))
    r["l3f_top"] = f(np.repeat(np.eye(9, dtype=np.float32)[:, 8:], 128, 1))
    r["l3f_w"] = f(np.concatenate([G3("W1"), G3("W2"), G3("b1")[:, :, None], G3("b2")[:, :, None],
                                   np.zeros((8, D, 2), np.float32)], 2))
    r["L1_ffn_weight"], r["l1f_bias"] = f(a["L1_ffn_weight"]), f(a["L1_ffn_bias"][:, None])
    A = lambda n: a["L2_attn_" + n]
    for n in ("q", "k", "v"):
        r["l2a_w" + n] = f(A("w" + n).reshape(D, 1024))
    r["l2a_wo"] = f(A("wo").reshape(8, 128, D).transpose(1, 0, 2))
    r["l2a_bq"], r["l2a_bk"] = f(A("bq").reshape(8, 128).T), f(A("bk").reshape(8, 128).T)
    r["l2a_bv"], r["l2a_bo"] = f(np.tile(A("bv").reshape(1, 1024), (128, 1))), f(A("bo")[:, None])
    r["l3a_w"] = f(np.stack([a["L3_attn_W" + n] for n in "qkvo"], 1))
    r["ctx_rows"] = f(pad.reshape(B, NKC, KC, D).transpose(0, 2, 1, 3))
    M = a["mask_BxS2_ik0"]
    r["ctx_mask"] = f(np.concatenate([M, np.zeros((B, SP2 - S2), M.dtype)], 1).reshape(1, B * SP2))
    Q = lambda n: a["L1_xattn_" + n]
    for n in ("q", "k", "v"):
        r["l1x_w" + n] = f(Q("W" + n).T.reshape(8, 128, D).transpose(1, 0, 2))
    r["l1x_wo"] = f(Q("Wo").reshape(8, 128, D).transpose(1, 0, 2))
    r["l1x_bq"], r["l1x_bv"], r["l1x_bo"] = f(Q("bq").reshape(8, 128).T), f(Q("bv").reshape(8, 128).T), f(Q("bo")[:, None])
    V = lambda n: a["L2_xattn_" + n]
    r["l2x_w"] = f(np.stack([V(n + "_w").T for n in "qkv"], 1))
    r["l2x_b"] = f(np.stack([V(n + "_b") for n in "qkv"], 1))
    E = lambda n: a["L1_attn_" + n]
    r["l1d_ln"] = f(np.stack([E("ln_w"), E("ln_b")], 1))
    r["l1d_wp"] = f(np.stack([E(n).T for n in ("Wq", "Wk", "Wa", "WaR")], 1))
    r["l1d_wv"] = f(E("Wv").T)
    r["l1d_wo"] = f(E("Wo").T.reshape(8, 128, D).transpose(1, 0, 2))
    r["l1d_wbg"] = f(np.stack([E("Wb").T, E("Wg").T], 1))
    r["l1d_ab"] = f(np.stack([E("ba").reshape(8, 128).T, E("baR").reshape(8, 128).T], 1))
    r["l1d_bg"] = f(np.stack([E("bb"), E("bg")], 1))
    p128 = np.arange(128)
    head_of = 2 * np.arange(8)[None] + p128[:, None] // 64
    hot = (head_of[:, :, None] == np.arange(H)).astype(np.float32)
    r["l1d_hsum"] = f(hot)
    r["l1d_hsel"] = np.concatenate([hot.transpose(2, 1, 0), np.zeros((128 - H, 8, 128), np.float32)])
    step_of, lm = p128 % T, np.zeros((128, LEVELS, T // 2), np.int32)
    for lv in range(LEVELS):
        m = 1 << lv
        up = np.arange(T).reshape(-1, 2, m)[:, 1].reshape(-1)
        lm[:, lv] = (step_of[:, None] // (2 * m) == up[None] // (2 * m)) & ((step_of[:, None] // m) % 2 == 0)
    r["l1d_lmask"] = lm
    r["l1d_imask"] = (step_of[:, None] == np.arange(T)[None]).astype(np.int32)
    for n in ("q", "k", "v"):
        r["L0_xattn_kernel_" + n] = f(a["L0_xattn_kernel_" + n].reshape(D, D))
    return r


def kernel(**inputs):
    import concourse.bacc as bacc
    from concourse.bass_utils import run_bass_kernel_spmd

    nc = bacc.Bacc("TRN2", target_bir_lowering=False, num_devices=1)
    arrays = laid_out({n: np.asarray(v) for n, v in inputs.items()})
    arr = {n: nc.dram_tensor("in_" + n, v.shape, mybir.dt.from_np(v.dtype), kind="ExternalInput").ap()
           for n, v in arrays.items()}
    out = nc.dram_tensor("out_xT", (D, N), F32, kind="ExternalOutput").ap()
    program(nc, arr, out)
    r = run_bass_kernel_spmd(nc, [{"in_" + n: v for n, v in arrays.items()}], core_ids=[0])
    return np.ascontiguousarray(r.results[0]["out_xT"].T).reshape(B, T, D)
```
